# Optimizing a Trainium2 kernel written in Bass

```python
import numpy as np
import jax
import jax.numpy as jnp

def _softmax(x, axis=-1):
    return jax.nn.softmax(x, axis=axis)

def _gelu(x):
    return jax.nn.gelu(x, approximate=True)

def _silu(x):
    return jax.nn.silu(x)

def _sigmoid(x):
    return jax.nn.sigmoid(x)

def _layernorm(x, axis=-1, eps=1e-05):
    m = jnp.mean(x, axis=axis, keepdims=True)
    v = jnp.var(x, axis=axis, keepdims=True)
    return (x - m) / jnp.sqrt(v + eps)

def _scatter_add(tgt, idx, src, axis=0):
    return tgt.at[idx].add(src)

def _segment_sum(src, seg, n):
    return jax.ops.segment_sum(src, seg, n)
kernel_name = 'mk_prb_d1_jaxref_r4_610d8c'

def setup_inputs(seed: int=0):
    np.random.seed(seed)
    _w = jnp.asarray

    def _L0_attn_setup():
        import jax, jax.numpy as jnp
        import numpy as np
        B, T, C = (2, 512, 512)
        H, KVH = (16, 4)
        HD = C // H
        REP = H // KVH

        def _alibi_slopes(n_head):
            start = 2.0 ** (-2.0 ** (-(np.log2(n_head) - 3.0)))
            return jnp.asarray([start ** (i + 1) for i in range(n_head)], jnp.float32)
        key = jax.random.key(seed)
        ks = jax.random.split(key, 4)
        sc = 0.02
        return {'x': jax.random.normal(ks[0], (B, T, C), jnp.float32), 'Wq': jax.random.normal(ks[1], (C, C), jnp.float32) * sc, 'Wkv': jax.random.normal(ks[2], (C, HD * KVH * 2), jnp.float32) * sc, 'Wo': jax.random.normal(ks[3], (C, C), jnp.float32) * sc, 'bo': jnp.zeros((C,), jnp.float32)}
    _L0_attn_in = _L0_attn_setup()

    def _L0_ffn_setup():
        import jax, jax.numpy as jnp
        import numpy as np
        BLOCK_SIZE = 32
        HIDDEN_SIZE = 512
        MLP_DIM = 4096
        NVFP4_LUT = jnp.array([0.0, 0.5, 1.0, 1.5, 2.0, 3.0, 4.0, 6.0, 0.0, -0.5, -1.0, -1.5, -2.0, -3.0, -4.0, -6.0], dtype=jnp.float32)

        def dequant_nvfp4(W_packed, scales, block=BLOCK_SIZE):
            N = W_packed.shape[0]
            low = W_packed & 15
            high = W_packed >> 4 & 15
            idx = jnp.stack([low, high], axis=-1).reshape(N, -1)
            vals = NVFP4_LUT[idx]
            K = vals.shape[1]
            vals = vals.reshape(N, K // block, block) * scales[:, :, None]
            return vals.reshape(N, K)
        key = jax.random.key(seed)
        ks = jax.random.split(key, 7)
        x = jax.random.normal(ks[0], (4, 32, HIDDEN_SIZE), dtype=jnp.float32)
        gate_W_packed = jax.random.randint(ks[1], (MLP_DIM, HIDDEN_SIZE // 2), 0, 64, dtype=jnp.int32)
        gate_scales = jax.random.uniform(ks[2], (MLP_DIM, HIDDEN_SIZE // BLOCK_SIZE), dtype=jnp.float32) * 0.1 + 0.001
        up_W_packed = jax.random.randint(ks[3], (MLP_DIM, HIDDEN_SIZE // 2), 0, 64, dtype=jnp.int32)
        up_scales = jax.random.uniform(ks[4], (MLP_DIM, HIDDEN_SIZE // BLOCK_SIZE), dtype=jnp.float32) * 0.1 + 0.001
        down_W_packed = jax.random.randint(ks[5], (HIDDEN_SIZE, MLP_DIM // 2), 0, 64, dtype=jnp.int32)
        down_scales = jax.random.uniform(ks[6], (HIDDEN_SIZE, MLP_DIM // BLOCK_SIZE), dtype=jnp.float32) * 0.1 + 0.001
        return {'x': x, 'gate_W_packed': gate_W_packed, 'gate_scales': gate_scales, 'up_W_packed': up_W_packed, 'up_scales': up_scales, 'down_W_packed': down_W_packed, 'down_scales': down_scales}
    _L0_ffn_in = _L0_ffn_setup()
    _d = {'L0_attn_x': _L0_attn_in['x'], 'L0_attn_Wq': _L0_attn_in['Wq'], 'L0_attn_Wkv': _L0_attn_in['Wkv'], 'L0_attn_Wo': _L0_attn_in['Wo'], 'L0_attn_bo': _L0_attn_in['bo'], 'L0_ffn_gate_W_packed': _L0_ffn_in['gate_W_packed'], 'L0_ffn_gate_scales': _L0_ffn_in['gate_scales'], 'L0_ffn_up_W_packed': _L0_ffn_in['up_W_packed'], 'L0_ffn_up_scales': _L0_ffn_in['up_scales'], 'L0_ffn_down_W_packed': _L0_ffn_in['down_W_packed'], 'L0_ffn_down_scales': _L0_ffn_in['down_scales']}
    _x0 = _d['L0_attn_x']
    _d['L0_attn_x'] = jax.random.normal(jax.random.fold_in(jax.random.key(seed), 1), (1, 2048, 512), dtype=_x0.dtype)
    del _x0
    return _d

def reference(L0_attn_x, L0_attn_Wq, L0_attn_Wkv, L0_attn_Wo, L0_attn_bo, L0_ffn_gate_W_packed, L0_ffn_gate_scales, L0_ffn_up_W_packed, L0_ffn_up_scales, L0_ffn_down_W_packed, L0_ffn_down_scales):

    def _L0_attn_ref(x, Wq, Wkv, Wo, bo):
        import jax, jax.numpy as jnp
        import numpy as np
        B, T, C = (2, 512, 512)
        H, KVH = (16, 4)
        HD = C // H
        REP = H // KVH

        def _alibi_slopes(n_head):
            start = 2.0 ** (-2.0 ** (-(np.log2(n_head) - 3.0)))
            return jnp.asarray([start ** (i + 1) for i in range(n_head)], jnp.float32)
        Bv, Tv, Cv = x.shape
        q = (x @ Wq).reshape(Bv, Tv, H, HD).transpose(0, 2, 1, 3)
        k, v = jnp.split(x @ Wkv, 2, axis=-1)
        k = k.reshape(Bv, Tv, KVH, HD).transpose(0, 2, 1, 3)
        v = v.reshape(Bv, Tv, KVH, HD).transpose(0, 2, 1, 3)
        qg = q.reshape(Bv, REP, KVH, Tv, HD)
        scores = jnp.einsum('brgtd,bgsd->brgts', qg, k) / jnp.sqrt(jnp.float32(HD))
        idx = jnp.arange(Tv)
        diff = (idx[None, :] - idx[:, None]).astype(jnp.float32)
        slopes = _alibi_slopes(H).reshape(REP, KVH)
        bias = jnp.tril(diff)[None, None] * slopes[:, :, None, None]
        causal = idx[None, :] <= idx[:, None]
        scores = jnp.where(causal[None, None, None], scores + bias[None], -jnp.inf)
        attn = jax.nn.softmax(scores, axis=-1)
        out = jnp.einsum('brgts,bgsd->brgtd', attn, v)
        out = out.reshape(Bv, H, Tv, HD).transpose(0, 2, 1, 3).reshape(Bv, Tv, Cv)
        return out @ Wo + bo

    def _L0_ffn_ref(x, gate_W_packed, gate_scales, up_W_packed, up_scales, down_W_packed, down_scales):
        import jax, jax.numpy as jnp
        import numpy as np
        BLOCK_SIZE = 32
        HIDDEN_SIZE = 512
        MLP_DIM = 4096
        NVFP4_LUT = jnp.array([0.0, 0.5, 1.0, 1.5, 2.0, 3.0, 4.0, 6.0, 0.0, -0.5, -1.0, -1.5, -2.0, -3.0, -4.0, -6.0], dtype=jnp.float32)

        def dequant_nvfp4(W_packed, scales, block=BLOCK_SIZE):
            N = W_packed.shape[0]
            low = W_packed & 15
            high = W_packed >> 4 & 15
            idx = jnp.stack([low, high], axis=-1).reshape(N, -1)
            vals = NVFP4_LUT[idx]
            K = vals.shape[1]
            vals = vals.reshape(N, K // block, block) * scales[:, :, None]
            return vals.reshape(N, K)
        B, S, H = x.shape
        xt = x.reshape(B * S, H)
        Wg = dequant_nvfp4(gate_W_packed, gate_scales)
        Wu = dequant_nvfp4(up_W_packed, up_scales)
        Wd = dequant_nvfp4(down_W_packed, down_scales)
        gate = jnp.einsum('th,nh->tn', xt, Wg)
        up = jnp.einsum('th,nh->tn', xt, Wu)
        gelu = jnp.tanh(0.7978845608028654 * (gate + 0.044715 * gate ** 3)) * gate * 0.5 + gate * 0.5
        inter = gelu * up
        out = jnp.einsum('tn,hn->th', inter, Wd)
        return out.reshape(B, S, H)
    x = L0_attn_x
    xn = _layernorm(x, axis=-1)
    x = x + _L0_attn_ref(xn, L0_attn_Wq, L0_attn_Wkv, L0_attn_Wo, L0_attn_bo) + _L0_ffn_ref(xn, L0_ffn_gate_W_packed, L0_ffn_gate_scales, L0_ffn_up_W_packed, L0_ffn_up_scales, L0_ffn_down_W_packed, L0_ffn_down_scales)
    return x

_drawn_inputs = setup_inputs


def setup_inputs(seed=0):
    import zlib

    import numpy as np

    out = dict(_drawn_inputs(seed))
    spreads = {'L0_attn_bo': (0.0, 2.0)}
    factors = {'L0_attn_Wq': 8.0, 'L0_attn_Wkv': 8.0, 'L0_attn_Wo': 8.0}
    for name, (base, spread) in spreads.items():
        noise = np.random.default_rng([zlib.crc32(name.encode()), seed]).standard_normal(out[name].shape)
        drawn = base * np.exp(spread * noise) if base else spread * noise
        out[name] = jnp.asarray(drawn.astype(out[name].dtype))
    for name, factor in factors.items():
        out[name] = (out[name] * factor).astype(out[name].dtype)
    return out
```

```python
from contextlib import ExitStack

import numpy as np

import concourse.bass as bass
from concourse import mybir

F32 = mybir.dt.float32
F32R = mybir.dt.float32r
F16 = mybir.dt.float16
BF16 = mybir.dt.bfloat16
I32 = mybir.dt.int32
ALU = mybir.AluOpType
ACT = mybir.ActivationFunctionType
AX = mybir.AxisListType
RMAX = bass.bass_isa.ReduceOp.max

P = 128
T, C = 2048, 512
HEADS, KVH, HD = 16, 4, 32
REP = HEADS // KVH
MLP = 4096
BLOCK = 32
EPS = 1e-5
KT = C // P
CH = 512
NCH = T // CH
TPC = CH // P
NT = T // P
GROUP = 2 * P
NG = MLP // GROUP
WORDS = GROUP * C // 2 // P
SB = WORDS * 2 // BLOCK
assert NG == HEADS

AUG = 8
NB = 2

XS = 2.0 ** 4
WS = 2.0 ** 8
NIB = 2.0 ** 14
IS = 2.0 ** -10
LIM = 2.0 ** 60
GELU_C = 0.7978845608028654
GELU_A = 0.044715

SLOTS = 48
PV_LAG = 3


def score_blocks():
    out = []
    for c in range(NCH):
        d = TPC * c
        out += [(c, [(j, 0, 0)], CH) for j in range(d + 1)]
        out.append((c, [(d + 1, 0, P), (d + 3, 3 * P, 3 * P)], CH))
        out.append((c, [(d + 2, 0, 2 * P)], 2 * P))
    return out


BLOCKS = score_blocks()
NBLK = len(BLOCKS)
BLK_END = [sum(b[0] <= c for b in BLOCKS) for c in range(NCH)]
MAXP = [(c, i, m) for c in range(NCH) for i in range(TPC) for m in range(c + 1)]
NMAX = len(MAXP)
MAX_END = [sum(m[0] <= c for m in MAXP) for c in range(NCH)]
MAX_PER_SLOT = [2, 2, 2, 2, 2, 2] + [2, 1] * 4 + [2, 1] * 5 + [1]
MAX_AT = [list(range(sum(MAX_PER_SLOT[:s]), sum(MAX_PER_SLOT[:s + 1]))) for s in range(SLOTS)]
assert sum(MAX_PER_SLOT) == NMAX
TURN_MAX_AT = {3: 0, 7: 1, 14: 2, 25: 3}
SCORE_SLOTS = [s for s in range(6, SLOTS) if s - 1 not in TURN_MAX_AT][:NBLK]
SCORE_AT = {s: n for n, s in enumerate(SCORE_SLOTS)}
BLOCKS_BY_TURN = [sum(s <= turn for s in SCORE_SLOTS) for turn in TURN_MAX_AT]
VALUES_AT = {s + PV_LAG: n for s, n in SCORE_AT.items()}
assert max(VALUES_AT) < SLOTS
DECODE_FROM = {26: 0, 31: 1, 36: 2}
DECODE_AT = {s + i: (m, i) for s, m in DECODE_FROM.items() for i in range(5)}
TURN_W_AT = {31: (0, 0), 32: (0, 1), 36: (1, 0), 37: (1, 1), 41: (2, 0), 42: (2, 1)}


def ffn_pieces():
    out = []
    for w in range(NCH):
        for a in range(2):
            out += [("gate", w, a, 0), ("gate", w, a, 1), ("up", w, a, 0), ("up", w, a, 1)]
            if w:
                out += [("down", w - 1, 2 * a, 0), ("down", w - 1, 2 * a + 1, 0)]
    return out + [("down", NCH - 1, t, 0) for t in range(TPC)]


PIECES = ffn_pieces()
assert len(PIECES) == SLOTS


def build(nc, x, Wq, Wkv, Wo, bo, packed, scales, augq, augk, out):
    x_d = x.rearrange("b t c -> (b t) c")
    out_d = out.rearrange("b t c -> (b t) c")

    q_s = nc.dram_tensor("q_parts", [2, HEADS * HD, T], F32, kind="Internal").ap()
    k_s = nc.dram_tensor("k_parts", [2, KVH * HD, T], F32, kind="Internal").ap()
    v_s = nc.dram_tensor("v_parts", [KVH, P, NT, 2 * HD], F32, kind="Internal").ap()
    aug_s = nc.dram_tensor("aug_rows", [HEADS * AUG, T], F32, kind="Internal").ap()
    o_s = nc.dram_tensor("o_parts", [3, HEADS * HD, T], F32, kind="Internal").ap()

    with ExitStack() as ctx:
        def sb(name, shape, dt, c=ctx):
            return c.enter_context(nc.sbuf_tensor(name, shape, dt))

        def bank(name, c=ctx):
            return c.enter_context(nc.psum_tensor(name, [P, CH], F32))

        def sem(name):
            return ctx.enter_context(nc.semaphore(name))

        xh = sb("xh", [P, KT, T], F16)
        xl = sb("xl", [P, KT, T], F16)
        acc = sb("acc", [P, NT, C], F32)
        ident = sb("ident", [P, P], F32)
        identb = sb("identb", [P, P], BF16)
        mask_ts = sb("mask_ts", [P, P], BF16)
        mask_st = sb("mask_st", [P, P], BF16)
        sc = [sb(f"sc{m}", [P, NG, SB], F32) for m in range(3)]
        tab = sb("tab", [P, NG, 6], F32)
        oscale = sb("oscale", [P, KT], F32)

        preamble(nc, locals())
        main_loop(nc, locals())
        epilogue(nc, locals())


def preamble(nc, e):
    (x_d, Wq, Wkv, scales, augq, augk, q_s, k_s, v_s, aug_s) = (
        e[n] for n in ("x_d", "Wq", "Wkv", "scales", "augq", "augk", "q_s", "k_s", "v_s", "aug_s"))
    xh, xl, acc, ident, identb, mask_ts, mask_st, sc, tab, oscale = (
        e[n] for n in ("xh", "xl", "acc", "ident", "identb", "mask_ts", "mask_st", "sc", "tab", "oscale"))
    with ExitStack() as ctx:
        def sb(name, shape, dt):
            return ctx.enter_context(nc.sbuf_tensor(name, shape, dt))

        def sem(name):
            return ctx.enter_context(nc.semaphore(name))

        xin = [sb(f"xin{i}", [P, TPC, C], F32) for i in range(2)]
        xt = [sb(f"xt{i}", [P, KT, CH], F32) for i in range(2)]
        wq = sb("wq", [P, KT, C], F32)
        wqn = sb("wqn", [P, KT, C], F32)
        wkv = sb("wkv", [P, KT, 2 * KVH * HD], F32)
        ph = [sb(f"ph{i}", [P, CH], F32R) for i in range(2)]
        pl = [sb(f"pl{i}", [P, CH], F32R) for i in range(2)]
        vt = sb("vt", [P, TPC, KVH, 2, HD], F32R)
        augf = sb("augf", [P, T], F32)
        augr = sb("augr", [P, T], F32R)
        stats = sb("stats", [P, TPC, 6], F32)
        mv = sb("mv", [P, TPC, 2], F32)
        ve = sb("ve", [P, TPC], F32)
        sd = sb("sd", [P, TPC], F32)
        rs = sb("rs", [P, TPC], F32)
        nt_ = sb("nt_", [P, TPC], F32)
        sraw = [sb(f"sraw{m}", [P, NG * SB], F32) for m in range(3)]
        big = [sb(f"big{m}", [P, 2 * NG if m < 2 else KT], F32) for m in range(3)]
        low = [sb(f"low{m}", [P, 2 * NG if m < 2 else KT], F32) for m in range(3)]
        inv = [sb(f"inv{m}", [P, 2 * NG if m < 2 else KT], F32) for m in range(3)]
        rr = sb("rr", [P, 2 * NG], F32)
        rmax = sb("rmax", [P, 1], F32)
        rall = sb("rall", [P, 1], F32)
        rinv = sb("rinv", [P, 1], F32)
        turn = [ctx.enter_context(nc.psum_tensor(f"turn{i}", [P, CH], F32)) for i in range(2)]
        proj = [ctx.enter_context(nc.psum_tensor(f"proj{i}", [P, CH], F32)) for i in range(2)]
        vps = ctx.enter_context(nc.psum_tensor("vps", [P, CH], F32))

        x_in = [sem(f"x_in{i}") for i in range(2)]
        w_in = sem("w_in")
        wq_done = sem("wq_done")
        sc_in = sem("sc_in")
        aug_in = sem("aug_in")
        ident_done = sem("ident_done")
        pool_step = sem("pool_step")
        dve_step = sem("dve_step")
        var_done = sem("var_done")
        sqrt_done = sem("sqrt_done")
        xn_done = sem("xn_done")
        turned = sem("turned")
        xt_done = sem("xt_done")
        xh_done = sem("xh_done")
        xl_done = sem("xl_done")
        projected = sem("projected")
        part_hi = sem("part_hi")
        part_lo = sem("part_lo")
        v_sum = sem("v_sum")
        v_hi = sem("v_hi")
        v_lo = sem("v_lo")
        q_out = [sem(f"q_out{i}") for i in range(2)]
        v_out = sem("v_out")
        aug_done = sem("aug_done")
        aug_out = sem("aug_out")
        rmax_done = sem("rmax_done")
        rall_done = sem("rall_done")
        NPROJ = KVH + 1

        with nc.Block() as block:
            @block.sync
            def _(sp):
                def load_x(c):
                    if c >= 2:
                        sp.wait_ge(turned, KT * (c - 1))
                    sp.dma_start(xin[c % 2][:], x_d[c * CH:(c + 1) * CH, :].rearrange("(j p) h -> p j h", p=P)
                                 ).then_inc(x_in[c % 2], 16)

                load_x(0)
                sp.dma_start(wqn[:], Wq.rearrange("(k p) n -> p k n", p=P)).then_inc(w_in, 16)
                sp.dma_start(wkv[:], Wkv.rearrange("(k p) n -> p k n", p=P)).then_inc(w_in, 16)
                load_x(1)
                for m in range(2):
                    sp.dma_start(sraw[m][:].rearrange("p (t b) -> p t b", b=C // BLOCK),
                                 scales[m].rearrange("(t p) b -> p t b", p=P)).then_inc(sc_in, 16)
                sp.dma_start(sraw[2][:].rearrange("p (k b) -> p k b", k=KT),
                             scales[2].rearrange("(k p) b -> p k b", p=P)).then_inc(sc_in, 16)
                sp.dma_start(augf[:], augq).then_inc(aug_in, 16)
                sp.wait_ge(aug_done, 1)
                sp.dma_start(aug_s, augr[:].bitcast(F32)).then_inc(aug_out, 16)
                for c in range(NCH):
                    cols = slice(c * CH, (c + 1) * CH)
                    if c + 2 < NCH:
                        load_x(c + 2)
                    for m in range(NPROJ):
                        n = NPROJ * c + m
                        dst = q_s if m < KVH else k_s
                        rows = slice(m * P, (m + 1) * P) if m < KVH else slice(0, P)
                        sp.wait_ge(part_lo, n + 1)
                        sp.dma_start(dst[0, rows, cols], ph[n % 2][:].bitcast(F32)).then_inc(q_out[n % 2], 16)
                        sp.dma_start(dst[1, rows, cols], pl[n % 2][:].bitcast(F32)).then_inc(q_out[n % 2], 16)
                    sp.wait_ge(v_lo, c + 1)
                    for g in range(KVH):
                        sp.dma_start(v_s[g, :, TPC * c:TPC * (c + 1), :],
                                     vt[:, :, g, :, :].rearrange("p j a d -> p j (a d)").bitcast(F32)).then_inc(v_out, 16)
                for i in range(2):
                    sp.wait_ge(q_out[i], 32 * (NPROJ * NCH // 2))
                sp.wait_ge(v_out, 16 * KVH * NCH)
                sp.wait_ge(aug_out, 16)

            @block.gpsimd
            def _(pool):
                nc.gpsimd.memset(ident[:], 0.0).then_inc(pool_step, 1)
                nc.gpsimd.memset(mask_ts[:], 0.0).then_inc(pool_step, 1)
                nc.gpsimd.memset(mask_st[:], 0.0).then_inc(pool_step, 1)
                pool.wait_ge(pool_step, 3)
                nc.gpsimd.affine_select(out=ident[:], in_=ident[:], compare_op=ALU.not_equal, fill=1.0, base=0,
                                        pattern=[[-1, P]], channel_multiplier=1).then_inc(pool_step, 1)
                nc.gpsimd.affine_select(out=mask_ts[:], in_=mask_ts[:], compare_op=ALU.is_ge, fill=-1e30, base=0,
                                        pattern=[[-1, P]], channel_multiplier=1).then_inc(pool_step, 1)
                nc.gpsimd.affine_select(out=mask_st[:], in_=mask_st[:], compare_op=ALU.is_ge, fill=-1e30, base=0,
                                        pattern=[[1, P]], channel_multiplier=-1).then_inc(pool_step, 1)
                pool.wait_ge(pool_step, 6)
                nc.gpsimd.tensor_copy(identb[:], ident[:]).then_inc(ident_done, 1)
                nc.gpsimd.memset(acc[:], 0.0).then_inc(pool_step, 1)
                pool.wait_ge(rmax_done, 1)
                nc.gpsimd.partition_all_reduce(rall[:], rmax[:], P, RMAX).then_inc(rall_done, 1)

            @block.tensor
            def _(pe):
                pe.wait_ge(ident_done, 1)
                for c in range(NCH):
                    pe.wait_ge(xn_done, c + 1)
                    if c >= 2:
                        pe.wait_ge(projected, NPROJ * (c - 1))
                        pe.wait_ge(v_sum, c - 1)
                    for k in range(KT):
                        n = KT * c + k
                        if n >= 2:
                            pe.wait_ge(xl_done, n - 1)
                            pe.wait_ge(xt_done, n - 1)
                        for j in range(TPC):
                            mm = nc.tensor.transpose(turn[n % 2][:, j * P:(j + 1) * P],
                                                     xin[c % 2][:, j, k * P:(k + 1) * P], ident[:])
                        mm.then_inc(turned, 1)
                    pe.wait_ge(xt_done, KT * (c + 1))
                    pe.wait_ge(w_in, 32)
                    pe.wait_ge(wq_done, KT)
                    for m in range(NPROJ):
                        n = NPROJ * c + m
                        if n >= 2:
                            pe.wait_ge(part_lo, n - 1)
                        for k in range(KT):
                            if m < KVH:
                                lhs = wq[:, k, m * P:(m + 1) * P]
                            else:
                                lhs = wkv[:, k, 0:KVH * HD]
                            mm = nc.tensor.matmul(proj[n % 2][:], lhs, xt[c % 2][:, k, :],
                                                  start=(k == 0), stop=(k == KT - 1))
                        mm.then_inc(projected, 1)
                    if c >= 1:
                        pe.wait_ge(v_lo, c)
                    for j in range(TPC):
                        for k in range(KT):
                            mm = nc.tensor.matmul(vps[:, j * P:(j + 1) * P], xt[c % 2][:, k, j * P:(j + 1) * P],
                                                  wkv[:, k, KVH * HD:], start=(k == 0), stop=(k == KT - 1))
                    mm.then_inc(v_sum, 1)

            @block.scalar
            def _(act):
                def root(c):
                    act.wait_ge(var_done, c + 1)
                    nc.scalar.activation(sd[:], ve[:], ACT.Sqrt).then_inc(sqrt_done, 1)

                root(0)
                for c in range(NCH):
                    cols = slice(c * CH, (c + 1) * CH)
                    if c >= 2:
                        act.wait_ge(v_sum, c - 1)
                    for k in range(KT):
                        n = KT * c + k
                        act.wait_ge(turned, n + 1)
                        nc.scalar.activation(xt[c % 2][:, k, :], turn[n % 2][:], ACT.Copy).then_inc(xt_done, 1)
                        nc.scalar.activation(xh[:, k, cols], turn[n % 2][:], ACT.Copy, scale=XS).then_inc(xh_done, 1)
                    if c + 1 < NCH:
                        root(c + 1)
                    for m in range(NPROJ):
                        n = NPROJ * c + m
                        act.wait_ge(projected, n + 1)
                        if n >= 2:
                            act.wait_ge(q_out[n % 2], 32 * (n // 2))
                        nc.scalar.activation(ph[n % 2][:], proj[n % 2][:], ACT.Copy,
                                             scale=float(np.float32(1 / np.sqrt(np.float32(HD)))) if m < KVH else 1.0
                                             ).then_inc(part_hi, 1)
                    act.wait_ge(v_sum, c + 1)
                    if c >= 1:
                        act.wait_ge(v_out, 16 * KVH * c)
                    nc.scalar.activation(vt[:, :, :, 0, :], vps[:].rearrange("p (j g d) -> p j g d", j=TPC, g=KVH),
                                         ACT.Copy).then_inc(v_hi, 1)

            @block.vector
            def _(dve):
                steps = [0]

                def link(ins):
                    steps[0] += 1
                    ins.then_inc(dve_step, 1)
                    dve.wait_ge(dve_step, steps[0])

                def layer_norm(c):
                    xc = xin[c % 2]
                    dve.wait_ge(x_in[c % 2], 16 * (c // 2 + 1))
                    for j in range(TPC):
                        last = nc.vector.bn_stats(stats[:, j, :], xc[:, j, :])
                    link(last)
                    for j in range(TPC):
                        last = nc.vector.bn_aggr(mv[:, j, :], stats[:, j, :])
                    link(last)
                    if c:
                        dve.wait_ge(sqrt_done, c)
                    link(nc.vector.tensor_scalar(ve[:], mv[:, :, 1], EPS, None, ALU.add))
                    nc.vector.tensor_copy(nt_[:], ve[:]).then_inc(var_done, 1)
                    dve.wait_ge(sqrt_done, c + 1)
                    link(nc.vector.reciprocal(rs[:], sd[:]))
                    link(nc.vector.tensor_tensor(nt_[:], rs[:], rs[:], ALU.mult))
                    link(nc.vector.tensor_tensor(nt_[:], nt_[:], ve[:], ALU.mult))
                    link(nc.vector.tensor_scalar(nt_[:], nt_[:], -0.5, 1.5, ALU.mult, ALU.add))
                    link(nc.vector.tensor_tensor(rs[:], rs[:], nt_[:], ALU.mult))
                    for j in range(TPC):
                        last = nc.vector.tensor_scalar(xc[:, j, :], xc[:, j, :], mv[:, j, 0:1], rs[:, j:j + 1],
                                                       ALU.subtract, ALU.mult)
                    last.then_inc(xn_done, 1)

                def powers(src, dst, idst, step):
                    link(nc.vector.tensor_reduce(dst, src, AX.X, ALU.max))
                    link(nc.vector.tensor_reduce(idst, src, AX.X, ALU.min))
                    link(nc.vector.scalar_tensor_tensor(dst, idst, -1.0, dst, ALU.mult, ALU.max))
                    link(nc.vector.tensor_scalar(dst, dst, 1 / LIM, LIM, ALU.max, ALU.min))
                    link(nc.vector.tensor_scalar(dst.bitcast(I32), dst.bitcast(I32), 0x7F800000, None, ALU.bitwise_and))
                    link(nc.vector.tensor_scalar(idst.bitcast(I32), dst.bitcast(I32), -1.0, float(254 << 23),
                                                 ALU.mult, ALU.add))

                def scale_tables():
                    dve.wait_ge(sc_in, 48)
                    for m in range(2):
                        src = sraw[m][:].rearrange("p (t b) -> p t b", b=C // BLOCK)
                        powers(src, big[m][:], inv[m][:], 0)
                        link(nc.vector.scalar_tensor_tensor(
                            sc[m][:].rearrange("p g (a b) -> p (g a) b", a=2), src, NIB * WS,
                            inv[m][:].unsqueeze(2).broadcast_to([P, 2 * NG, C // BLOCK]), ALU.mult, ALU.mult))
                    src = sraw[2][:].rearrange("p (k b) -> p k b", k=KT)
                    powers(src, big[2][:], inv[2][:], 0)
                    for k in range(KT):
                        link(nc.vector.tensor_scalar(
                            sc[2][:].rearrange("p g (k b) -> p k g b", k=KT)[:, k],
                            src[:, k, :].rearrange("p (g b) -> p g b", g=NG), inv[2][:, k:k + 1], NIB * WS,
                            ALU.mult, ALU.mult))
                    rows = big[0][:].rearrange("p (g a) -> p g a", a=2)
                    link(nc.vector.tensor_scalar(tab[:, :, 0:2], rows, float(np.sqrt(GELU_A)) / (XS * WS), None, ALU.mult))
                    link(nc.vector.tensor_scalar(tab[:, :, 2:4], rows, GELU_C / (XS * WS), None, ALU.mult))
                    link(nc.vector.tensor_tensor(rr[:], big[0][:], big[1][:], ALU.mult))
                    nc.vector.tensor_reduce(rmax[:], rr[:], AX.X, ALU.max).then_inc(rmax_done, 1)
                    dve.wait_ge(rall_done, 1)
                    link(nc.vector.tensor_scalar(rinv[:].bitcast(I32), rall[:].bitcast(I32), -1.0, float(254 << 23),
                                                 ALU.mult, ALU.add))
                    link(nc.vector.tensor_scalar(tab[:, :, 4:6], rr[:].rearrange("p (g a) -> p g a", a=2),
                                                 rinv[:, 0:1], None, ALU.mult))
                    link(nc.vector.tensor_scalar(oscale[:], big[2][:], rall[:, 0:1], 1 / (WS * IS), ALU.mult, ALU.mult))

                layer_norm(0)
                dve.wait_ge(w_in, 32)
                for k in range(KT):
                    nc.vector.tensor_copy(wq[:, k, :].rearrange("p (g r d) -> p g r d", r=REP, g=KVH),
                                          wqn[:, k, :].rearrange("p (r g d) -> p g r d", r=REP, g=KVH)
                                          ).then_inc(wq_done, 1)
                dve.wait_ge(aug_in, 16)
                nc.vector.tensor_copy(augr[:], augf[:]).then_inc(aug_done, 1)
                for c in range(NCH):
                    cols = slice(c * CH, (c + 1) * CH)
                    for k in range(KT):
                        n = KT * c + k
                        dve.wait_ge(xh_done, n + 1)
                        nc.vector.scalar_tensor_tensor(xl[:, k, cols], turn[n % 2][:], XS, xh[:, k, cols],
                                                       ALU.mult, ALU.subtract).then_inc(xl_done, 1)
                    if c + 1 < NCH:
                        layer_norm(c + 1)
                    for m in range(NPROJ):
                        n = NPROJ * c + m
                        dve.wait_ge(part_hi, n + 1)
                        if n >= 2:
                            dve.wait_ge(q_out[n % 2], 32 * (n // 2))
                        nc.vector.scalar_tensor_tensor(
                            pl[n % 2][:], proj[n % 2][:],
                            float(np.float32(1 / np.sqrt(np.float32(HD)))) if m < KVH else 1.0,
                            ph[n % 2][:].bitcast(F32), ALU.mult, ALU.subtract).then_inc(part_lo, 1)
                    dve.wait_ge(v_hi, c + 1)
                    nc.vector.tensor_tensor(vt[:, :, :, 1, :], vps[:].rearrange("p (j g d) -> p j g d", j=TPC, g=KVH),
                                            vt[:, :, :, 0, :].bitcast(F32), ALU.subtract).then_inc(v_lo, 1)
                    if c == 0:
                        scale_tables()
                dve.wait_ge(pool_step, 7)


def main_loop(nc, e):
    packed, augk = e["packed"], e["augk"]
    q_s, k_s, v_s, aug_s, o_s = (e[n] for n in ("q_s", "k_s", "v_s", "aug_s", "o_s"))
    xh, xl, acc, ident, identb, mask_ts, mask_st, sc, tab = (
        e[n] for n in ("xh", "xl", "acc", "ident", "identb", "mask_ts", "mask_st", "sc", "tab"))
    with ExitStack() as ctx:
        def sb(name, shape, dt):
            return ctx.enter_context(nc.sbuf_tensor(name, shape, dt))

        def bank(name):
            return ctx.enter_context(nc.psum_tensor(name, [P, CH], F32))

        def sem(name):
            return ctx.enter_context(nc.semaphore(name))

        raw = [sb(f"raw{m}", [P, WORDS], I32) for m in range(3)]
        dec = sb("dec", [P, 2, WORDS], I32)
        wf = sb("wf", [P, 2 * WORDS], F32)
        wh = [sb(f"wh{b}", [P, 3, 2, C], F16) for b in range(2)]
        wl = [sb(f"wl{b}", [P, 3, 2, C], F16) for b in range(2)]
        cur = [sb(f"cur{b}", [P, 6], F32) for b in range(2)]
        gl = [sb(f"gl{a}", [P, CH], F32) for a in range(2)]
        prod = [sb(f"prod{a}", [P, CH], F32) for a in range(2)]
        ih = [sb(f"ih{b}", [P, 2, CH], F16) for b in range(2)]
        il = [sb(f"il{b}", [P, 2, CH], F16) for b in range(2)]
        qst = sb("qst", [P, NCH, CH], F32R)
        kst = [sb(f"kst{b}", [P, T], F32R) for b in range(2)]
        vst = [sb(f"vst{b}", [P, NT, 3 * HD], F32R) for b in range(2)]
        PR, PP = 3, 4
        p32 = [sb(f"p32_{i}", [P, CH], F32) for i in range(PR)]
        phi = [sb(f"phi{i}", [P, CH], F32R) for i in range(PP)]
        plo = [sb(f"plo{i}", [P, CH], F32R) for i in range(PP)]
        mxp = [sb(f"mxp{i}", [P, TPC, NCH], F32) for i in range(2)]
        mxc = sb("mxc", [P, TPC], F32)
        nmx = sb("nmx", [P, TPC, NB], F32)
        bhi = sb("bhi", [NB, CH], F32R)
        keep = sb("keep", [NB, 1], F32)
        oraw = [sb(f"oraw{i}", [3 * HD, CH], F32) for i in range(2)]

        gate_ps, up_ps, turn_ps, max_ps, score_ps, o_ps = (
            bank(n) for n in ("gate_ps", "up_ps", "turn_ps", "max_ps", "score_ps", "o_ps"))
        down_ps = [bank(f"down_ps{i}") for i in range(2)]
        pair_ps = (max_ps, turn_ps)

        raw_in = [sem(f"raw_in{m}") for m in range(3)]
        kv_in = [sem(f"kv_in{b}") for b in range(2)]
        q_in = [sem(f"q_in{c}") for c in range(NCH)]
        const_in = sem("const_in")
        const_r = sem("const_r")
        keep_in = sem("keep_in")
        o_out = [sem(f"o_out{i}") for i in range(2)]
        gate_done = sem("gate_done")
        up_done = sem("up_done")
        down_done = sem("down_done")
        max_done = sem("max_done")
        maxt_done = sem("maxt_done")
        score_done = sem("score_done")
        pv_done = sem("pv_done")
        wturn_done = sem("wturn_done")
        square_done = sem("square_done")
        inner_done = sem("inner_done")
        tanh_done = sem("tanh_done")
        gelu_done = sem("gelu_done")
        prod_done = sem("prod_done")
        ih_done = sem("ih_done")
        il_done = sem("il_done")
        exp_done = sem("exp_done")
        phi_done = sem("phi_done")
        plo_done = sem("plo_done")
        bhi_done = sem("bhi_done")
        brow_done = sem("brow_done")
        oraw_done = sem("oraw_done")
        red_done = sem("red_done")
        mxc_done = sem("mxc_done")
        nmx_done = sem("nmx_done")
        acc_done = sem("acc_done")
        cur_done = sem("cur_done")
        dec_step = sem("dec_step")
        wf_done = sem("wf_done")
        wh_done = sem("wh_done")
        wl_done = sem("wl_done")

        def loop(eng, body):
            with eng.Fori(0, HEADS // 2) as pair:
                for par in range(2):
                    body(pair * 2 + par, par, pair)

        SEEDED = (gelu_done, prod_done, acc_done, red_done, brow_done, exp_done, oraw_done, plo_done, il_done,
                  pv_done, down_done, mxc_done, maxt_done, square_done, *o_out)

        def after(signals):
            return signals + 1

        def since(base, k, ring):
            return base + max(k - ring + 1, 0)

        GU = 2 * NCH
        ND = NCH * TPC

        def decode_step(dve, m, step, g, before, n_w):
            if step == 0:
                dve.wait_ge(raw_in[m], (before + 1) * 16)
                nc.vector.tensor_scalar(dec[:, 0], raw[m][:], 28, 19, ALU.logical_shift_left,
                                        ALU.arith_shift_right).then_inc(dec_step, 1)
            if step == 1:
                nc.vector.tensor_scalar(dec[:, 1], raw[m][:], 24, 19, ALU.logical_shift_left,
                                        ALU.arith_shift_right).then_inc(dec_step, 1)
            if step == 2:
                dve.wait_ge(dec_step, before * 9 + m * 3 + 2)
                nc.vector.tensor_scalar(dec[:].rearrange("p a w -> p (a w)"), dec[:].rearrange("p a w -> p (a w)"),
                                        0x8E00, None, ALU.bitwise_and).then_inc(dec_step, 1)
            if step >= 3:
                b = step - 3
                if b == 0:
                    dve.wait_ge(dec_step, before * 9 + m * 3 + 3)
                    dve.wait_ge(wturn_done, before * 6 + 2 * m)
                codes = dec[:, b].bitcast(F16).rearrange("p (s j two) -> p s j two", j=BLOCK // 2, two=2)[:, :, :, 0]
                nc.vector.tensor_tensor(
                    wf[:].rearrange("p (s j two) -> p s j two", j=BLOCK // 2, two=2)[:, :, :, b], codes,
                    sc[m][:, bass.ds(g, 1), :].rearrange("p o s -> p (o s)").unsqueeze(2).broadcast_to([P, SB, BLOCK // 2]),
                    ALU.mult).then_inc(wf_done, 1)

        def turn_weights(pe, m, a, before, maxima):
            pe.wait_ge(wf_done, before * 6 + 2 * m + 2)
            if maxima is not None or 2 * m + a >= 2:
                pe.wait_ge(wl_done, before * 6 + 2 * m + a - 1)
            if maxima is not None:
                pe.wait_ge(red_done, after(maxima))
            for k in range(KT):
                at = a * C + k * P if m < 2 else k * GROUP + a * P
                mm = nc.tensor.transpose(pair_ps[a][:, k * P:(k + 1) * P], wf[:, at:at + P], ident[:])
            mm.then_inc(wturn_done, 1)

        def weights_hi(act, m, a, before, b):
            act.wait_ge(wturn_done, before * 6 + 2 * m + a + 1)
            if m == 2:
                act.wait_ge(cur_done, before + 1)
            nc.scalar.activation(wh[b][:, m, a, :], pair_ps[a][:], ACT.Copy,
                                 scale=1.0 if m < 2 else cur[b][:, 4 + a:5 + a]).then_inc(wh_done, 1)

        def weights_lo(dve, m, a, before, b):
            dve.wait_ge(wh_done, before * 6 + 2 * m + a + 1)
            nc.vector.scalar_tensor_tensor(wl[b][:, m, a, :], pair_ps[a][:], 1.0 if m < 2 else cur[b][:, 4 + a:5 + a],
                                           wh[b][:, m, a, :], ALU.mult, ALU.subtract).then_inc(wl_done, 1)

        with nc.Block() as block:
            @block.sync
            def _(sp):
                def load_raw(m, g):
                    if m < 2:
                        src = packed[m].rearrange("(g a p) w -> g p a w", a=2, p=P)[bass.ds(g, 1)]
                        dst = raw[m][:].rearrange("p (a w) -> p a w", a=2)
                    else:
                        src = packed[2].rearrange("(k p) (g w) -> g p k w", p=P, w=GROUP // 2)[bass.ds(g, 1)]
                        dst = raw[m][:].rearrange("p (k w) -> p k w", k=KT)
                    sp.dma_start(dst, src.rearrange("o p a w -> (o p) a w")).then_inc(raw_in[m], 16)

                def load_kv(i, b):
                    g = i // REP
                    for part, at in ((0, HD), (0, 2 * HD), (1, 3 * HD)):
                        sp.dma_start(kst[b][at:at + HD, :].bitcast(F32), k_s[part, bass.ds(g * HD, HD), :]).then_inc(kv_in[b], 16)
                    sp.dma_start(vst[b][:, :, 0:2 * HD].bitcast(F32), v_s[bass.ds(g, 1)].rearrange("o p t d -> (o p) t d")
                                 ).then_inc(kv_in[b], 16)

                def load_q(i, c):
                    cols = slice(c * CH, (c + 1) * CH)
                    sp.dma_start(qst[0:AUG, c, :].bitcast(F32), aug_s[bass.ds(i * AUG, AUG), cols]).then_inc(q_in[c], 16)
                    for part, at in ((0, HD), (1, 2 * HD), (0, 3 * HD)):
                        sp.dma_start(qst[at:at + HD, c, :].bitcast(F32), q_s[part, bass.ds(i * HD, HD), cols]).then_inc(q_in[c], 16)

                sp.dma_start(p32[0][0:AUG, :], augk[:, 0:CH]).then_inc(const_in, 16)
                for m in range(3):
                    load_raw(m, 0)
                for seeded in SEEDED:
                    sp.sem_inc(seeded, 1)
                for c in range(1, NCH):
                    sp.wait_ge(const_r, c)
                    sp.dma_start(p32[0][0:AUG, :], augk[:, c * CH:(c + 1) * CH]).then_inc(const_in, 16)
                sp.wait_ge(const_r, NCH + 3)
                load_kv(0, 0)
                for c in range(NCH):
                    load_q(0, c)
                for m in range(3):
                    sp.wait_ge(wf_done, 2 * m + 2)
                    load_raw(m, 1)

                def body(i, par, pair):
                    nxt = (i + 1) % HEADS
                    sp.wait_ge(pv_done, after(i * NBLK))
                    load_kv(nxt, 1 - par)
                    for c in range(NCH):
                        sp.wait_ge(score_done, i * NBLK + BLK_END[c])
                        load_q(nxt, c)
                        if c:
                            store_o(i, c - 1)
                    for m in range(3):
                        sp.wait_ge(wf_done, (i + 1) * 6 + 2 * m + 2)
                        load_raw(m, (i + 2) % HEADS)
                    store_o(i, NCH - 1)

                def store_o(i, c):
                    sp.wait_ge(oraw_done, after(i * NCH + c + 1))
                    for part in range(3):
                        sp.dma_start(o_s[part, bass.ds(i * HD, HD), c * CH:(c + 1) * CH],
                                     oraw[c % 2][part * HD:(part + 1) * HD, :]).then_inc(o_out[c % 2], 16)

                loop(sp, body)
                for m in range(3):
                    sp.wait_ge(raw_in[m], 16 * (HEADS + 2))
                sp.wait_ge(kv_in[0], 64 * (HEADS // 2 + 1))
                for c in range(NCH):
                    sp.wait_ge(q_in[c], 64 * (HEADS + 1))
                for b in range(2):
                    sp.wait_ge(o_out[b], after(48 * HEADS * NCH // 2))

            @block.tensor
            def _(pe):
                for m in range(3):
                    for a in range(2):
                        turn_weights(pe, m, a, 0, None)

                def body(i, par, pair):
                    def mlp(s, half):
                        kind, w, a, part = PIECES[s]
                        if kind == "down":
                            n = w * TPC + a
                            dst = down_ps[n % 2]
                            for q in range(3 * half, 3 * half + 3):
                                if q == 0:
                                    pe.wait_ge(ih_done, i * GU + 2 * w + 2)
                                    pe.wait_ge(acc_done, after(since(i * ND, n, 2)))
                                b, term = q // 3, q % 3
                                if term == 2:
                                    pe.wait_ge(il_done, after(i * GU + 2 * w + b + 1))
                                lhs = (ih, ih, il)[term][w % 2][:, b, a * P:(a + 1) * P]
                                rhs = (wh, wl, wh)[term][par][:, 2, b, :]
                                mm = nc.tensor.matmul(dst[:], lhs, rhs, start=(q == 0), stop=(q == 5))
                            if half:
                                mm.then_inc(down_done, 1)
                            return
                        m = 0 if kind == "gate" else 1
                        dst = gate_ps if m == 0 else up_ps
                        n = 2 * w + a
                        for q in range(6 * part + 3 * half, 6 * part + 3 * half + 3):
                            if q == 0:
                                pe.wait_ge(gelu_done if m == 0 else prod_done, after(i * GU + n))
                            k, term = q // 3, q % 3
                            lhs = (wh, wl, wh)[term][par][:, m, a, k * P:(k + 1) * P]
                            rhs = (xh, xh, xl)[term][:, k, w * CH:(w + 1) * CH]
                            mm = nc.tensor.matmul(dst[:], lhs, rhs, start=(q == 0), stop=(q == 11))
                        if part and half:
                            mm.then_inc(gate_done if m == 0 else up_done, 1)

                    def maximum(n):
                        c, t, m = MAXP[n]
                        if t == 0 and m == 0:
                            pe.wait_ge(q_in[c], (i + 1) * 64)
                        pe.wait_ge(red_done, after(since(i * NMAX, n, 2)))
                        dst = pair_ps[n % 2]
                        diag = m == c
                        cols = (t + 1) * P if diag else CH
                        mm = nc.tensor.matmul(dst[:, 0:cols], qst[:, c, t * P:(t + 1) * P],
                                                 kst[par][:, m * CH:m * CH + cols], start=True, stop=True)
                        if diag:
                            mm = nc.tensor.matmul(dst[:, cols - P:cols], identb[:], mask_ts[:], start=False,
                                                     stop=True, skip_group_check=True)
                        mm.then_inc(max_done, 1)

                    def turn_max(c):
                        pe.wait_ge(nmx_done, i * NCH + c + 1)
                        pe.wait_ge(exp_done, after(i * NBLK + BLOCKS_BY_TURN[c]))
                        for t in range(TPC):
                            mm = nc.tensor.transpose(score_ps[0:NB, t * P:(t + 1) * P], nmx[:, t, :], ident[:])
                        mm.then_inc(maxt_done, 1)

                    def score(n):
                        c, tiles, _ = BLOCKS[n]
                        if n in BLOCKS_BY_TURN:
                            pe.wait_ge(brow_done, after(i * NCH + BLOCKS_BY_TURN.index(n) + 1))
                        pe.wait_ge(exp_done, after(i * NBLK + n))
                        for at, (j, col, tok) in enumerate(tiles):
                            width = CH - tok
                            diag = j >= TPC * c
                            mm = nc.tensor.matmul(score_ps[:, col:col + width], kst[par][:, j * P:(j + 1) * P],
                                                  qst[:, c, tok:CH], start=True, stop=True,
                                                  skip_group_check=True)
                            if diag:
                                mm = nc.tensor.matmul(score_ps[:, col:col + P], identb[:], mask_st[:], start=False,
                                                      stop=True, skip_group_check=True)
                        mm.then_inc(score_done, 1)

                    def values(n):
                        c, tiles, _ = BLOCKS[n]
                        if n == 0 or BLOCKS[n - 1][0] != c:
                            pe.wait_ge(oraw_done, after(i * NCH + c))
                        pe.wait_ge(phi_done, i * NBLK + n + 1)
                        pe.wait_ge(plo_done, after(i * NBLK + n + 1))
                        for src in (phi, plo):
                            for j, col, tok in tiles:
                                width = CH - tok
                                mm = nc.tensor.matmul(
                                    o_ps[0:3 * HD, tok:CH], vst[par][:, j, :], src[n % PP][:, col:col + width],
                                    start=(j == 0 and src is phi), stop=(n == BLK_END[c] - 1 and src is plo),
                                    skip_group_check=True)
                        mm.then_inc(pv_done, 1)

                    pe.wait_ge(kv_in[par], (pair + 1) * 64)
                    pe.wait_ge(wl_done, (i + 1) * 6)
                    for s in range(SLOTS):
                        if s in SCORE_AT:
                            score(SCORE_AT[s])
                        if MAX_AT[s]:
                            maximum(MAX_AT[s][0])
                        mlp(s, 0)
                        if s in VALUES_AT:
                            values(VALUES_AT[s])
                        if len(MAX_AT[s]) > 1:
                            maximum(MAX_AT[s][1])
                        mlp(s, 1)
                        if s in TURN_MAX_AT:
                            turn_max(TURN_MAX_AT[s])
                        if s in TURN_W_AT:
                            m, a = TURN_W_AT[s]
                            turn_weights(pe, m, a, i + 1, (i + 1) * NMAX)

                loop(pe, body)

            @block.scalar
            def _(act):
                for m in range(3):
                    for a in range(2):
                        weights_hi(act, m, a, 0, 0)

                def body(i, par, pair):
                    def square(n):
                        a = n % 2
                        act.wait_ge(gate_done, i * GU + n + 1)
                        act.wait_ge(prod_done, after(since(i * GU, n, 2)))
                        nc.scalar.activation(gl[a][:], gate_ps[:], ACT.Square,
                                             scale=cur[par][:, a:a + 1]).then_inc(square_done, 1)

                    def tanh(n):
                        a = n % 2
                        act.wait_ge(inner_done, i * GU + n + 1)
                        nc.scalar.activation(gl[a][:], gl[a][:], ACT.Tanh,
                                             scale=cur[par][:, 2 + a:3 + a]).then_inc(tanh_done, 1)

                    def exp(n):
                        cols = BLOCKS[n][2]
                        act.wait_ge(score_done, i * NBLK + n + 1)
                        act.wait_ge(plo_done, after(since(i * NBLK, n, PR)))
                        nc.scalar.activation(p32[n % PR][:, 0:cols], score_ps[:, 0:cols], ACT.Exp).then_inc(exp_done, 1)

                    def max_hi(c):
                        act.wait_ge(maxt_done, after(i * NCH + c + 1))
                        act.wait_ge(brow_done, after(i * NCH + c))
                        nc.scalar.activation(bhi[:], score_ps[0:NB, :], ACT.Copy).then_inc(bhi_done, 1)

                    def o_copy(c):
                        act.wait_ge(pv_done, after(i * NBLK + BLK_END[c]))
                        act.wait_ge(o_out[c % 2], after((i * 2 + c // 2) * 48))
                        nc.scalar.activation(oraw[c % 2][:], o_ps[0:3 * HD, :], ACT.Copy).then_inc(oraw_done, 1)

                    act.wait_ge(cur_done, i + 1)
                    for s in range(SLOTS + 2):
                        if s - 1 in TURN_MAX_AT:
                            max_hi(TURN_MAX_AT[s - 1])
                        if 1 <= s <= SLOTS and PIECES[s - 1][0] == "gate" and PIECES[s - 1][3]:
                            square(2 * PIECES[s - 1][1] + PIECES[s - 1][2])
                        if s in SCORE_AT:
                            exp(SCORE_AT[s])
                        if 2 <= s and PIECES[s - 2][0] == "gate" and PIECES[s - 2][3]:
                            tanh(2 * PIECES[s - 2][1] + PIECES[s - 2][2])
                        if s - 1 in TURN_W_AT:
                            m, a = TURN_W_AT[s - 1]
                            if (m, a) == (0, 0):
                                act.wait_ge(down_done, after(i * ND))
                            weights_hi(act, m, a, i + 1, 1 - par)
                        if VALUES_AT.get(s, -1) + 1 in BLK_END:
                            o_copy(BLOCKS[VALUES_AT[s]][0])

                loop(act, body)

            @block.vector
            def _(dve):
                for b in range(2):
                    nc.vector.memset(kst[b][0:HD, :].bitcast(F32), 0.0).then_inc(keep_in, 1)
                nc.vector.memset(qst[0:HD, :, :].bitcast(F32), 0.0).then_inc(keep_in, 1)
                dve.wait_ge(keep_in, 3)
                for c in range(NCH):
                    dve.wait_ge(const_in, 16 * (c + 1))
                    for b in range(2):
                        last = nc.vector.tensor_copy(kst[b][0:AUG, c * CH:(c + 1) * CH], p32[0][0:AUG, :])
                    last.then_inc(const_r, 1)
                nc.vector.memset(vst[0][:, :, 2 * HD:].bitcast(F32), 1.0).then_inc(const_r, 1)
                nc.vector.memset(vst[1][:, :, 2 * HD:].bitcast(F32), 1.0).then_inc(const_r, 1)
                nc.vector.tensor_scalar(keep[:], ident[0:NB, 1:2], -1.0, None, ALU.mult).then_inc(const_r, 1)
                nc.vector.tensor_copy(cur[0][:], tab[:, 0, :]).then_inc(cur_done, 1)
                for m in range(3):
                    for step in range(5):
                        decode_step(dve, m, step, 0, 0, 0)
                    for a in range(2):
                        weights_lo(dve, m, a, 0, 0)

                def body(i, par, pair):
                    nxt = (i + 1) % HEADS

                    def inner(n):
                        a = n % 2
                        dve.wait_ge(square_done, after(i * GU + n + 1))
                        nc.vector.scalar_tensor_tensor(gl[a][:], gl[a][:], 1.0, gate_ps[:], ALU.add, ALU.mult
                                                       ).then_inc(inner_done, 1)

                    def gelu(n):
                        a = n % 2
                        dve.wait_ge(tanh_done, i * GU + n + 1)
                        nc.vector.scalar_tensor_tensor(gl[a][:], gl[a][:], 1.0, gate_ps[:], ALU.add, ALU.mult
                                                       ).then_inc(gelu_done, 1)

                    def product(n):
                        a = n % 2
                        dve.wait_ge(up_done, i * GU + n + 1)
                        dve.wait_ge(gelu_done, after(i * GU + n + 1))
                        dve.wait_ge(il_done, after(since(i * GU, n, 2)))
                        nc.vector.scalar_tensor_tensor(prod[a][:], gl[a][:], 0.5 * IS / (XS * WS) ** 2, up_ps[:],
                                                       ALU.mult, ALU.mult).then_inc(prod_done, 1)

                    def product_hi(n):
                        w, a = n // 2, n % 2
                        dve.wait_ge(prod_done, after(i * GU + n + 1))
                        if a == 0:
                            dve.wait_ge(down_done, after(i * ND + max(TPC * (w - 1), 0)))
                        nc.vector.tensor_copy(ih[w % 2][:, a, :], prod[a][:]).then_inc(ih_done, 1)

                    def accumulate(n):
                        dve.wait_ge(down_done, after(i * ND + n + 1))
                        nc.vector.tensor_tensor(acc[:, n, :], down_ps[n % 2][:], acc[:, n, :], ALU.add
                                                ).then_inc(acc_done, 1)

                    def reduce(n):
                        c, t, m = MAXP[n]
                        cols = (t + 1) * P if m == c else CH
                        dve.wait_ge(max_done, i * NMAX + n + 1)
                        if t == 0 and m == 0:
                            dve.wait_ge(mxc_done, after(since(i * NCH, c, 2)))
                        nc.vector.tensor_reduce(mxp[c % 2][:, t, m:m + 1], pair_ps[n % 2][:, 0:cols], AX.X, ALU.max
                                                ).then_inc(red_done, 1)

                    def negate_max(c):
                        dve.wait_ge(red_done, after(i * NMAX + MAX_END[c]))
                        nc.vector.tensor_reduce(mxc[:], mxp[c % 2][:, :, 0:c + 1], AX.X, ALU.max).then_inc(mxc_done, 1)
                        dve.wait_ge(mxc_done, after(i * NCH + c + 1))
                        dve.wait_ge(maxt_done, after(i * NCH + c))
                        nc.vector.tensor_scalar(nmx[:], mxc[:].unsqueeze(2).broadcast_to([P, TPC, NB]), -1.0, None,
                                                ALU.mult).then_inc(nmx_done, 1)

                    def max_rows(c):
                        dve.wait_ge(bhi_done, i * NCH + c + 1)
                        nc.vector.scalar_tensor_tensor(qst[0:NB, c, :], bhi[:].bitcast(F32), keep[:, 0:1],
                                                       score_ps[0:NB, :], ALU.mult, ALU.add).then_inc(brow_done, 1)

                    def prob_hi(n):
                        cols = BLOCKS[n][2]
                        dve.wait_ge(exp_done, after(i * NBLK + n + 1))
                        dve.wait_ge(pv_done, after(since(i * NBLK, n, PP)))
                        nc.vector.tensor_copy(phi[n % PP][:, 0:cols], p32[n % PR][:, 0:cols]).then_inc(phi_done, 1)

                    dve.wait_ge(acc_done, after(i * ND))
                    for s in range(SLOTS + 2):
                        last = PIECES[s - 1] if 1 <= s <= SLOTS else ("", 0, 0, 0)
                        n = 2 * last[1] + last[2]
                        if last[0] == "down":
                            accumulate(last[1] * TPC + last[2])
                        if s < SLOTS and MAX_AT[s]:
                            reduce(MAX_AT[s][0])
                        if last[0] == "up" and last[3]:
                            product(n)
                        if last[0] == "gate" and last[3]:
                            inner(n)
                        if s < SLOTS and MAX_AT[s] and MAX_AT[s][0] + 1 in MAX_END:
                            negate_max(MAXP[MAX_AT[s][0]][0])
                        if s in SCORE_AT:
                            prob_hi(SCORE_AT[s])
                        if last[0] == "up" and last[3]:
                            product_hi(n)
                        if s - 1 in TURN_MAX_AT:
                            max_rows(TURN_MAX_AT[s - 1])
                        if s < SLOTS and len(MAX_AT[s]) > 1:
                            reduce(MAX_AT[s][1])
                            if MAX_AT[s][1] + 1 in MAX_END:
                                negate_max(MAXP[MAX_AT[s][1]][0])
                        gate = PIECES[s - 2] if 2 <= s else ("", 0, 0, 0)
                        if gate[0] == "gate" and gate[3]:
                            gelu(2 * gate[1] + gate[2])
                        if s == DECODE_FIRST:
                            dve.wait_ge(gelu_done, after(i * GU))
                            dve.wait_ge(square_done, after(i * GU))
                            dve.wait_ge(wl_done, (i + 1) * 6)
                            nc.vector.tensor_copy(cur[1 - par][:], tab[:, bass.ds(nxt, 1), :].rearrange("p o c -> p (o c)")
                                                  ).then_inc(cur_done, 1)
                        if s in DECODE_AT:
                            decode_step(dve, *DECODE_AT[s], nxt, i + 1, 0)
                        if s - 1 in TURN_W_AT:
                            weights_lo(dve, *TURN_W_AT[s - 1], i + 1, 1 - par)

                loop(dve, body)

            @block.gpsimd
            def _(pool):
                def body(i, par, pair):
                    def prob_lo(n):
                        cols = BLOCKS[n][2]
                        pool.wait_ge(phi_done, i * NBLK + n + 1)
                        pool.wait_ge(pv_done, after(since(i * NBLK, n, PP)))
                        nc.gpsimd.tensor_tensor(plo[n % PP][:, 0:cols], p32[n % PR][:, 0:cols],
                                                phi[n % PP][:, 0:cols].bitcast(F32), ALU.subtract).then_inc(plo_done, 1)

                    def product_lo(n):
                        w, a = n // 2, n % 2
                        pool.wait_ge(ih_done, i * GU + n + 1)
                        pool.wait_ge(down_done, after(i * ND + max(TPC * (w - 1), 0)))
                        nc.gpsimd.tensor_tensor(il[w % 2][:, a, :], prod[a][:], ih[w % 2][:, a, :], ALU.subtract
                                                ).then_inc(il_done, 1)

                    for s in range(SLOTS + 1):
                        if 1 <= s and PIECES[s - 1][0] == "up" and PIECES[s - 1][3]:
                            product_lo(2 * PIECES[s - 1][1] + PIECES[s - 1][2])
                        if s in SCORE_AT:
                            prob_lo(SCORE_AT[s])

                loop(pool, body)


DECODE_FIRST = min(DECODE_FROM)


def epilogue(nc, e):
    x_d, out_d, Wo, bo, o_s = (e[n] for n in ("x_d", "out_d", "Wo", "bo", "o_s"))
    acc, ident, oscale = (e[n] for n in ("acc", "ident", "oscale"))
    with ExitStack() as ctx:
        def sb(name, shape, dt):
            return ctx.enter_context(nc.sbuf_tensor(name, shape, dt))

        def sem(name):
            return ctx.enter_context(nc.semaphore(name))

        wo = sb("wo", [P, KVH, C], F32)
        bias = sb("bias", [P, C], F32)
        ones = sb("ones", [P, P], F32)
        diag = sb("diag", [P, KT, P], F32)
        orow = sb("orow", [P, C], F32)
        o3 = [sb(f"o3_{i}", [P, 3, KVH, CH], F32) for i in range(2)]
        xr = [sb(f"xr{i}", [P, TPC, C], F32) for i in range(2)]
        row_ps = ctx.enter_context(nc.psum_tensor("row_ps", [P, C], F32))
        y_ps = [ctx.enter_context(nc.psum_tensor(f"y_ps{i}", [P, C], F32)) for i in range(4)]
        wo_in = sem("wo_in")
        bias_in = sem("bias_in")
        o_in = [sem(f"o_in{i}") for i in range(2)]
        x_in2 = [sem(f"x_in2{i}") for i in range(2)]
        step = sem("step")
        diag_done = sem("diag_done")
        row_done = sem("row_done")
        o_done = sem("o_done")
        y_done = sem("y_done")
        sum_done = sem("sum_done")
        y_read = sem("y_read")
        out_done = [sem(f"out_done{i}") for i in range(2)]

        with nc.Block() as block:
            @block.sync
            def _(sp):
                for g in range(KVH):
                    for r in range(REP):
                        h = r * KVH + g
                        sp.dma_start(wo[r * HD:(r + 1) * HD, g, :], Wo[h * HD:(h + 1) * HD, :]).then_inc(wo_in, 16)
                sp.dma_start(bias[:], bo.rearrange("(o n) -> o n", o=1).broadcast_to([P, C])).then_inc(bias_in, 16)
                for c in range(NCH):
                    b = c % 2
                    if c >= 2:
                        sp.wait_ge(y_done, TPC * (c - 1))
                        sp.wait_ge(out_done[b], 16 * (c // 2))
                    for part in range(3):
                        sp.dma_start(o3[b][:, part], o_s[part, :, c * CH:(c + 1) * CH].rearrange("(g p) t -> p g t", p=P)
                                     ).then_inc(o_in[b], 16)
                    sp.dma_start(xr[b][:], x_d[c * CH:(c + 1) * CH, :].rearrange("(j p) h -> p j h", p=P)
                                 ).then_inc(x_in2[b], 16)

            @block.scalar
            def _(act):
                for c in range(NCH):
                    act.wait_ge(sum_done, TPC * (c + 1))
                    act.dma_start(out_d[c * CH:(c + 1) * CH, :].rearrange("(j p) h -> p j h", p=P), xr[c % 2][:]
                                  ).then_inc(out_done[c % 2], 16)
                for b in range(2):
                    act.wait_ge(out_done[b], 16 * NCH // 2)

            @block.tensor
            def _(pe):
                pe.wait_ge(diag_done, KT + 1)
                for k in range(KT):
                    mm = nc.tensor.matmul(row_ps[:, k * P:(k + 1) * P], ones[:], diag[:, k, :], start=True, stop=True)
                mm.then_inc(row_done, 1)
                pe.wait_ge(wo_in, 16 * HEADS)
                for c in range(NCH):
                    pe.wait_ge(o_done, c + 1)
                    for t in range(TPC):
                        n = TPC * c + t
                        if n >= 4:
                            pe.wait_ge(y_read, n - 3)
                        for g in range(KVH):
                            mm = nc.tensor.matmul(y_ps[n % 4][:], o3[c % 2][:, 0, g, t * P:(t + 1) * P], wo[:, g, :],
                                                  start=(g == 0), stop=(g == KVH - 1))
                        mm.then_inc(y_done, 1)

            @block.vector
            def _(dve):
                steps = [0]

                def link(ins):
                    steps[0] += 1
                    ins.then_inc(step, 1)
                    dve.wait_ge(step, steps[0])

                nc.vector.memset(ones[:], 1.0).then_inc(diag_done, 1)
                for k in range(KT):
                    nc.vector.tensor_scalar(diag[:, k, :], ident[:], oscale[:, k:k + 1], None, ALU.mult
                                            ).then_inc(diag_done, 1)
                dve.wait_ge(row_done, 1)
                link(nc.vector.tensor_copy(orow[:], row_ps[:]))
                dve.wait_ge(bias_in, 16)

                def heads(c):
                    b = c % 2
                    dve.wait_ge(o_in[b], 48 * (c // 2 + 1))
                    flat = [o3[b][:, part].rearrange("p g t -> p (g t)") for part in range(3)]
                    link(nc.vector.tensor_tensor(flat[0], flat[0], flat[1], ALU.add))
                    link(nc.vector.reciprocal(flat[2], flat[2]))
                    nc.vector.tensor_tensor(flat[0], flat[0], flat[2], ALU.mult).then_inc(o_done, 1)

                heads(0)
                for c in range(NCH):
                    b = c % 2
                    if c + 1 < NCH:
                        heads(c + 1)
                    dve.wait_ge(x_in2[b], 16 * (c // 2 + 1))
                    for t in range(TPC):
                        n = TPC * c + t
                        link(nc.vector.tensor_tensor(acc[:, n, :], acc[:, n, :], orow[:], ALU.mult))
                        link(nc.vector.tensor_tensor(xr[b][:, t, :], xr[b][:, t, :], bias[:], ALU.add))
                        link(nc.vector.tensor_tensor(acc[:, n, :], acc[:, n, :], xr[b][:, t, :], ALU.add))
                        dve.wait_ge(y_done, n + 1)
                        ins = nc.vector.tensor_tensor(xr[b][:, t, :], y_ps[n % 4][:], acc[:, n, :], ALU.add)
                        ins.then_inc(y_read, 1)
                        dve.wait_ge(y_read, n + 1)
                        nc.vector.tensor_copy(acc[:, n, 0:1], acc[:, n, 1:2]).then_inc(sum_done, 1)


def _round12(v):
    m, ex = np.frexp(np.asarray(v, np.float64))
    return np.ldexp(np.rint(m * 4096) / 4096, ex)


def _alibi_rows():
    start = 2.0 ** (-2.0 ** (-(np.log2(HEADS) - 3.0)))
    pos = np.arange(T, dtype=np.float64)
    rows = np.zeros((HEADS, AUG, T))
    for i in range(HEADS):
        h = (i % REP) * KVH + i // REP
        slope = float(np.float32(start ** (h + 1)))
        hi = float(_round12(slope))
        lo = slope - hi
        a, c = -hi * pos, -lo * pos
        rows[i, 2], rows[i, 3] = hi, lo
        rows[i, 4] = _round12(a)
        rows[i, 5] = a - rows[i, 4]
        rows[i, 6] = _round12(c)
        rows[i, 7] = c - rows[i, 6]
    keys = np.ones((AUG, T))
    keys[2] = keys[3] = pos
    return rows.reshape(HEADS * AUG, T).astype(np.float32), keys.astype(np.float32)


_INS = ["L0_attn_x", "L0_attn_Wq", "L0_attn_Wkv", "L0_attn_Wo", "L0_attn_bo", "L0_ffn_gate_W_packed",
        "L0_ffn_gate_scales", "L0_ffn_up_W_packed", "L0_ffn_up_scales", "L0_ffn_down_W_packed", "L0_ffn_down_scales"]


def kernel(**inputs):
    import concourse.bacc as _bacc
    from concourse.bass_utils import run_bass_kernel_spmd as _run

    nc = _bacc.Bacc("TRN2", target_bir_lowering=False, num_devices=1)
    arrays, ap = {}, {}
    augq, augk = _alibi_rows()
    given = {name: np.ascontiguousarray(inputs[name]) for name in _INS}
    given["augq"], given["augk"] = augq, augk
    for name, a in given.items():
        arrays[f"in_{name}_dram"] = a
        ap[name] = nc.dram_tensor(f"in_{name}_dram", a.shape, mybir.dt.from_np(a.dtype), kind="ExternalInput").ap()
    out = nc.dram_tensor("out_0_dram", (1, T, C), F32, kind="ExternalOutput").ap()
    build(nc, ap["L0_attn_x"], ap["L0_attn_Wq"], ap["L0_attn_Wkv"], ap["L0_attn_Wo"], ap["L0_attn_bo"],
          [ap[f"L0_ffn_{m}_W_packed"] for m in ("gate", "up", "down")],
          [ap[f"L0_ffn_{m}_scales"] for m in ("gate", "up", "down")], ap["augq"], ap["augk"], out)
    r = _run(nc, [arrays], core_ids=[0])
    return r.results[0]["out_0_dram"]
```

```python
from contextlib import ExitStack

import numpy as np

import concourse.bass as bass
from concourse import mybir

F32 = mybir.dt.float32
F32R = mybir.dt.float32r
F16 = mybir.dt.float16
BF16 = mybir.dt.bfloat16
I32 = mybir.dt.int32
ALU = mybir.AluOpType
ACT = mybir.ActivationFunctionType
AX = mybir.AxisListType
RMAX = bass.bass_isa.ReduceOp.max

P = 128
T, C = 2048, 512
HEADS, KVH, HD = 16, 4, 32
REP = HEADS // KVH
MLP = 4096
BLOCK = 32
EPS = 1e-5
KT = C // P
CH = 512
NCH = T // CH
TPC = CH // P
NT = T // P
GROUP = 2 * P
NG = MLP // GROUP
WORDS = GROUP * C // 2 // P
SB = WORDS * 2 // BLOCK
assert NG == HEADS

K_FIRST = 3 * 16 * NCH
AUG = 8
NB = 2

XS = 2.0 ** 4
WS = 2.0 ** 8
NIB = 2.0 ** 14
IS = 2.0 ** -10
LIM = 2.0 ** 60
GELU_C = 0.7978845608028654
GELU_A = 0.044715

SLOTS = 48
PV_LAG = 3


def score_blocks():
    out = []
    for c in range(NCH):
        d = TPC * c
        out += [(c, [(j, 0, 0)], CH) for j in range(d + 1)]
        out.append((c, [(d + 1, 0, P), (d + 3, 3 * P, 3 * P)], CH))
        out.append((c, [(d + 2, 0, 2 * P)], 2 * P))
    return out


BLOCKS = score_blocks()
NBLK = len(BLOCKS)
BLK_END = [sum(b[0] <= c for b in BLOCKS) for c in range(NCH)]
MAXP = [(c, i, m) for c in range(NCH) for i in range(TPC) for m in range(c + 1)]
NMAX = len(MAXP)
MAX_END = [sum(m[0] <= c for m in MAXP) for c in range(NCH)]
MAX_PER_SLOT = [2, 2, 2, 2, 1, 2, 1] + [2, 1] * 4 + [2, 1] * 4 + [2, 1, 1]
MAX_AT = [list(range(sum(MAX_PER_SLOT[:s]), sum(MAX_PER_SLOT[:s + 1]))) for s in range(SLOTS)]
assert sum(MAX_PER_SLOT) == NMAX
TURN_MAX_AT = {3: 0, 7: 1, 15: 2, 26: 3}
SCORE_SLOTS = [s for s in range(6, SLOTS) if s - 1 not in TURN_MAX_AT][:NBLK]
SCORE_AT = {s: n for n, s in enumerate(SCORE_SLOTS)}
BLOCKS_BY_TURN = [sum(s <= turn for s in SCORE_SLOTS) for turn in TURN_MAX_AT]
VALUES_AT = {s + PV_LAG: n for s, n in SCORE_AT.items()}
assert max(VALUES_AT) < SLOTS
DECODE_FROM = {26: 0, 31: 1, 36: 2}
DECODE_AT = {s + i: (m, i) for s, m in DECODE_FROM.items() for i in range(5)}
DECODE_FIRST = min(DECODE_FROM)
TURN_W_AT = {31: (0, 0), 32: (0, 1), 36: (1, 0), 37: (1, 1), 41: (2, 0), 42: (2, 1)}

RECIP_AT = {20: 0, 21: 1, 22: 2, 23: 3}
ADD_PARTS_AT, NORMALISE_AT = 22, 25


NORM_STEP = 1
SCALES_AT = {(0, 3): 0, (0, 4): 1, (1, 3): 2}
TABLES_AT = (1, 4)
DECODE_FIRST_AT = {(2, 0): 0, (2, 2): 1, (2, 4): 2}
TURN_FIRST_AT = {(2, 1): 0, (2, 3): 1, (3, 0): 2}


def ffn_pieces():
    out = []
    for w in range(NCH):
        for a in range(2):
            out += [("gate", w, a, 0), ("gate", w, a, 1), ("up", w, a, 0), ("up", w, a, 1)]
            if w:
                out += [("down", w - 1, 2 * a, 0), ("down", w - 1, 2 * a + 1, 0)]
    return out + [("down", NCH - 1, t, 0) for t in range(TPC)]


PIECES = ffn_pieces()
assert len(PIECES) == SLOTS


def build(nc, x, Wq, Wkv, Wo, bo, packed, scales, augq, augk, out):
    x_d = x.rearrange("b t c -> (b t) c")
    out_d = out.rearrange("b t c -> (b t) c")

    q_s = nc.dram_tensor("q_parts", [2, HEADS * HD, T], F32, kind="Internal").ap()
    k_s = nc.dram_tensor("k_parts", [2, KVH * HD, T], F32, kind="Internal").ap()
    v_s = nc.dram_tensor("v_parts", [KVH, P, NT, 2 * HD], F32, kind="Internal").ap()
    aug_s = nc.dram_tensor("aug_rows", [HEADS * AUG, T], F32, kind="Internal").ap()
    o_s = nc.dram_tensor("o_heads", [HEADS + 1, HD, T], F32, kind="Internal").ap()

    with ExitStack() as ctx:
        def sb(name, shape, dt, c=ctx):
            return c.enter_context(nc.sbuf_tensor(name, shape, dt))

        def sem(name):
            return ctx.enter_context(nc.semaphore(name))

        xh = sb("xh", [P, KT, T], F16)
        xl = sb("xl", [P, KT, T], F16)
        acc = sb("acc", [P, NT, C], F32)
        ident = sb("ident", [P, P], F32)
        identb = sb("identb", [P, P], BF16)
        identr = sb("identr", [P, P], F32R)
        mask_ts = sb("mask_ts", [P, P], BF16)
        mask_st = sb("mask_st", [P, P], BF16)
        sc = [sb(f"sc{m}", [P, NG, SB], F32) for m in range(3)]
        tab = sb("tab", [P, NG, 6], F32)
        on = sb("on", [P, CH], F32)
        oscale = sb("oscale", [P, KT], F32)

        wo, *oc = [t[:].rearrange("p k t -> p (k t)").bitcast(F32).rearrange("p (h g n) -> p h g n", h=2, n=CH)[:, h]
                   for t in (xh, xl) for h in range(2)]
        wo_in = sem("wo_in")
        o_in = [sem(f"o_in{c}") for c in range(NCH)]

        with ExitStack() as work:
            def tile(name, shape, dt):
                return sb(name, shape, dt, work)

            raw = [tile(f"raw{m}", [P, WORDS], I32) for m in range(3)]
            dec = tile("dec", [P, 2, WORDS], I32)
            wf = tile("wf", [P, 2 * WORDS], F32)
            wh = [tile(f"wh{b}", [P, 3, 2, C], F16) for b in range(2)]
            wl = [tile(f"wl{b}", [P, 3, 2, C], F16) for b in range(2)]
            cur = [tile(f"cur{b}", [P, 6], F32) for b in range(2)]
            qst = tile("qst", [P, NCH, CH], F32R)
            kst = [tile(f"kst{b}", [P, T], F32R) for b in range(2)]
            vst = [tile(f"vst{b}", [P, NT, 3 * HD], F32R) for b in range(2)]
            o3 = [tile(f"o3_{b}", [P, 3, CH], F32) for b in range(2)]

            raw_in = [sem(f"raw_in{m}") for m in range(3)]
            k_in = [sem(f"k_in{b}") for b in range(2)]
            v_in = [sem(f"v_in{b}") for b in range(2)]
            q_in = [sem(f"q_in{c}") for c in range(NCH)]
            p_out = [sem(f"p_out{j}") for j in range(1 + KVH)]
            v_out = sem("v_out")
            dec_step = sem("dec_step")
            cur_done = sem("cur_done")
            wf_done = sem("wf_done")
            wturn_done = sem("wturn_done")
            wh_done = sem("wh_done")
            wl_done = sem("wl_done")

            preamble(nc, locals())
            main_loop(nc, locals())

        epilogue(nc, locals())


def load_heads(sp, oc, o_s, o_in, c):
    for g in range(KVH):
        heads = REP if g < KVH - 1 else REP - 1
        sp.dma_start(oc[c][0:heads * HD, g, :],
                     o_s[1 + g * REP:1 + g * REP + heads, :, c * CH:(c + 1) * CH].rearrange("r d t -> (r d) t")
                     ).then_inc(o_in[c], 16)


def weight_steps(nc, e, banks):
    packed, ident, sc = e["packed"], e["ident"], e["sc"]
    raw, dec, wf, wh, wl, cur = (e[n] for n in ("raw", "dec", "wf", "wh", "wl", "cur"))
    raw_in, dec_step, cur_done, wf_done, wturn_done, wh_done, wl_done = (
        e[n] for n in ("raw_in", "dec_step", "cur_done", "wf_done", "wturn_done", "wh_done", "wl_done"))

    def load_raw(sp, m, g):
        if m < 2:
            src = packed[m].rearrange("(g a p) w -> g p a w", a=2, p=P)[bass.ds(g, 1)]
            dst = raw[m][:].rearrange("p (a w) -> p a w", a=2)
        else:
            src = packed[2].rearrange("(k p) (g w) -> g p k w", p=P, w=GROUP // 2)[bass.ds(g, 1)]
            dst = raw[m][:].rearrange("p (k w) -> p k w", k=KT)
        sp.dma_start(dst, src.rearrange("o p a w -> (o p) a w")).then_inc(raw_in[m], 16)

    def decode_step(dve, m, step, g, before):
        if step == 0:
            dve.wait_ge(raw_in[m], (before + 1) * 16)
            if m or not isinstance(before, int):
                dve.wait_ge(wf_done, before * 6 + 2 * m)
            nc.vector.tensor_scalar(dec[:, 0], raw[m][:], 28, 19, ALU.logical_shift_left,
                                    ALU.arith_shift_right).then_inc(dec_step, 1)
        if step == 1:
            nc.vector.tensor_scalar(dec[:, 1], raw[m][:], 24, 19, ALU.logical_shift_left,
                                    ALU.arith_shift_right).then_inc(dec_step, 1)
        if step == 2:
            dve.wait_ge(dec_step, before * 9 + m * 3 + 2)
            nc.vector.tensor_scalar(dec[:].rearrange("p a w -> p (a w)"), dec[:].rearrange("p a w -> p (a w)"),
                                    0x8E00, None, ALU.bitwise_and).then_inc(dec_step, 1)
        if step >= 3:
            b = step - 3
            if b == 0:
                dve.wait_ge(dec_step, before * 9 + m * 3 + 3)
                dve.wait_ge(wturn_done, before * 6 + 2 * m)
            codes = dec[:, b].bitcast(F16).rearrange("p (s j two) -> p s j two", j=BLOCK // 2, two=2)[:, :, :, 0]
            nc.vector.tensor_tensor(
                wf[:].rearrange("p (s j two) -> p s j two", j=BLOCK // 2, two=2)[:, :, :, b], codes,
                sc[m][:, bass.ds(g, 1), :].rearrange("p o s -> p (o s)").unsqueeze(2).broadcast_to([P, SB, BLOCK // 2]),
                ALU.mult).then_inc(wf_done, 1)

    def turn_weights(pe, m, a, before, maxima):
        pe.wait_ge(wf_done, before * 6 + 2 * m + 2)
        if maxima is not None or 2 * m + a >= 2:
            pe.wait_ge(wl_done, before * 6 + 2 * m + a - 1)
        if maxima is not None:
            pe.wait_ge(*maxima)
        for k in range(KT):
            at = a * C + k * P if m < 2 else k * GROUP + a * P
            mm = nc.tensor.transpose(banks[a][:, k * P:(k + 1) * P], wf[:, at:at + P], ident[:])
        mm.then_inc(wturn_done, 1)

    def weights_hi(act, m, a, before, b):
        act.wait_ge(wturn_done, before * 6 + 2 * m + a + 1)
        if m == 2:
            act.wait_ge(cur_done, before + 1)
        nc.scalar.activation(wh[b][:, m, a, :], banks[a][:], ACT.Copy,
                             scale=1.0 if m < 2 else cur[b][:, 4 + a:5 + a]).then_inc(wh_done, 1)

    def weights_lo(dve, m, a, before, b):
        dve.wait_ge(wh_done, before * 6 + 2 * m + a + 1)
        nc.vector.scalar_tensor_tensor(wl[b][:, m, a, :], banks[a][:], 1.0 if m < 2 else cur[b][:, 4 + a:5 + a],
                                       wh[b][:, m, a, :], ALU.mult, ALU.subtract).then_inc(wl_done, 1)

    return load_raw, decode_step, turn_weights, weights_hi, weights_lo


def preamble(nc, e):
    (x_d, Wq, Wkv, scales, augq, augk, q_s, k_s, v_s, aug_s) = (
        e[n] for n in ("x_d", "Wq", "Wkv", "scales", "augq", "augk", "q_s", "k_s", "v_s", "aug_s"))
    xh, xl, acc, ident, identb, identr, mask_ts, mask_st, sc, tab, oscale = (
        e[n] for n in ("xh", "xl", "acc", "ident", "identb", "identr", "mask_ts", "mask_st", "sc", "tab", "oscale"))
    dec, wf, wh, wl, cur, qst, kst, vst, o3 = (
        e[n] for n in ("dec", "wf", "wh", "wl", "cur", "qst", "kst", "vst", "o3"))
    k_in, q_in, p_out, v_out, cur_done = (e[n] for n in ("k_in", "q_in", "p_out", "v_out", "cur_done"))
    with ExitStack() as ctx:
        def sb(name, shape, dt):
            return ctx.enter_context(nc.sbuf_tensor(name, shape, dt))

        def sem(name):
            return ctx.enter_context(nc.semaphore(name))

        xin = [acc[:, i * TPC:(i + 1) * TPC, :] for i in range(2)]
        wqn = acc[:, 2 * TPC:2 * TPC + KT, :]
        sraw = [acc[:, 2 * TPC + KT + m, :] for m in range(3)]
        augs = acc[:, 2 * TPC:2 * TPC + KT, :].rearrange("p k n -> p (k n)")
        augk_in = [t.rearrange("p (c n) -> p c n", n=CH) for t in (dec[:].rearrange("p a w -> p (a w)").bitcast(F32), wf[:])]
        xt = [sb(f"xt{i}", [P, KT, CH], F32) for i in range(2)]
        wq = sb("wq", [P, KT, C], F32)
        wkv = sb("wkv", [P, KT, 2 * KVH * HD], F32)
        ph = [o3[0][:, i, :].bitcast(F32R) for i in range(2)]
        pl = [o3[0][:, 2, :].bitcast(F32R), wl[1][:, 0].rearrange("p a n -> p (a n)").bitcast(F32R)]
        vt = wh[1][:, 0:2].rearrange("p m a n -> p (m a n)").bitcast(F32R).rearrange(
            "p (j g a d) -> p j g a d", j=TPC, g=KVH, a=2)
        stats = sb("stats", [P, TPC, 6], F32)
        mv = sb("mv", [P, TPC, 2], F32)
        ve = sb("ve", [P, TPC], F32)
        sd = sb("sd", [P, TPC], F32)
        rs = sb("rs", [P, TPC], F32)
        nt_ = sb("nt_", [P, TPC], F32)
        big = [sb(f"big{m}", [P, 2 * NG if m < 2 else KT], F32) for m in range(3)]
        low = [sb(f"low{m}", [P, 2 * NG if m < 2 else KT], F32) for m in range(3)]
        inv = [sb(f"inv{m}", [P, 2 * NG if m < 2 else KT], F32) for m in range(3)]
        rr = sb("rr", [P, 2 * NG], F32)
        rmax = sb("rmax", [P, 1], F32)
        rall = sb("rall", [P, 1], F32)
        rinv = sb("rinv", [P, 1], F32)
        turn = [ctx.enter_context(nc.psum_tensor(f"turn{i}", [P, CH], F32)) for i in range(2)]
        proj = [ctx.enter_context(nc.psum_tensor(f"proj{i}", [P, CH], F32)) for i in range(2)]
        w_ps = [ctx.enter_context(nc.psum_tensor(f"w_ps{i}", [P, CH], F32)) for i in range(2)]
        vps = ctx.enter_context(nc.psum_tensor("vps", [P, CH], F32))

        x_in = [sem(f"x_in{i}") for i in range(2)]
        w_in = sem("w_in")
        wq_done = sem("wq_done")
        sc_in = sem("sc_in")
        augk_loaded = sem("augk_loaded")
        augk_done = sem("augk_done")
        augq_in = sem("augq_in")
        augq_done = sem("augq_done")
        aug_out = sem("aug_out")
        ident_done = sem("ident_done")
        pool_step = sem("pool_step")
        dve_step = sem("dve_step")
        var_done = sem("var_done")
        sqrt_done = sem("sqrt_done")
        xn_done = sem("xn_done")
        turned = sem("turned")
        xt_done = sem("xt_done")
        xh_done = sem("xh_done")
        xl_done = sem("xl_done")
        projected = sem("projected")
        part_hi = sem("part_hi")
        part_lo = sem("part_lo")
        v_sum = sem("v_sum")
        v_hi = sem("v_hi")
        v_lo = sem("v_lo")
        cleared = sem("cleared")
        rmax_done = sem("rmax_done")
        rall_done = sem("rall_done")
        NPROJ = 1 + KVH
        CLEARED = 7
        load_raw, decode_step, turn_weights, weights_hi, weights_lo = weight_steps(nc, e, w_ps)
        QSCALE = float(np.float32(1 / np.sqrt(np.float32(HD))))

        def wait_stored(eng, n):
            eng.wait_ge(p_out[n % NPROJ], 32 * (n // NPROJ + 1))

        with nc.Block() as block:
            @block.sync
            def _(sp):
                def load_x(c):
                    if c >= 2:
                        sp.wait_ge(turned, KT * (c - 1))
                    sp.dma_start(xin[c % 2], x_d[c * CH:(c + 1) * CH, :].rearrange("(j p) h -> p j h", p=P)
                                 ).then_inc(x_in[c % 2], 16)

                def first_head(c):
                    cols = slice(c * CH, (c + 1) * CH)
                    wait_stored(sp, NPROJ * c)
                    for part, at in ((0, HD), (0, 2 * HD), (1, 3 * HD)):
                        sp.dma_start(kst[0][at:at + HD, cols].bitcast(F32), k_s[part, 0:HD, cols]).then_inc(k_in[0], 16)
                    wait_stored(sp, NPROJ * c + 1)
                    sp.dma_start(qst[0:AUG, c, :].bitcast(F32), aug_s[0:AUG, cols]).then_inc(q_in[c], 16)
                    for part, at in ((0, HD), (1, 2 * HD), (0, 3 * HD)):
                        sp.dma_start(qst[at:at + HD, c, :].bitcast(F32), q_s[part, 0:HD, cols]).then_inc(q_in[c], 16)

                load_x(0)
                for h in range(2):
                    sp.dma_start(augk_in[h][0:AUG], augk[:, h * 2 * CH:(h + 1) * 2 * CH].rearrange("p (c n) -> p c n", n=CH)
                                 ).then_inc(augk_loaded, 16)
                sp.dma_start(wkv[:], Wkv.rearrange("(k p) n -> p k n", p=P)).then_inc(w_in, 16)
                sp.dma_start(wqn, Wq.rearrange("(k p) n -> p k n", p=P)).then_inc(w_in, 16)
                load_x(1)
                for m in range(2):
                    sp.dma_start(sraw[m].rearrange("p (t b) -> p t b", b=C // BLOCK),
                                 scales[m].rearrange("(t p) b -> p t b", p=P)).then_inc(sc_in, 16)
                sp.dma_start(sraw[2].rearrange("p (k b) -> p k b", k=KT),
                             scales[2].rearrange("(k p) b -> p k b", p=P)).then_inc(sc_in, 16)
                for m in range(3):
                    load_raw(sp, m, 0)
                sp.wait_ge(wq_done, KT)
                sp.dma_start(augs, augq).then_inc(augq_in, 16)
                for c in range(NCH):
                    cols = slice(c * CH, (c + 1) * CH)
                    if c + 2 < NCH:
                        load_x(c + 2)
                    for j in range(NPROJ):
                        n = NPROJ * c + j
                        dst = k_s if j == 0 else q_s
                        rows = slice(0, P) if j == 0 else slice((j - 1) * P, j * P)
                        sp.wait_ge(part_lo, n + 1)
                        sp.dma_start(dst[0, rows, cols], ph[n % 2].bitcast(F32)).then_inc(p_out[j], 16)
                        sp.dma_start(dst[1, rows, cols], pl[n % 2].bitcast(F32)).then_inc(p_out[j], 16)
                        if (c, j) == (0, 0):
                            sp.wait_ge(augq_done, NCH)
                            sp.dma_start(aug_s, augs).then_inc(aug_out, 16)
                        if j == NPROJ - 2:
                            if c == 0:
                                sp.wait_ge(aug_out, 16)
                                sp.wait_ge(cleared, CLEARED)
                            first_head(c)
                    sp.wait_ge(v_lo, c + 1)
                    for g in range(KVH):
                        sp.dma_start(v_s[g, :, TPC * c:TPC * (c + 1), :],
                                     vt[:, :, g, :, :].rearrange("p j a d -> p j (a d)").bitcast(F32)).then_inc(v_out, 16)

            @block.gpsimd
            def _(pool):
                nc.gpsimd.memset(ident[:], 0.0).then_inc(pool_step, 1)
                nc.gpsimd.memset(mask_ts[:], 0.0).then_inc(pool_step, 1)
                nc.gpsimd.memset(mask_st[:], 0.0).then_inc(pool_step, 1)
                pool.wait_ge(pool_step, 3)
                nc.gpsimd.affine_select(out=ident[:], in_=ident[:], compare_op=ALU.not_equal, fill=1.0, base=0,
                                        pattern=[[-1, P]], channel_multiplier=1).then_inc(pool_step, 1)
                nc.gpsimd.affine_select(out=mask_ts[:], in_=mask_ts[:], compare_op=ALU.is_ge, fill=-1e30, base=0,
                                        pattern=[[-1, P]], channel_multiplier=1).then_inc(pool_step, 1)
                nc.gpsimd.affine_select(out=mask_st[:], in_=mask_st[:], compare_op=ALU.is_ge, fill=-1e30, base=0,
                                        pattern=[[1, P]], channel_multiplier=-1).then_inc(pool_step, 1)
                pool.wait_ge(pool_step, 6)
                nc.gpsimd.tensor_copy(identb[:], ident[:]).then_inc(ident_done, 1)
                for b in range(2):
                    nc.gpsimd.memset(kst[b][0:HD, :].bitcast(F32), 0.0).then_inc(cleared, 1)
                nc.gpsimd.memset(qst[0:HD, :, :].bitcast(F32), 0.0).then_inc(cleared, 1)
                for b in range(2):
                    nc.gpsimd.memset(vst[b][:, :, 2 * HD:].bitcast(F32), 1.0).then_inc(cleared, 1)
                nc.gpsimd.memset(o3[1][:], 1.0).then_inc(cleared, 1)
                nc.gpsimd.tensor_scalar(identr[:], ident[:], 1.0, 1.0, ALU.mult, ALU.mult).then_inc(cleared, 1)
                pool.wait_ge(augk_loaded, 32)
                pool.wait_ge(cleared, CLEARED)
                for b in range(2):
                    for c in range(NCH):
                        nc.gpsimd.tensor_scalar(kst[b][0:AUG, c * CH:(c + 1) * CH], augk_in[c // 2][0:AUG, c % 2], 1.0,
                                                1.0, ALU.mult, ALU.mult).then_inc(augk_done, 1)
                pool.wait_ge(augq_in, 16)
                for c in range(NCH):
                    part = augs[:, c * CH:(c + 1) * CH]
                    nc.gpsimd.tensor_scalar(part.bitcast(F32R), part, 1.0, 1.0, ALU.mult, ALU.mult
                                            ).then_inc(augq_done, 1)
                pool.wait_ge(rmax_done, 1)
                nc.gpsimd.partition_all_reduce(rall[:], rmax[:], P, RMAX).then_inc(rall_done, 1)

            @block.tensor
            def _(pe):
                def turn_x(c, k):
                    n = KT * c + k
                    if k == 0:
                        pe.wait_ge(xn_done, c + 1)
                    if n >= 2:
                        pe.wait_ge(xl_done, n - 1)
                        pe.wait_ge(xt_done, n - 1)
                    for j in range(TPC):
                        mm = nc.tensor.transpose(turn[n % 2][:, j * P:(j + 1) * P],
                                                 xin[c % 2][:, j, k * P:(k + 1) * P], ident[:])
                    mm.then_inc(turned, 1)

                def project(c, j):
                    n = NPROJ * c + j
                    if n >= 2:
                        pe.wait_ge(part_lo, n - 1)
                    for k in range(KT):
                        lhs = wkv[:, k, 0:KVH * HD] if j == 0 else wq[:, k, (j - 1) * P:j * P]
                        mm = nc.tensor.matmul(proj[n % 2][:], lhs, xt[c % 2][:, k, :],
                                              start=(k == 0), stop=(k == KT - 1))
                    mm.then_inc(projected, 1)

                pe.wait_ge(ident_done, 1)
                for k in range(KT):
                    turn_x(0, k)
                for c in range(NCH):
                    pe.wait_ge(xt_done, KT * (c + 1))
                    if c == 0:
                        pe.wait_ge(w_in, 32)
                    for j in range(NPROJ):
                        if c == 0 and j == 1:
                            pe.wait_ge(wq_done, KT)
                        project(c, j)
                        if c + 1 < NCH and j >= 1:
                            turn_x(c + 1, j - 1)
                        if (c, j) in TURN_FIRST_AT:
                            for a in range(2):
                                turn_weights(pe, TURN_FIRST_AT[c, j], a, 0, None)
                    if c >= 1:
                        pe.wait_ge(v_lo, c)
                    for j in range(TPC):
                        for k in range(KT):
                            mm = nc.tensor.matmul(vps[:, j * P:(j + 1) * P], xt[c % 2][:, k, j * P:(j + 1) * P],
                                                  wkv[:, k, KVH * HD:], start=(k == 0), stop=(k == KT - 1))
                    mm.then_inc(v_sum, 1)

            @block.scalar
            def _(act):
                def root(c):
                    act.wait_ge(var_done, c + 1)
                    nc.scalar.activation(sd[:], ve[:], ACT.Sqrt).then_inc(sqrt_done, 1)

                def turned_hi(c, k):
                    n = KT * c + k
                    if k == 0 and c >= 2:
                        act.wait_ge(v_sum, c - 1)
                    act.wait_ge(turned, n + 1)
                    nc.scalar.activation(xt[c % 2][:, k, :], turn[n % 2][:], ACT.Copy).then_inc(xt_done, 1)
                    nc.scalar.activation(xh[:, k, c * CH:(c + 1) * CH], turn[n % 2][:], ACT.Copy, scale=XS
                                         ).then_inc(xh_done, 1)

                root(0)
                for k in range(KT):
                    turned_hi(0, k)
                root(1)
                for c in range(NCH):
                    for j in range(NPROJ):
                        n = NPROJ * c + j
                        act.wait_ge(projected, n + 1)
                        if n >= 2:
                            wait_stored(act, n - 2)
                        nc.scalar.activation(ph[n % 2], proj[n % 2][:], ACT.Copy, scale=QSCALE if j else 1.0
                                             ).then_inc(part_hi, 1)
                        if c + 1 < NCH and j >= 1:
                            turned_hi(c + 1, j - 1)
                        if c + 2 < NCH and j == NORM_STEP:
                            root(c + 2)
                        if (c, j) in TURN_FIRST_AT:
                            for a in range(2):
                                weights_hi(act, TURN_FIRST_AT[c, j], a, 0, 0)
                    act.wait_ge(v_sum, c + 1)
                    if c >= 1:
                        act.wait_ge(v_out, 16 * KVH * c)
                    nc.scalar.activation(vt[:, :, :, 0, :], vps[:].rearrange("p (j g d) -> p j g d", j=TPC, g=KVH),
                                         ACT.Copy).then_inc(v_hi, 1)

            @block.vector
            def _(dve):
                steps = [0]

                def link(ins):
                    steps[0] += 1
                    ins.then_inc(dve_step, 1)
                    dve.wait_ge(dve_step, steps[0])

                def layer_norm(c):
                    xc = xin[c % 2]
                    dve.wait_ge(x_in[c % 2], 16 * (c // 2 + 1))
                    for j in range(TPC):
                        last = nc.vector.bn_stats(stats[:, j, :], xc[:, j, :])
                    link(last)
                    for j in range(TPC):
                        last = nc.vector.bn_aggr(mv[:, j, :], stats[:, j, :])
                    link(last)
                    if c:
                        dve.wait_ge(sqrt_done, c)
                    link(nc.vector.tensor_scalar(ve[:], mv[:, :, 1], EPS, None, ALU.add))
                    nc.vector.tensor_copy(nt_[:], ve[:]).then_inc(var_done, 1)
                    dve.wait_ge(sqrt_done, c + 1)
                    link(nc.vector.reciprocal(rs[:], sd[:]))
                    link(nc.vector.tensor_tensor(nt_[:], rs[:], rs[:], ALU.mult))
                    link(nc.vector.tensor_tensor(nt_[:], nt_[:], ve[:], ALU.mult))
                    link(nc.vector.tensor_scalar(nt_[:], nt_[:], -0.5, 1.5, ALU.mult, ALU.add))
                    link(nc.vector.tensor_tensor(rs[:], rs[:], nt_[:], ALU.mult))
                    for j in range(TPC):
                        last = nc.vector.tensor_scalar(xc[:, j, :], xc[:, j, :], mv[:, j, 0:1], rs[:, j:j + 1],
                                                       ALU.subtract, ALU.mult)
                    last.then_inc(xn_done, 1)

                def powers(src, dst, idst):
                    link(nc.vector.tensor_reduce(dst, src, AX.X, ALU.max))
                    link(nc.vector.tensor_reduce(idst, src, AX.X, ALU.min))
                    link(nc.vector.scalar_tensor_tensor(dst, idst, -1.0, dst, ALU.mult, ALU.max))
                    link(nc.vector.tensor_scalar(dst, dst, 1 / LIM, LIM, ALU.max, ALU.min))
                    link(nc.vector.tensor_scalar(dst.bitcast(I32), dst.bitcast(I32), 0x7F800000, None, ALU.bitwise_and))
                    link(nc.vector.tensor_scalar(idst.bitcast(I32), dst.bitcast(I32), -1.0, float(254 << 23),
                                                 ALU.mult, ALU.add))

                def row_scales(m):
                    dve.wait_ge(sc_in, 48)
                    if m < 2:
                        src = sraw[m].rearrange("p (t b) -> p t b", b=C // BLOCK)
                        powers(src, big[m][:], inv[m][:])
                        link(nc.vector.scalar_tensor_tensor(
                            sc[m][:].rearrange("p g (a b) -> p (g a) b", a=2), src, NIB * WS,
                            inv[m][:].unsqueeze(2).broadcast_to([P, 2 * NG, C // BLOCK]), ALU.mult, ALU.mult))
                        return
                    src = sraw[2].rearrange("p (k b) -> p k b", k=KT)
                    powers(src, big[2][:], inv[2][:])
                    for k in range(KT):
                        link(nc.vector.tensor_scalar(
                            sc[2][:].rearrange("p g (k b) -> p k g b", k=KT)[:, k],
                            src[:, k, :].rearrange("p (g b) -> p g b", g=NG), inv[2][:, k:k + 1], NIB * WS,
                            ALU.mult, ALU.mult))

                def scale_tables():
                    rows = big[0][:].rearrange("p (g a) -> p g a", a=2)
                    link(nc.vector.tensor_scalar(tab[:, :, 0:2], rows, float(np.sqrt(GELU_A)) / (XS * WS), None, ALU.mult))
                    link(nc.vector.tensor_scalar(tab[:, :, 2:4], rows, GELU_C / (XS * WS), None, ALU.mult))
                    link(nc.vector.tensor_tensor(rr[:], big[0][:], big[1][:], ALU.mult))
                    nc.vector.tensor_reduce(rmax[:], rr[:], AX.X, ALU.max).then_inc(rmax_done, 1)
                    dve.wait_ge(rall_done, 1)
                    link(nc.vector.tensor_scalar(rinv[:].bitcast(I32), rall[:].bitcast(I32), -1.0, float(254 << 23),
                                                 ALU.mult, ALU.add))
                    link(nc.vector.tensor_scalar(tab[:, :, 4:6], rr[:].rearrange("p (g a) -> p g a", a=2),
                                                 rinv[:, 0:1], None, ALU.mult))
                    link(nc.vector.tensor_scalar(oscale[:], big[2][:], rall[:, 0:1], 1 / (WS * IS), ALU.mult, ALU.mult))
                    nc.vector.tensor_copy(cur[0][:], tab[:, 0, :]).then_inc(cur_done, 1)

                def turned_lo(c, k):
                    n = KT * c + k
                    dve.wait_ge(xh_done, n + 1)
                    nc.vector.scalar_tensor_tensor(xl[:, k, c * CH:(c + 1) * CH], turn[n % 2][:], XS,
                                                   xh[:, k, c * CH:(c + 1) * CH], ALU.mult, ALU.subtract
                                                   ).then_inc(xl_done, 1)

                layer_norm(0)
                dve.wait_ge(w_in, 32)
                for k in range(KT):
                    nc.vector.tensor_copy(wq[:, k, :].rearrange("p (g r d) -> p g r d", r=REP, g=KVH),
                                          wqn[:, k, :].rearrange("p (r g d) -> p g r d", r=REP, g=KVH)
                                          ).then_inc(wq_done, 1)
                for k in range(KT):
                    turned_lo(0, k)
                layer_norm(1)
                for c in range(NCH):
                    for j in range(NPROJ):
                        n = NPROJ * c + j
                        dve.wait_ge(part_hi, n + 1)
                        if n >= 2:
                            wait_stored(dve, n - 2)
                        nc.vector.scalar_tensor_tensor(pl[n % 2], proj[n % 2][:], QSCALE if j else 1.0,
                                                       ph[n % 2].bitcast(F32), ALU.mult, ALU.subtract
                                                       ).then_inc(part_lo, 1)
                        if c + 1 < NCH and j >= 1:
                            turned_lo(c + 1, j - 1)
                        if c + 2 < NCH and j == NORM_STEP:
                            layer_norm(c + 2)
                        if (c, j) in TURN_FIRST_AT:
                            for a in range(2):
                                weights_lo(dve, TURN_FIRST_AT[c, j], a, 0, 0)
                        if (c, j) in SCALES_AT:
                            row_scales(SCALES_AT[c, j])
                        if (c, j) == TABLES_AT:
                            scale_tables()
                        if (c, j) in DECODE_FIRST_AT:
                            if DECODE_FIRST_AT[c, j] == 0:
                                dve.wait_ge(augk_done, 2 * NCH)
                            for step in range(5):
                                decode_step(dve, DECODE_FIRST_AT[c, j], step, 0, 0)
                    dve.wait_ge(v_hi, c + 1)
                    nc.vector.tensor_tensor(vt[:, :, :, 1, :], vps[:].rearrange("p (j g d) -> p j g d", j=TPC, g=KVH),
                                            vt[:, :, :, 0, :].bitcast(F32), ALU.subtract).then_inc(v_lo, 1)


def main_loop(nc, e):
    q_s, k_s, v_s, aug_s, o_s = (e[n] for n in ("q_s", "k_s", "v_s", "aug_s", "o_s"))
    xh, xl, acc, ident, identb, mask_ts, mask_st, tab, on = (
        e[n] for n in ("xh", "xl", "acc", "ident", "identb", "mask_ts", "mask_st", "tab", "on"))
    identr, wh, wl, cur, qst, kst, vst, o3 = (
        e[n] for n in ("identr", "wh", "wl", "cur", "qst", "kst", "vst", "o3"))
    Wo, wo, oc, wo_in, o_in = (e[n] for n in ("Wo", "wo", "oc", "wo_in", "o_in"))
    raw_in, k_in, v_in, q_in, p_out, v_out, cur_done, wf_done, wl_done = (
        e[n] for n in ("raw_in", "k_in", "v_in", "q_in", "p_out", "v_out", "cur_done", "wf_done", "wl_done"))
    with ExitStack() as ctx:
        def sb(name, shape, dt):
            return ctx.enter_context(nc.sbuf_tensor(name, shape, dt))

        def bank(name):
            return ctx.enter_context(nc.psum_tensor(name, [P, CH], F32))

        def sem(name):
            return ctx.enter_context(nc.semaphore(name))

        gl = [sb(f"gl{a}", [P, CH], F32) for a in range(2)]
        prod = [sb(f"prod{a}", [P, CH], F32) for a in range(2)]
        ih = [sb(f"ih{b}", [P, 2, CH], F16) for b in range(2)]
        il = [sb(f"il{b}", [P, 2, CH], F16) for b in range(2)]
        PR, PP = 3, 4
        p32 = [sb(f"p32_{i}", [P, CH], F32) for i in range(PR)]
        phi = [sb(f"phi{i}", [P, CH], F32R) for i in range(PP)]
        plo = [sb(f"plo{i}", [P, CH], F32R) for i in range(PP)]
        mxp = [sb(f"mxp{i}", [P, TPC, NCH], F32) for i in range(2)]
        mxc = sb("mxc", [P, TPC], F32)
        nmx = sb("nmx", [P, TPC, NB], F32R)
        oraw = [sb(f"oraw{i}", [3 * HD, CH], F32) for i in range(2)]

        gate_ps, up_ps, turn_ps, max_ps, score_ps, o_ps = (
            bank(n) for n in ("gate_ps", "up_ps", "turn_ps", "max_ps", "score_ps", "o_ps"))
        down_ps = [bank(f"down_ps{i}") for i in range(2)]
        pair_ps = (max_ps, turn_ps)

        o_out = [sem(f"o_out{i}") for i in range(2)]
        on_out = sem("on_out")
        recip_done = sem("recip_done")
        osum_done = sem("osum_done")
        on_done = sem("on_done")
        gate_done = sem("gate_done")
        up_done = sem("up_done")
        down_done = sem("down_done")
        max_done = sem("max_done")
        maxt_done = sem("maxt_done")
        score_done = sem("score_done")
        pv_done = sem("pv_done")
        square_done = sem("square_done")
        inner_done = sem("inner_done")
        tanh_done = sem("tanh_done")
        gelu_done = sem("gelu_done")
        prod_done = sem("prod_done")
        ih_done = sem("ih_done")
        il_done = sem("il_done")
        exp_done = sem("exp_done")
        phi_done = sem("phi_done")
        plo_done = sem("plo_done")
        brow_done = sem("brow_done")
        oraw_done = sem("oraw_done")
        red_done = sem("red_done")
        mxc_done = sem("mxc_done")
        nhi_done = sem("nhi_done")
        nmx_done = sem("nmx_done")
        acc_done = sem("acc_done")

        load_raw, decode_step, turn_weights, weights_hi, weights_lo = weight_steps(nc, e, pair_ps)

        def loop(eng, body):
            with eng.Fori(0, HEADS // 2) as pair:
                for par in range(2):
                    body(pair * 2 + par, par, pair)

        SEEDED = (gelu_done, prod_done, red_done, brow_done, exp_done, oraw_done, plo_done, il_done,
                  pv_done, down_done, mxc_done, maxt_done, square_done, on_done, on_out, *o_out)

        def after(signals):
            return signals + 1

        def since(base, k, ring):
            return base + max(k - ring + 1, 0)

        GU = 2 * NCH
        ND = NCH * TPC

        with nc.Block() as block:
            @block.sync
            def _(sp):
                def load_k(i, b):
                    for part, at in ((0, HD), (0, 2 * HD), (1, 3 * HD)):
                        sp.dma_start(kst[b][at:at + HD, :].bitcast(F32), k_s[part, bass.ds(i // REP * HD, HD), :]
                                     ).then_inc(k_in[b], 16)

                def load_v(i, b):
                    sp.dma_start(vst[b][:, :, 0:2 * HD].bitcast(F32),
                                 v_s[bass.ds(i // REP, 1)].rearrange("o p t d -> (o p) t d")).then_inc(v_in[b], 16)

                def load_q(i, c):
                    cols = slice(c * CH, (c + 1) * CH)
                    sp.dma_start(qst[0:AUG, c, :].bitcast(F32), aug_s[bass.ds(i * AUG, AUG), cols]).then_inc(q_in[c], 16)
                    for part, at in ((0, HD), (1, 2 * HD), (0, 3 * HD)):
                        sp.dma_start(qst[at:at + HD, c, :].bitcast(F32), q_s[part, bass.ds(i * HD, HD), cols]).then_inc(q_in[c], 16)

                for seeded in SEEDED:
                    sp.sem_inc(seeded, 1)
                sp.wait_ge(v_out, 16 * KVH * NCH)
                for stored in p_out:
                    sp.wait_ge(stored, 32 * NCH)
                load_v(0, 0)
                for m in range(3):
                    load_raw(sp, m, 1)

                def body(i, par, pair):
                    nxt = (i + 1) % HEADS
                    sp.wait_ge(pv_done, after(i * NBLK))
                    load_k(nxt, 1 - par)
                    load_v(nxt, 1 - par)
                    for c in range(NCH):
                        sp.wait_ge(score_done, i * NBLK + BLK_END[c])
                        load_q(nxt, c)
                        if c:
                            gather_o(i, c - 1, par)
                        if c == 2:
                            store_on(i)
                    for m in range(3):
                        sp.wait_ge(wf_done, (i + 1) * 6 + 2 * m + 2)
                        load_raw(sp, m, (i + 2) % HEADS)
                    gather_o(i, NCH - 1, par)

                def gather_o(i, c, par):
                    sp.wait_ge(oraw_done, after(i * NCH + c + 1))
                    if c == 0:
                        sp.wait_ge(on_done, after(i))
                    for part in range(3):
                        sp.dma_start(o3[par][c * HD:(c + 1) * HD, part, :],
                                     oraw[c % 2][part * HD:(part + 1) * HD, :]).then_inc(o_out[c % 2], 16)

                def store_on(i):
                    sp.wait_ge(on_done, after(i + 1))
                    sp.dma_start(o_s[bass.ds(i, 1)].rearrange("o d (c t) -> (o c) d t", c=NCH), on[:]
                                 ).then_inc(on_out, 16)

                loop(sp, body)
                sp.wait_ge(on_out, after(16 * HEADS))
                sp.wait_ge(up_done, HEADS * GU)
                for g in range(KVH):
                    sp.dma_start(wo[:, g, :], Wo.rearrange("(r g d) n -> g r d n", r=REP, g=KVH)[g]).then_inc(wo_in, 16)
                for c in range(len(oc)):
                    load_heads(sp, oc, o_s, o_in, c)
                for m in range(3):
                    sp.wait_ge(raw_in[m], 16 * (HEADS + 2))
                sp.wait_ge(k_in[0], K_FIRST + 48 * (HEADS // 2))
                sp.wait_ge(v_in[0], 16 * (HEADS // 2 + 1))
                for c in range(NCH):
                    sp.wait_ge(q_in[c], 64 * (HEADS + 1))
                for b in range(2):
                    sp.wait_ge(o_out[b], after(48 * HEADS * NCH // 2))

            @block.tensor
            def _(pe):
                def body(i, par, pair):
                    def mlp(s, half):
                        kind, w, a, part = PIECES[s]
                        if kind == "down":
                            n = w * TPC + a
                            dst = down_ps[n % 2]
                            for q in range(3 * half, 3 * half + 3):
                                if q == 0:
                                    pe.wait_ge(ih_done, i * GU + 2 * w + 2)
                                    pe.wait_ge(acc_done, after(since(i * ND, n, 2)))
                                b, term = q // 3, q % 3
                                if term == 2:
                                    pe.wait_ge(il_done, after(i * GU + 2 * w + b + 1))
                                lhs = (ih, ih, il)[term][w % 2][:, b, a * P:(a + 1) * P]
                                rhs = (wh, wl, wh)[term][par][:, 2, b, :]
                                mm = nc.tensor.matmul(dst[:], lhs, rhs, start=(q == 0), stop=(q == 5))
                            if half:
                                mm.then_inc(down_done, 1)
                            return
                        m = 0 if kind == "gate" else 1
                        dst = gate_ps if m == 0 else up_ps
                        n = 2 * w + a
                        for q in range(6 * part + 3 * half, 6 * part + 3 * half + 3):
                            if q == 0:
                                pe.wait_ge(gelu_done if m == 0 else prod_done, after(i * GU + n))
                            k, term = q // 3, q % 3
                            lhs = (wh, wl, wh)[term][par][:, m, a, k * P:(k + 1) * P]
                            rhs = (xh, xh, xl)[term][:, k, w * CH:(w + 1) * CH]
                            mm = nc.tensor.matmul(dst[:], lhs, rhs, start=(q == 0), stop=(q == 11))
                        if part and half:
                            mm.then_inc(gate_done if m == 0 else up_done, 1)

                    def maximum(n):
                        c, t, m = MAXP[n]
                        if t == 0 and m == 0:
                            pe.wait_ge(q_in[c], (i + 1) * 64)
                        pe.wait_ge(red_done, after(since(i * NMAX, n, 2)))
                        dst = pair_ps[n % 2]
                        diag = m == c
                        cols = (t + 1) * P if diag else CH
                        mm = nc.tensor.matmul(dst[:, 0:cols], qst[:, c, t * P:(t + 1) * P],
                                                 kst[par][:, m * CH:m * CH + cols], start=True, stop=True)
                        if diag:
                            mm = nc.tensor.matmul(dst[:, cols - P:cols], identb[:], mask_ts[:], start=False,
                                                     stop=True, skip_group_check=True)
                        mm.then_inc(max_done, 1)

                    def turn_max(c):
                        pe.wait_ge(nmx_done, i * NCH + c + 1)
                        pe.wait_ge(exp_done, after(i * NBLK + BLOCKS_BY_TURN[c]))
                        for t in range(TPC):
                            mm = nc.tensor.matmul(score_ps[0:NB, t * P:(t + 1) * P], nmx[:, t, :], identr[:],
                                                  start=True, stop=True)
                        mm.then_inc(maxt_done, 1)

                    def score(n):
                        c, tiles, _ = BLOCKS[n]
                        if n in BLOCKS_BY_TURN:
                            pe.wait_ge(brow_done, after(i * NCH + BLOCKS_BY_TURN.index(n) + 1))
                        pe.wait_ge(exp_done, after(i * NBLK + n))
                        for at, (j, col, tok) in enumerate(tiles):
                            width = CH - tok
                            diag = j >= TPC * c
                            mm = nc.tensor.matmul(score_ps[:, col:col + width], kst[par][:, j * P:(j + 1) * P],
                                                  qst[:, c, tok:CH], start=True, stop=True,
                                                  skip_group_check=True)
                            if diag:
                                mm = nc.tensor.matmul(score_ps[:, col:col + P], identb[:], mask_st[:], start=False,
                                                      stop=True, skip_group_check=True)
                        mm.then_inc(score_done, 1)

                    def values(n):
                        c, tiles, _ = BLOCKS[n]
                        if n == 0:
                            pe.wait_ge(v_in[par], (pair + 1) * 16)
                        if n == 0 or BLOCKS[n - 1][0] != c:
                            pe.wait_ge(oraw_done, after(i * NCH + c))
                        pe.wait_ge(phi_done, i * NBLK + n + 1)
                        pe.wait_ge(plo_done, after(i * NBLK + n + 1))
                        for src in (phi, plo):
                            for j, col, tok in tiles:
                                width = CH - tok
                                mm = nc.tensor.matmul(
                                    o_ps[0:3 * HD, tok:CH], vst[par][:, j, :], src[n % PP][:, col:col + width],
                                    start=(j == 0 and src is phi), stop=(n == BLK_END[c] - 1 and src is plo),
                                    skip_group_check=True)
                        mm.then_inc(pv_done, 1)

                    pe.wait_ge(k_in[par], pair * 48 + (K_FIRST if par == 0 else 48))
                    pe.wait_ge(wl_done, (i + 1) * 6)
                    for s in range(SLOTS):
                        if s in SCORE_AT:
                            score(SCORE_AT[s])
                        if MAX_AT[s]:
                            maximum(MAX_AT[s][0])
                        mlp(s, 0)
                        if s in VALUES_AT:
                            values(VALUES_AT[s])
                        if len(MAX_AT[s]) > 1:
                            maximum(MAX_AT[s][1])
                        mlp(s, 1)
                        if s in TURN_MAX_AT:
                            turn_max(TURN_MAX_AT[s])
                        if s in TURN_W_AT:
                            m, a = TURN_W_AT[s]
                            turn_weights(pe, m, a, i + 1, (red_done, after((i + 1) * NMAX)))

                loop(pe, body)

            @block.scalar
            def _(act):
                def body(i, par, pair):
                    def square(n):
                        a = n % 2
                        act.wait_ge(gate_done, i * GU + n + 1)
                        act.wait_ge(prod_done, after(since(i * GU, n, 2)))
                        nc.scalar.activation(gl[a][:], gate_ps[:], ACT.Square,
                                             scale=cur[par][:, a:a + 1]).then_inc(square_done, 1)

                    def tanh(n):
                        a = n % 2
                        act.wait_ge(inner_done, i * GU + n + 1)
                        nc.scalar.activation(gl[a][:], gl[a][:], ACT.Tanh,
                                             scale=cur[par][:, 2 + a:3 + a]).then_inc(tanh_done, 1)

                    def exp(n):
                        cols = BLOCKS[n][2]
                        act.wait_ge(score_done, i * NBLK + n + 1)
                        act.wait_ge(plo_done, after(since(i * NBLK, n, PR)))
                        nc.scalar.activation(p32[n % PR][:, 0:cols], score_ps[:, 0:cols], ACT.Exp).then_inc(exp_done, 1)

                    def prob_hi(n):
                        cols = BLOCKS[n][2]
                        act.wait_ge(exp_done, after(i * NBLK + n + 1))
                        act.wait_ge(pv_done, after(since(i * NBLK, n, PP)))
                        nc.scalar.activation(phi[n % PP][:, 0:cols], p32[n % PR][:, 0:cols], ACT.Copy).then_inc(phi_done, 1)

                    def max_rows(c):
                        act.wait_ge(maxt_done, after(i * NCH + c + 1))
                        nc.scalar.activation(qst[0:NB, c, :], score_ps[0:NB, :], ACT.Copy).then_inc(brow_done, 1)

                    def o_copy(c):
                        act.wait_ge(pv_done, after(i * NBLK + BLK_END[c]))
                        act.wait_ge(o_out[c % 2], after((i * 2 + c // 2) * 48))
                        nc.scalar.activation(oraw[c % 2][:], o_ps[0:3 * HD, :], ACT.Copy).then_inc(oraw_done, 1)

                    act.wait_ge(cur_done, i + 1)
                    for s in range(SLOTS + 2):
                        if s - 1 in TURN_MAX_AT:
                            max_rows(TURN_MAX_AT[s - 1])
                        if 1 <= s <= SLOTS and PIECES[s - 1][0] == "gate" and PIECES[s - 1][3]:
                            square(2 * PIECES[s - 1][1] + PIECES[s - 1][2])
                        if s in SCORE_AT:
                            exp(SCORE_AT[s])
                        if 2 <= s and PIECES[s - 2][0] == "gate" and PIECES[s - 2][3]:
                            tanh(2 * PIECES[s - 2][1] + PIECES[s - 2][2])
                        if s - 1 in TURN_W_AT:
                            m, a = TURN_W_AT[s - 1]
                            if (m, a) == (0, 0):
                                act.wait_ge(down_done, after(i * ND))
                            weights_hi(act, m, a, i + 1, 1 - par)
                        if s in SCORE_AT:
                            prob_hi(SCORE_AT[s])
                        if VALUES_AT.get(s, -1) + 1 in BLK_END:
                            o_copy(BLOCKS[VALUES_AT[s]][0])

                loop(act, body)

            @block.vector
            def _(dve):
                def reciprocals(i, q, b):
                    if q == 0:
                        for o in o_out:
                            dve.wait_ge(o, after(i * NCH // 2 * 48))
                    cols = slice(q * P, (q + 1) * P)
                    nc.vector.reciprocal(o3[b][:, 2, cols], o3[b][:, 2, cols]).then_inc(recip_done, 1)

                def body(i, par, pair):
                    nxt = (i + 1) % HEADS

                    def inner(n):
                        a = n % 2
                        dve.wait_ge(square_done, after(i * GU + n + 1))
                        nc.vector.scalar_tensor_tensor(gl[a][:], gl[a][:], 1.0, gate_ps[:], ALU.add, ALU.mult
                                                       ).then_inc(inner_done, 1)

                    def gelu(n):
                        a = n % 2
                        dve.wait_ge(tanh_done, i * GU + n + 1)
                        nc.vector.scalar_tensor_tensor(gl[a][:], gl[a][:], 1.0, gate_ps[:], ALU.add, ALU.mult
                                                       ).then_inc(gelu_done, 1)

                    def product(n):
                        a = n % 2
                        dve.wait_ge(up_done, i * GU + n + 1)
                        dve.wait_ge(gelu_done, after(i * GU + n + 1))
                        dve.wait_ge(il_done, after(since(i * GU, n, 2)))
                        nc.vector.scalar_tensor_tensor(prod[a][:], gl[a][:], 0.5 * IS / (XS * WS) ** 2, up_ps[:],
                                                       ALU.mult, ALU.mult).then_inc(prod_done, 1)

                    def product_hi(n):
                        w, a = n // 2, n % 2
                        dve.wait_ge(prod_done, after(i * GU + n + 1))
                        if a == 0:
                            dve.wait_ge(down_done, after(i * ND + max(TPC * (w - 1), 0)))
                        nc.vector.tensor_copy(ih[w % 2][:, a, :], prod[a][:]).then_inc(ih_done, 1)

                    def accumulate(n):
                        dve.wait_ge(down_done, after(i * ND + n + 1))
                        if n == 0:
                            dve.wait_ge(acc_done, after(i * ND))
                        nc.vector.tensor_tensor(acc[:, n, :], down_ps[n % 2][:], acc[:, n, :], ALU.add
                                                ).then_inc(acc_done, 1)

                    def reduce(n):
                        c, t, m = MAXP[n]
                        cols = (t + 1) * P if m == c else CH
                        dve.wait_ge(max_done, i * NMAX + n + 1)
                        if t == 0 and m == 0:
                            dve.wait_ge(mxc_done, after(since(i * NCH, c, 2)))
                        nc.vector.tensor_reduce(mxp[c % 2][:, t, m:m + 1], pair_ps[n % 2][:, 0:cols], AX.X, ALU.max
                                                ).then_inc(red_done, 1)

                    def negate_max(c):
                        dve.wait_ge(red_done, after(i * NMAX + MAX_END[c]))
                        nc.vector.tensor_reduce(mxc[:], mxp[c % 2][:, :, 0:c + 1], AX.X, ALU.max).then_inc(mxc_done, 1)
                        dve.wait_ge(mxc_done, after(i * NCH + c + 1))
                        dve.wait_ge(maxt_done, after(i * NCH + c))
                        nc.vector.tensor_scalar(nmx[:, :, 0], mxc[:], -1.0, None, ALU.mult).then_inc(nhi_done, 1)
                        dve.wait_ge(nhi_done, i * NCH + c + 1)
                        nc.vector.scalar_tensor_tensor(nmx[:, :, 1], mxc[:], -1.0, nmx[:, :, 0].bitcast(F32),
                                                       ALU.mult, ALU.subtract).then_inc(nmx_done, 1)

                    for s in range(SLOTS + 2):
                        if s in RECIP_AT:
                            reciprocals(i, RECIP_AT[s], 1 - par)
                        last = PIECES[s - 1] if 1 <= s <= SLOTS else ("", 0, 0, 0)
                        n = 2 * last[1] + last[2]
                        if last[0] == "down":
                            accumulate(last[1] * TPC + last[2])
                        if s < SLOTS and MAX_AT[s]:
                            reduce(MAX_AT[s][0])
                        if last[0] == "up" and last[3]:
                            product(n)
                        if last[0] == "gate" and last[3]:
                            inner(n)
                        if s < SLOTS and MAX_AT[s] and MAX_AT[s][0] + 1 in MAX_END:
                            negate_max(MAXP[MAX_AT[s][0]][0])
                        if last[0] == "up" and last[3]:
                            product_hi(n)
                        if s < SLOTS and len(MAX_AT[s]) > 1:
                            reduce(MAX_AT[s][1])
                            if MAX_AT[s][1] + 1 in MAX_END:
                                negate_max(MAXP[MAX_AT[s][1]][0])
                        gate = PIECES[s - 2] if 2 <= s else ("", 0, 0, 0)
                        if gate[0] == "gate" and gate[3]:
                            gelu(2 * gate[1] + gate[2])
                        if s == DECODE_FIRST:
                            dve.wait_ge(gelu_done, after(i * GU))
                            dve.wait_ge(square_done, after(i * GU))
                            dve.wait_ge(wl_done, (i + 1) * 6)
                            nc.vector.tensor_copy(cur[1 - par][:], tab[:, bass.ds(nxt, 1), :].rearrange("p o c -> p (o c)")
                                                  ).then_inc(cur_done, 1)
                        if s in DECODE_AT:
                            decode_step(dve, *DECODE_AT[s], nxt, i + 1)
                        if s - 1 in TURN_W_AT:
                            weights_lo(dve, *TURN_W_AT[s - 1], i + 1, 1 - par)

                loop(dve, body)
                for q in range(4):
                    reciprocals(HEADS, q, 1)

            @block.gpsimd
            def _(pool):
                nc.gpsimd.memset(acc[:], 0.0).then_inc(acc_done, 1)

                def add_parts(i, b):
                    for o in o_out:
                        pool.wait_ge(o, after(i * NCH // 2 * 48))
                    pool.wait_ge(on_out, after(16 * i))
                    nc.gpsimd.tensor_tensor(on[:], o3[b][:, 0, :], o3[b][:, 1, :], ALU.add).then_inc(osum_done, 1)

                def normalise(i, b):
                    pool.wait_ge(recip_done, 4 * (i + 1))
                    pool.wait_ge(osum_done, i + 1)
                    nc.gpsimd.tensor_tensor(on[:], on[:], o3[b][:, 2, :], ALU.mult).then_inc(on_done, 1)

                def body(i, par, pair):
                    def prob_lo(n):
                        cols = BLOCKS[n][2]
                        pool.wait_ge(phi_done, i * NBLK + n + 1)
                        pool.wait_ge(pv_done, after(since(i * NBLK, n, PP)))
                        nc.gpsimd.tensor_tensor(plo[n % PP][:, 0:cols], p32[n % PR][:, 0:cols],
                                                phi[n % PP][:, 0:cols].bitcast(F32), ALU.subtract).then_inc(plo_done, 1)

                    def product_lo(n):
                        w, a = n // 2, n % 2
                        pool.wait_ge(ih_done, i * GU + n + 1)
                        pool.wait_ge(down_done, after(i * ND + max(TPC * (w - 1), 0)))
                        nc.gpsimd.tensor_tensor(il[w % 2][:, a, :], prod[a][:], ih[w % 2][:, a, :], ALU.subtract
                                                ).then_inc(il_done, 1)

                    for s in range(SLOTS + 1):
                        if s == ADD_PARTS_AT:
                            add_parts(i, 1 - par)
                        if s == NORMALISE_AT:
                            normalise(i, 1 - par)
                        if 1 <= s and PIECES[s - 1][0] == "up" and PIECES[s - 1][3]:
                            product_lo(2 * PIECES[s - 1][1] + PIECES[s - 1][2])
                        if s in SCORE_AT:
                            prob_lo(SCORE_AT[s])

                loop(pool, body)
                add_parts(HEADS, 1)
                normalise(HEADS, 1)


def epilogue(nc, e):
    x_d, out_d, bo, o_s = (e[n] for n in ("x_d", "out_d", "bo", "o_s"))
    acc, ident, oscale, on, wo, wo_in, o_in = (e[n] for n in ("acc", "ident", "oscale", "on", "wo", "wo_in", "o_in"))
    with ExitStack() as ctx:
        def sb(name, shape, dt):
            return ctx.enter_context(nc.sbuf_tensor(name, shape, dt))

        def sem(name):
            return ctx.enter_context(nc.semaphore(name))

        oc = e["oc"] + [sb("oc_last", [P, KVH, CH], F32)]
        woh, wol = (sb(n, [P, KVH, C], F32R) for n in ("woh", "wol"))
        och, ocl = ([sb(f"{n}{i}", [P, KVH, CH], F32R) for i in range(2)] for n in ("och", "ocl"))
        bias = sb("bias", [P, C], F32)
        ones = sb("ones", [P, P], F32)
        diag = sb("diag", [P, KT, P], F32)
        orow = sb("orow", [P, C], F32)
        xr = [sb(f"xr{c}", [P, TPC, C], F32) for c in range(NCH)]
        row_ps = ctx.enter_context(nc.psum_tensor("row_ps", [P, C], F32))
        YB = 6
        y_ps = [ctx.enter_context(nc.psum_tensor(f"y_ps{i}", [P, C], F32)) for i in range(YB)]
        bias_in = sem("bias_in")
        last_in = [sem(f"last_in{c}") for c in range(NCH)]
        x_in2 = [sem(f"x_in2{c}") for c in range(NCH)]
        wo_hi = sem("wo_hi")
        wo_lo = sem("wo_lo")
        oc_hi = sem("oc_hi")
        oc_lo = [sem(f"oc_lo{c}") for c in range(NCH)]
        diag_done = sem("diag_done")
        row_done = sem("row_done")
        orow_done = sem("orow_done")
        xb_done = sem("xb_done")
        scaled = sem("scaled")
        base_done = sem("base_done")
        y_done = sem("y_done")
        y_read = sem("y_read")
        out_done = sem("out_done")
        PARTS = [(0, 0, KVH - 1), (0, KVH - 1, KVH)] + [(c, 0, KVH) for c in range(1, NCH)]

        with nc.Block() as block:
            @block.sync
            def _(sp):
                for c in range(NCH):
                    sp.dma_start(oc[c][(REP - 1) * HD:, KVH - 1, :], on[c * HD:(c + 1) * HD, :]).then_inc(last_in[c], 16)
                load_heads(sp, oc, o_s, o_in, NCH - 1)
                sp.dma_start(bias[:], bo.rearrange("(o n) -> o n", o=1).broadcast_to([P, C])).then_inc(bias_in, 16)
                for c in range(NCH):
                    sp.dma_start(xr[c][:], x_d[c * CH:(c + 1) * CH, :].rearrange("(j p) h -> p j h", p=P)
                                 ).then_inc(x_in2[c], 16)
                for n in range(NT):
                    sp.wait_ge(y_read, n + 1)
                    sp.dma_start(out_d[n * P:(n + 1) * P, :], xr[n // TPC][:, n % TPC, :]).then_inc(out_done, 16)
                sp.wait_ge(out_done, 16 * NT)

            def rest(eng, ops, part):
                c, g0, g1 = PARTS[part]
                eng.wait_ge(oc_hi, part + 1)
                ops.tensor_tensor(ocl[c % 2][:, g0:g1], oc[c][:, g0:g1], och[c % 2][:, g0:g1].bitcast(F32), ALU.subtract
                                  ).then_inc(oc_lo[c], 1)

            @block.scalar
            def _(act):
                act.wait_ge(wo_in, 16 * KVH)
                nc.scalar.activation(woh[:], wo, ACT.Copy).then_inc(wo_hi, 1)
                for part, (c, g0, g1) in enumerate(PARTS):
                    if g0 == 0:
                        act.wait_ge(o_in[c], 16 * KVH)
                    if g1 == KVH:
                        act.wait_ge(last_in[c], 16)
                    if c >= 2:
                        act.wait_ge(y_done, TPC * (c - 1))
                    nc.scalar.activation(och[c % 2][:, g0:g1], oc[c][:, g0:g1], ACT.Copy).then_inc(oc_hi, 1)

            @block.tensor
            def _(pe):
                def project(n, g):
                    c, t = n // TPC, n % TPC
                    cols = slice(t * P, (t + 1) * P)
                    terms = ((och, woh), (och, wol), (ocl, woh))
                    for q, (lhs, rhs) in enumerate(terms):
                        mm = nc.tensor.matmul(y_ps[n % YB][:], lhs[c % 2][:, g, cols], rhs[:, g, :],
                                              start=(g == 0 and q == 0), stop=(g == KVH - 1 and q == 2))
                    if g == KVH - 1:
                        mm.then_inc(y_done, 1)

                pe.wait_ge(diag_done, KT + 1)
                for k in range(KT):
                    mm = nc.tensor.matmul(row_ps[:, k * P:(k + 1) * P], ones[:], diag[:, k, :], start=True, stop=True)
                mm.then_inc(row_done, 1)
                pe.wait_ge(wo_lo, 1)
                pe.wait_ge(oc_lo[0], 1)
                for t in range(TPC):
                    for g in range(KVH - 1):
                        project(t, g)
                pe.wait_ge(oc_lo[0], 2)
                for t in range(TPC):
                    project(t, KVH - 1)
                for n in range(TPC, NT):
                    if n % TPC == 0:
                        pe.wait_ge(oc_lo[n // TPC], 1)
                    if n >= YB:
                        pe.wait_ge(y_read, n - YB + 1)
                    for g in range(KVH):
                        project(n, g)

            @block.gpsimd
            def _(pool):
                pool.wait_ge(bias_in, 16)
                for c in range(NCH):
                    if c:
                        rest(pool, nc.gpsimd, c + 1)
                    pool.wait_ge(x_in2[c], 16)
                    nc.gpsimd.tensor_tensor(xr[c][:], xr[c][:], bias[:].unsqueeze(1).broadcast_to([P, TPC, C]), ALU.add
                                            ).then_inc(xb_done, 1)

            @block.vector
            def _(dve):
                nc.vector.memset(ones[:], 1.0).then_inc(diag_done, 1)
                for k in range(KT):
                    nc.vector.tensor_scalar(diag[:, k, :], ident[:], oscale[:, k:k + 1], None, ALU.mult
                                            ).then_inc(diag_done, 1)
                dve.wait_ge(wo_hi, 1)
                nc.vector.tensor_tensor(wol[:], wo, woh[:].bitcast(F32), ALU.subtract).then_inc(wo_lo, 1)
                rest(dve, nc.vector, 0)
                rest(dve, nc.vector, 1)
                dve.wait_ge(row_done, 1)
                nc.vector.tensor_copy(orow[:], row_ps[:]).then_inc(orow_done, 1)
                dve.wait_ge(orow_done, 1)
                for c in range(NCH):
                    part = acc[:, c * TPC:(c + 1) * TPC, :]
                    nc.vector.tensor_tensor(part, part, orow[:].unsqueeze(1).broadcast_to([P, TPC, C]), ALU.mult
                                            ).then_inc(scaled, 1)
                    dve.wait_ge(scaled, c + 1)
                    dve.wait_ge(xb_done, c + 1)
                    nc.vector.tensor_tensor(part, part, xr[c][:], ALU.add).then_inc(base_done, 1)
                    dve.wait_ge(base_done, c + 1)
                    for t in range(TPC):
                        n = TPC * c + t
                        dve.wait_ge(y_done, n + 1)
                        nc.vector.tensor_tensor(xr[c][:, t, :], y_ps[n % YB][:], acc[:, n, :], ALU.add
                                                ).then_inc(y_read, 1)


def _round12(v):
    m, ex = np.frexp(np.asarray(v, np.float64))
    return np.ldexp(np.rint(m * 4096) / 4096, ex)


def _alibi_rows():
    start = 2.0 ** (-2.0 ** (-(np.log2(HEADS) - 3.0)))
    pos = np.arange(T, dtype=np.float64)
    rows = np.zeros((HEADS, AUG, T))
    for i in range(HEADS):
        h = (i % REP) * KVH + i // REP
        slope = float(np.float32(start ** (h + 1)))
        hi = float(_round12(slope))
        lo = slope - hi
        a, c = -hi * pos, -lo * pos
        rows[i, 2], rows[i, 3] = hi, lo
        rows[i, 4] = _round12(a)
        rows[i, 5] = a - rows[i, 4]
        rows[i, 6] = _round12(c)
        rows[i, 7] = c - rows[i, 6]
    keys = np.ones((AUG, T))
    keys[2] = keys[3] = pos
    return rows.reshape(HEADS * AUG, T).astype(np.float32), keys.astype(np.float32)


_INS = ["L0_attn_x", "L0_attn_Wq", "L0_attn_Wkv", "L0_attn_Wo", "L0_attn_bo", "L0_ffn_gate_W_packed",
        "L0_ffn_gate_scales", "L0_ffn_up_W_packed", "L0_ffn_up_scales", "L0_ffn_down_W_packed", "L0_ffn_down_scales"]


def kernel(**inputs):
    import concourse.bacc as _bacc
    from concourse.bass_utils import run_bass_kernel_spmd as _run

    nc = _bacc.Bacc("TRN2", target_bir_lowering=False, num_devices=1)
    arrays, ap = {}, {}
    augq, augk = _alibi_rows()
    given = {name: np.ascontiguousarray(inputs[name]) for name in _INS}
    given["augq"], given["augk"] = augq, augk
    for name, a in given.items():
        arrays[f"in_{name}_dram"] = a
        ap[name] = nc.dram_tensor(f"in_{name}_dram", a.shape, mybir.dt.from_np(a.dtype), kind="ExternalInput").ap()
    out = nc.dram_tensor("out_0_dram", (1, T, C), F32, kind="ExternalOutput").ap()
    build(nc, ap["L0_attn_x"], ap["L0_attn_Wq"], ap["L0_attn_Wkv"], ap["L0_attn_Wo"], ap["L0_attn_bo"],
          [ap[f"L0_ffn_{m}_W_packed"] for m in ("gate", "up", "down")],
          [ap[f"L0_ffn_{m}_scales"] for m in ("gate", "up", "down")], ap["augq"], ap["augk"], out)
    r = _run(nc, [arrays], core_ids=[0])
    return r.results[0]["out_0_dram"]
```

```python
from contextlib import ExitStack

import numpy as np

import concourse.bass as bass
from concourse import mybir

F32 = mybir.dt.float32
F32R = mybir.dt.float32r
F16 = mybir.dt.float16
BF16 = mybir.dt.bfloat16
I32 = mybir.dt.int32
ALU = mybir.AluOpType
ACT = mybir.ActivationFunctionType
AX = mybir.AxisListType
RMAX = bass.bass_isa.ReduceOp.max

P = 128
T, C = 2048, 512
HEADS, KVH, HD = 16, 4, 32
REP = HEADS // KVH
MLP = 4096
BLOCK = 32
EPS = 1e-5
KT = C // P
CH = 512
NCH = T // CH
TPC = CH // P
NT = T // P
GROUP = 2 * P
NG = MLP // GROUP
WORDS = GROUP * C // 2 // P
SB = WORDS * 2 // BLOCK
assert NG == HEADS

K_FIRST = 3 * 16 * NCH
AUG = 8
NB = 2

XS = 2.0 ** 4
WS = 2.0 ** 8
NIB = 2.0 ** 14
IS = 2.0 ** -10
LIM = 2.0 ** 60
GELU_C = 0.7978845608028654
GELU_A = 0.044715

SLOTS = 48
PV_LAG = 3


def score_blocks():
    out = []
    for c in range(NCH):
        d = TPC * c
        out += [(c, [(j, 0, 0)], CH) for j in range(d + 1)]
        out.append((c, [(d + 1, 0, P), (d + 3, 3 * P, 3 * P)], CH))
        out.append((c, [(d + 2, 0, 2 * P)], 2 * P))
    return out


BLOCKS = score_blocks()
NBLK = len(BLOCKS)
DIAG = [n for n, b in enumerate(BLOCKS) if b[1][0][0] >= TPC * b[0]]
BLK_END = [sum(b[0] <= c for b in BLOCKS) for c in range(NCH)]
MAXP = [(c, i, m) for c in range(NCH) for i in range(TPC) for m in range(c + 1)]
NMAX = len(MAXP)
MAX_END = [sum(m[0] <= c for m in MAXP) for c in range(NCH)]
MAX_PER_SLOT = [2, 2, 2, 2, 1, 2, 1] + [2, 1] * 4 + [2, 1] * 4 + [2, 1, 1]
MAX_AT = [list(range(sum(MAX_PER_SLOT[:s]), sum(MAX_PER_SLOT[:s + 1]))) for s in range(SLOTS)]
assert sum(MAX_PER_SLOT) == NMAX
DVE_MASKS_FROM = 2
TURN_MAX_AT = {3: 0, 7: 1, 15: 2, 26: 3}
SCORE_SLOTS = [s for s in range(6, SLOTS) if s - 1 not in TURN_MAX_AT][:NBLK]
SCORE_AT = {s: n for n, s in enumerate(SCORE_SLOTS)}
BLOCKS_BY_TURN = [sum(s <= turn for s in SCORE_SLOTS) for turn in TURN_MAX_AT]
VALUES_AT = {s + PV_LAG: n for s, n in SCORE_AT.items()}
assert max(VALUES_AT) < SLOTS
DECODE_FROM = {26: 0, 31: 1, 36: 2}
DECODE_AT = {s + i: (m, i) for s, m in DECODE_FROM.items() for i in range(5)}
DECODE_FIRST = min(DECODE_FROM)
TURN_W_AT = {31: (0, 0), 32: (0, 1), 36: (1, 0), 37: (1, 1), 41: (2, 0), 42: (2, 1)}
RECIP_AT = {20: 0, 21: 1, 22: 2, 23: 3}
ADD_PARTS_AT, NORMALISE_AT = 22, 25

NORM_STEP = 1
SCALES_AT = {(0, 4): 0, (1, 4): 1, (2, 1): 2}
TABLES_AT = (2, 2)
DECODE_FIRST_AT = {(2, 4): 0, (3, 0): 1, (3, 2): 2}
TURN_FIRST_AT = {(3, 0): 0, (3, 2): 1}


def ffn_pieces():
    out = []
    for w in range(NCH):
        for a in range(2):
            out += [("gate", w, a, 0), ("gate", w, a, 1), ("up", w, a, 0), ("up", w, a, 1)]
            if w:
                out += [("down", w - 1, 2 * a, 0), ("down", w - 1, 2 * a + 1, 0)]
    return out + [("down", NCH - 1, t, 0) for t in range(TPC)]


PIECES = ffn_pieces()
assert len(PIECES) == SLOTS


def build(nc, x, Wq, Wkv, Wo, bo, packed, scales, augq, augk, out):
    x_d = x.rearrange("b t c -> (b t) c")
    out_d = out.rearrange("b t c -> (b t) c")

    q_s = nc.dram_tensor("q_parts", [2, HEADS * HD, T], F32, kind="Internal").ap()
    k_s = nc.dram_tensor("k_parts", [2, KVH * HD, T], F32, kind="Internal").ap()
    v_s = nc.dram_tensor("v_parts", [KVH, P, NT, 2 * HD], F32, kind="Internal").ap()
    aug_s = nc.dram_tensor("aug_rows", [HEADS * AUG, T], F32, kind="Internal").ap()
    o_s = nc.dram_tensor("o_heads", [HEADS + 1, HD, T], F32, kind="Internal").ap()

    with ExitStack() as ctx:
        def sb(name, shape, dt, c=ctx):
            return c.enter_context(nc.sbuf_tensor(name, shape, dt))

        def sem(name):
            return ctx.enter_context(nc.semaphore(name))

        xh = sb("xh", [P, KT, T], F16)
        xl = sb("xl", [P, KT, T], F16)
        acc = sb("acc", [P, NT, C], F32)
        ident = sb("ident", [P, P], F32)
        identb = sb("identb", [P, P], BF16)
        mask_ts = sb("mask_ts", [P, P], BF16)
        mask_st = sb("mask_st", [P, P], BF16)
        sc = [sb(f"sc{m}", [P, NG, SB], F32) for m in range(3)]
        tab = sb("tab", [P, NG, 6], F32)
        on = sb("on", [P, CH], F32)
        o3 = [sb(f"o3_{b}", [P, 3, CH], F32) for b in range(2)]
        oscale = sb("oscale", [P, KT], F32)

        wo, *oc = [t[:].rearrange("p k t -> p (k t)").bitcast(F32).rearrange("p (h g n) -> p h g n", h=2, n=CH)[:, h]
                   for t in (xh, xl) for h in range(2)]
        o_out = [sem(f"o_out{i}") for i in range(2)]
        on_out = sem("on_out")
        recip_done = sem("recip_done")
        osum_done = sem("osum_done")
        on_done = sem("on_done")
        wo_in = sem("wo_in")
        o_in = [sem(f"o_in{c}") for c in range(NCH)]

        with ExitStack() as work:
            def tile(name, shape, dt):
                return sb(name, shape, dt, work)

            raw = [tile(f"raw{m}", [P, WORDS], I32) for m in range(3)]
            dec = tile("dec", [P, 2, WORDS], I32)
            wf = tile("wf", [P, 2 * WORDS], F32)
            wh = [tile(f"wh{b}", [P, 3, 2, C], F16) for b in range(2)]
            wl = [tile(f"wl{b}", [P, 3, 2, C], F16) for b in range(2)]
            cur = [tile(f"cur{b}", [P, 6], F32) for b in range(2)]
            qst = tile("qst", [P, NCH, CH], F32R)
            kst = [tile(f"kst{b}", [P, T], F32R) for b in range(2)]
            vst = [tile(f"vst{b}", [P, NT, 3 * HD], F32R) for b in range(2)]

            raw_in = [sem(f"raw_in{m}") for m in range(3)]
            k_in = [sem(f"k_in{b}") for b in range(2)]
            v_in = [sem(f"v_in{b}") for b in range(2)]
            q_in = [sem(f"q_in{c}") for c in range(NCH)]
            p_out = [sem(f"p_out{j}") for j in range(1 + KVH)]
            v_out = sem("v_out")
            dec_step = sem("dec_step")
            cur_done = sem("cur_done")
            wf_done = sem("wf_done")
            wturn_done = sem("wturn_done")
            wh_done = sem("wh_done")
            wl_done = sem("wl_done")

            preamble(nc, locals())
            main_loop(nc, locals())

        epilogue(nc, locals())


def after(signals):
    return signals + 1


def output_steps(nc, e):
    o3, on = e["o3"], e["on"]
    o_out, on_out, recip_done, osum_done, on_done = (
        e[n] for n in ("o_out", "on_out", "recip_done", "osum_done", "on_done"))

    def reciprocals(dve, i, q, b):
        if q == 0:
            for o in o_out:
                dve.wait_ge(o, after(i * NCH // 2 * 48))
        cols = slice(q * P, (q + 1) * P)
        nc.vector.reciprocal(o3[b][:, 2, cols], o3[b][:, 2, cols]).then_inc(recip_done, 1)

    def add_parts(pool, i, b):
        for o in o_out:
            pool.wait_ge(o, after(i * NCH // 2 * 48))
        pool.wait_ge(on_out, after(16 * i))
        nc.gpsimd.tensor_tensor(on[:], o3[b][:, 0, :], o3[b][:, 1, :], ALU.add).then_inc(osum_done, 1)

    def normalise(pool, i, b):
        pool.wait_ge(recip_done, 4 * (i + 1))
        pool.wait_ge(osum_done, i + 1)
        nc.gpsimd.tensor_tensor(on[:], on[:], o3[b][:, 2, :], ALU.mult).then_inc(on_done, 1)

    return reciprocals, add_parts, normalise


def load_heads(sp, oc, o_s, o_in, c):
    cols = slice(c * CH, (c + 1) * CH)
    full = KVH - 1
    sp.dma_start(oc[c][:, 0:full, :], o_s[1:1 + full * REP, :, cols].rearrange("(g r) d t -> (r d) g t", r=REP)
                 ).then_inc(o_in[c], 16)
    sp.dma_start(oc[c][0:(REP - 1) * HD, full, :], o_s[1 + full * REP:HEADS, :, cols].rearrange("r d t -> (r d) t")
                 ).then_inc(o_in[c], 16)


def weight_steps(nc, e, banks):
    packed, ident, sc = e["packed"], e["ident"], e["sc"]
    raw, dec, wf, wh, wl, cur = (e[n] for n in ("raw", "dec", "wf", "wh", "wl", "cur"))
    raw_in, dec_step, cur_done, wf_done, wturn_done, wh_done, wl_done = (
        e[n] for n in ("raw_in", "dec_step", "cur_done", "wf_done", "wturn_done", "wh_done", "wl_done"))

    def load_raw(sp, m, g):
        if m < 2:
            src = packed[m].rearrange("(g a p) w -> g p a w", a=2, p=P)[bass.ds(g, 1)]
            dst = raw[m][:].rearrange("p (a w) -> p a w", a=2)
        else:
            src = packed[2].rearrange("(k p) (g w) -> g p k w", p=P, w=GROUP // 2)[bass.ds(g, 1)]
            dst = raw[m][:].rearrange("p (k w) -> p k w", k=KT)
        sp.dma_start(dst, src.rearrange("o p a w -> (o p) a w")).then_inc(raw_in[m], 16)

    def decode_step(dve, m, step, g, before):
        if step == 0:
            dve.wait_ge(raw_in[m], (before + 1) * 16)
            if m or not isinstance(before, int):
                dve.wait_ge(wf_done, before * 6 + 2 * m)
            nc.vector.tensor_scalar(dec[:, 0], raw[m][:], 28, 19, ALU.logical_shift_left,
                                    ALU.arith_shift_right).then_inc(dec_step, 1)
        if step == 1:
            nc.vector.tensor_scalar(dec[:, 1], raw[m][:], 24, 19, ALU.logical_shift_left,
                                    ALU.arith_shift_right).then_inc(dec_step, 1)
        if step == 2:
            dve.wait_ge(dec_step, before * 9 + m * 3 + 2)
            nc.vector.tensor_scalar(dec[:].rearrange("p a w -> p (a w)"), dec[:].rearrange("p a w -> p (a w)"),
                                    0x8E00, None, ALU.bitwise_and).then_inc(dec_step, 1)
        if step >= 3:
            b = step - 3
            if b == 0:
                dve.wait_ge(dec_step, before * 9 + m * 3 + 3)
                dve.wait_ge(wturn_done, before * 6 + 2 * m)
            codes = dec[:, b].bitcast(F16).rearrange("p (s j two) -> p s j two", j=BLOCK // 2, two=2)[:, :, :, 0]
            nc.vector.tensor_tensor(
                wf[:].rearrange("p (s j two) -> p s j two", j=BLOCK // 2, two=2)[:, :, :, b], codes,
                sc[m][:, bass.ds(g, 1), :].rearrange("p o s -> p (o s)").unsqueeze(2).broadcast_to([P, SB, BLOCK // 2]),
                ALU.mult).then_inc(wf_done, 1)

    def turn_weights(pe, m, a, before, maxima):
        pe.wait_ge(wf_done, before * 6 + 2 * m + 2)
        if maxima is not None or 2 * m + a >= 2:
            pe.wait_ge(wl_done, before * 6 + 2 * m + a - 1)
        if maxima is not None:
            pe.wait_ge(*maxima)
        for k in range(KT):
            at = a * C + k * P if m < 2 else k * GROUP + a * P
            mm = nc.tensor.transpose(banks[a][:, k * P:(k + 1) * P], wf[:, at:at + P], ident[:])
        mm.then_inc(wturn_done, 1)

    def weights_hi(act, m, a, before, b):
        act.wait_ge(wturn_done, before * 6 + 2 * m + a + 1)
        if m == 2:
            act.wait_ge(cur_done, before + 1)
        nc.scalar.activation(wh[b][:, m, a, :], banks[a][:], ACT.Copy,
                             scale=1.0 if m < 2 else cur[b][:, 4 + a:5 + a]).then_inc(wh_done, 1)

    def weights_lo(dve, m, a, before, b):
        dve.wait_ge(wh_done, before * 6 + 2 * m + a + 1)
        nc.vector.scalar_tensor_tensor(wl[b][:, m, a, :], banks[a][:], 1.0 if m < 2 else cur[b][:, 4 + a:5 + a],
                                       wh[b][:, m, a, :], ALU.mult, ALU.subtract).then_inc(wl_done, 1)

    return load_raw, decode_step, turn_weights, weights_hi, weights_lo


def preamble(nc, e):
    (x_d, Wq, Wkv, scales, augq, augk, q_s, k_s, v_s, aug_s) = (
        e[n] for n in ("x_d", "Wq", "Wkv", "scales", "augq", "augk", "q_s", "k_s", "v_s", "aug_s"))
    xh, xl, acc, ident, identb, mask_ts, mask_st, sc, tab, oscale = (
        e[n] for n in ("xh", "xl", "acc", "ident", "identb", "mask_ts", "mask_st", "sc", "tab", "oscale"))
    dec, wf, wh, wl, cur, qst, kst, vst, o3 = (
        e[n] for n in ("dec", "wf", "wh", "wl", "cur", "qst", "kst", "vst", "o3"))
    k_in, q_in, p_out, v_out, cur_done = (e[n] for n in ("k_in", "q_in", "p_out", "v_out", "cur_done"))
    with ExitStack() as ctx:
        def sb(name, shape, dt):
            return ctx.enter_context(nc.sbuf_tensor(name, shape, dt))

        def sem(name):
            return ctx.enter_context(nc.semaphore(name))

        xin = [acc[:, i * TPC:(i + 1) * TPC, :] for i in range(2)]
        wqn = acc[:, 2 * TPC:2 * TPC + KT, :]
        sraw = [acc[:, 2 * TPC + KT + m, :] for m in range(3)]
        augs = acc[:, 2 * TPC:2 * TPC + KT, :].rearrange("p k n -> p (k n)")
        augk_in = [t.rearrange("p (c n) -> p c n", n=CH)
                   for t in (dec[:].rearrange("p a w -> p (a w)").bitcast(F32), wf[:])]
        wkv = xl[:, :, (NCH - 1) * CH:].bitcast(F32)
        xt = [[sb(f"xt{part}{i}", [P, KT, CH], F32R) for i in range(2)] for part in range(2)]
        wq = [sb(f"wq{part}", [P, KT, C], F32R) for part in range(2)]
        wkvs = [t[:].rearrange("p t n -> p (t n)")[:, 0:KT * 2 * KVH * HD].rearrange("p (k n) -> p k n", k=KT)
                for t in vst]
        ph = [o3[0][:, i, :].bitcast(F32R) for i in range(2)]
        pl = [o3[0][:, 2, :].bitcast(F32R), wl[1][:, 0].rearrange("p a n -> p (a n)").bitcast(F32R)]
        vsum = wh[1][:, 2].rearrange("p a n -> p (a n)").bitcast(F32)
        vt = wh[1][:, 0:2].rearrange("p m a n -> p (m a n)").bitcast(F32R).rearrange(
            "p (j g a d) -> p j g a d", j=TPC, g=KVH, a=2)
        small, used = acc[:, NT - 1, :], [0]

        def table(*dims):
            size = int(np.prod(dims))
            at = small[:, used[0]:used[0] + size]
            used[0] += size
            return at.rearrange("p (a b) -> p a b", a=dims[0]) if len(dims) == 2 else at

        stats, mv = table(TPC, 6), table(TPC, 2)
        ve, sd, rs, nt_ = (table(TPC) for _ in range(4))
        big = [table(2 * NG if m < 2 else KT) for m in range(3)]
        inv = [table(2 * NG if m < 2 else KT) for m in range(3)]
        rr = table(2 * NG)
        rmax, rall, rinv = (table(1) for _ in range(3))
        turn = [ctx.enter_context(nc.psum_tensor(f"turn{i}", [P, CH], F32)) for i in range(2)]
        proj = [ctx.enter_context(nc.psum_tensor(f"proj{i}", [P, CH], F32)) for i in range(2)]
        w_ps = [ctx.enter_context(nc.psum_tensor(f"w_ps{i}", [P, CH], F32)) for i in range(2)]
        vps = ctx.enter_context(nc.psum_tensor("vps", [P, CH], F32))

        x_in = [sem(f"x_in{i}") for i in range(2)]
        w_in = sem("w_in")
        kv_hi = sem("kv_hi")
        kv_lo = sem("kv_lo")
        q_hi = sem("q_hi")
        q_lo = sem("q_lo")
        sc_in = sem("sc_in")
        augk_loaded = sem("augk_loaded")
        augk_done = sem("augk_done")
        augq_in = sem("augq_in")
        augq_done = sem("augq_done")
        aug_out = sem("aug_out")
        ident_done = sem("ident_done")
        pool_step = sem("pool_step")
        dve_step = sem("dve_step")
        var_done = sem("var_done")
        stats_done = sem("stats_done")
        sqrt_done = sem("sqrt_done")
        xn_done = sem("xn_done")
        xn_rest = sem("xn_rest")
        turned = sem("turned")
        xtlo_done = sem("xtlo_done")
        rs_done = sem("rs_done")
        xh_done = sem("xh_done")
        xl_done = sem("xl_done")
        projected = sem("projected")
        part_hi = sem("part_hi")
        part_lo = sem("part_lo")
        v_sum = sem("v_sum")
        vsum_done = sem("vsum_done")
        v_turned = sem("v_turned")
        v_hi = sem("v_hi")
        v_lo = sem("v_lo")
        cleared = sem("cleared")
        rmax_done = sem("rmax_done")
        rall_done = sem("rall_done")
        NPROJ = 1 + KVH
        TERMS = ((0, 0), (1, 0), (0, 1))
        POOL_TILES = 2
        CLEARED = 3
        load_raw, decode_step, turn_weights, weights_hi, weights_lo = weight_steps(nc, e, w_ps)
        QSCALE = float(np.float32(1 / np.sqrt(np.float32(HD))))

        def as_given(w):
            return w.rearrange("p (r g d) -> p g r d", r=REP, g=KVH)

        def by_heads(w):
            return w.rearrange("p (g r d) -> p g r d", r=REP, g=KVH)

        def wait_stored(eng, n):
            eng.wait_ge(p_out[n % NPROJ], 32 * (n // NPROJ + 1))

        with nc.Block() as block:
            @block.sync
            def _(sp):
                def load_x(c):
                    if c >= 2:
                        sp.wait_ge(turned, KT * (c - 1))
                    sp.dma_start(xin[c % 2], x_d[c * CH:(c + 1) * CH, :].rearrange("(j p) h -> p j h", p=P)
                                 ).then_inc(x_in[c % 2], 16)

                def first_head(c):
                    cols = slice(c * CH, (c + 1) * CH)
                    wait_stored(sp, NPROJ * c)
                    for part, at in ((0, HD), (0, 2 * HD), (1, 3 * HD)):
                        sp.dma_start(kst[0][at:at + HD, cols].bitcast(F32), k_s[part, 0:HD, cols]).then_inc(k_in[0], 16)
                    wait_stored(sp, NPROJ * c + 1)
                    sp.dma_start(qst[0:AUG, c, :].bitcast(F32), aug_s[0:AUG, cols]).then_inc(q_in[c], 16)
                    for part, at in ((0, HD), (1, 2 * HD), (0, 3 * HD)):
                        sp.dma_start(qst[at:at + HD, c, :].bitcast(F32), q_s[part, 0:HD, cols]).then_inc(q_in[c], 16)

                def store_v(c):
                    sp.wait_ge(v_lo, c + 1)
                    for g in range(KVH):
                        sp.dma_start(v_s[g, :, TPC * c:TPC * (c + 1), :],
                                     vt[:, :, g, :, :].rearrange("p j a d -> p j (a d)").bitcast(F32)).then_inc(v_out, 16)

                load_x(0)
                for h in range(2):
                    half = augk[:, h * 2 * CH:(h + 1) * 2 * CH].rearrange("p (c n) -> p c n", n=CH)
                    sp.dma_start(augk_in[h][0:AUG], half).then_inc(augk_loaded, 16)
                sp.dma_start(wkv, Wkv.rearrange("(k p) n -> p k n", p=P)).then_inc(w_in, 16)
                sp.dma_start(wqn, Wq.rearrange("(k p) n -> p k n", p=P)).then_inc(w_in, 16)
                load_x(1)
                for m in range(2):
                    sp.dma_start(sraw[m].rearrange("p (t b) -> p t b", b=C // BLOCK),
                                 scales[m].rearrange("(t p) b -> p t b", p=P)).then_inc(sc_in, 16)
                sp.dma_start(sraw[2].rearrange("p (k b) -> p k b", k=KT),
                             scales[2].rearrange("(k p) b -> p k b", p=P)).then_inc(sc_in, 16)
                for m in range(3):
                    load_raw(sp, m, 0)
                sp.wait_ge(q_lo, KT)
                sp.dma_start(augs, augq).then_inc(augq_in, 16)
                for c in range(NCH):
                    cols = slice(c * CH, (c + 1) * CH)
                    if c + 2 < NCH:
                        load_x(c + 2)
                    for j in range(NPROJ):
                        n = NPROJ * c + j
                        dst = k_s if j == 0 else q_s
                        rows = slice(0, P) if j == 0 else slice((j - 1) * P, j * P)
                        sp.wait_ge(part_lo, n + 1)
                        sp.dma_start(dst[0, rows, cols], ph[n % 2].bitcast(F32)).then_inc(p_out[j], 16)
                        sp.dma_start(dst[1, rows, cols], pl[n % 2].bitcast(F32)).then_inc(p_out[j], 16)
                        if c and j == 1:
                            store_v(c - 1)
                        if (c, j) == (1, 0):
                            sp.wait_ge(augq_done, NCH)
                            sp.dma_start(aug_s, augs).then_inc(aug_out, 16)
                        if (c, j) == (1, 2):
                            sp.wait_ge(aug_out, 16)
                            sp.wait_ge(cleared, CLEARED)
                            first_head(0)
                            first_head(1)
                        if c >= 2 and j == 2:
                            first_head(c)
                store_v(NCH - 1)

            @block.gpsimd
            def _(pool):
                def normalise(c):
                    pool.wait_ge(rs_done, c + 1)
                    for j in range(POOL_TILES, TPC):
                        last = nc.gpsimd.tensor_scalar(xin[c % 2][:, j, :], xin[c % 2][:, j, :], mv[:, j, 0:1],
                                                       rs[:, j:j + 1], ALU.subtract, ALU.mult)
                    last.then_inc(xn_rest, 1)

                nc.gpsimd.memset(ident[:], 0.0).then_inc(pool_step, 1)
                nc.gpsimd.memset(mask_ts[:], 0.0).then_inc(pool_step, 1)
                nc.gpsimd.memset(mask_st[:], 0.0).then_inc(pool_step, 1)
                pool.wait_ge(pool_step, 3)
                nc.gpsimd.affine_select(out=ident[:], in_=ident[:], compare_op=ALU.not_equal, fill=1.0, base=0,
                                        pattern=[[-1, P]], channel_multiplier=1).then_inc(pool_step, 1)
                nc.gpsimd.affine_select(out=mask_ts[:], in_=mask_ts[:], compare_op=ALU.is_ge, fill=-1e30, base=0,
                                        pattern=[[-1, P]], channel_multiplier=1).then_inc(pool_step, 1)
                nc.gpsimd.affine_select(out=mask_st[:], in_=mask_st[:], compare_op=ALU.is_ge, fill=-1e30, base=0,
                                        pattern=[[1, P]], channel_multiplier=-1).then_inc(pool_step, 1)
                pool.wait_ge(pool_step, 6)
                nc.gpsimd.tensor_copy(identb[:], ident[:]).then_inc(ident_done, 1)
                for b in range(2):
                    nc.gpsimd.memset(kst[b][0:HD, :].bitcast(F32), 0.0).then_inc(cleared, 1)
                nc.gpsimd.memset(qst[0:HD, :, :].bitcast(F32), 0.0).then_inc(cleared, 1)
                pool.wait_ge(kv_hi, 1)
                nc.gpsimd.tensor_tensor(wkvs[1], wkv, wkvs[0].bitcast(F32), ALU.subtract).then_inc(kv_lo, 1)
                for k in range(KT):
                    pool.wait_ge(q_hi, k + 1)
                    nc.gpsimd.tensor_tensor(by_heads(wq[1][:, k, :]), as_given(wqn[:, k, :]),
                                            by_heads(wq[0][:, k, :]).bitcast(F32), ALU.subtract).then_inc(q_lo, 1)
                pool.wait_ge(augk_loaded, 32)
                pool.wait_ge(cleared, CLEARED)
                for b in range(2):
                    for c in range(NCH):
                        nc.gpsimd.tensor_scalar(kst[b][0:AUG, c * CH:(c + 1) * CH], augk_in[c // 2][0:AUG, c % 2], 1.0,
                                                1.0, ALU.mult, ALU.mult).then_inc(augk_done, 1)
                pool.wait_ge(augq_in, 16)
                for c in range(NCH):
                    part = augs[:, c * CH:(c + 1) * CH]
                    nc.gpsimd.tensor_scalar(part.bitcast(F32R), part, 1.0, 1.0, ALU.mult, ALU.mult
                                            ).then_inc(augq_done, 1)
                for c in range(2, NCH):
                    normalise(c)
                pool.wait_ge(rmax_done, 1)
                nc.gpsimd.partition_all_reduce(rall, rmax, P, RMAX).then_inc(rall_done, 1)

            @block.tensor
            def _(pe):
                def turn_x(c, k):
                    n = KT * c + k
                    if k == 0:
                        pe.wait_ge(xn_done, c + 1)
                        if c >= 2:
                            pe.wait_ge(xn_rest, c - 1)
                    if n >= 2:
                        pe.wait_ge(xl_done, n - 1)
                    for j in range(TPC):
                        mm = nc.tensor.transpose(turn[n % 2][:, j * P:(j + 1) * P],
                                                 xin[c % 2][:, j, k * P:(k + 1) * P], ident[:])
                    mm.then_inc(turned, 1)

                def project(c, j):
                    n = NPROJ * c + j
                    if n >= 2:
                        pe.wait_ge(part_lo, n - 1)
                    for k in range(KT):
                        for q, (wpart, xpart) in enumerate(TERMS):
                            lhs = wkvs[wpart][:, k, 0:KVH * HD] if j == 0 else wq[wpart][:, k, (j - 1) * P:j * P]
                            mm = nc.tensor.matmul(proj[n % 2][:], lhs, xt[xpart][c % 2][:, k, :],
                                                  start=(k == 0 and q == 0), stop=(k == KT - 1 and q == 2))
                    mm.then_inc(projected, 1)

                def project_v(c):
                    if c >= 1:
                        pe.wait_ge(v_lo, c)
                    for k in range(KT):
                        for q, (wpart, xpart) in enumerate(TERMS):
                            mm = nc.tensor.matmul(vps[:], wkvs[wpart][:, k, KVH * HD:], xt[xpart][c % 2][:, k, :],
                                                  start=(k == 0 and q == 0), stop=(k == KT - 1 and q == 2))
                    mm.then_inc(v_sum, 1)

                def turn_v(c):
                    pe.wait_ge(vsum_done, c + 1)
                    for j in range(TPC):
                        mm = nc.tensor.transpose(vps[:, j * P:(j + 1) * P], vsum[:, j * P:(j + 1) * P], ident[:])
                    mm.then_inc(v_turned, 1)

                pe.wait_ge(ident_done, 1)
                for k in range(KT):
                    turn_x(0, k)
                for c in range(NCH):
                    pe.wait_ge(xtlo_done, KT * (c + 1))
                    if c == 0:
                        pe.wait_ge(kv_lo, 1)
                    for j in range(NPROJ):
                        if c == 0 and j == 1:
                            pe.wait_ge(q_lo, KT)
                        project(c, j)
                        if c and j == 0:
                            turn_v(c - 1)
                        if c + 1 < NCH and j >= 1:
                            turn_x(c + 1, j - 1)
                        if (c, j) in TURN_FIRST_AT:
                            for a in range(2):
                                turn_weights(pe, TURN_FIRST_AT[c, j], a, 0, None)
                    project_v(c)
                    if c == NCH - 1:
                        for a in range(2):
                            turn_weights(pe, 2, a, 0, None)
                        turn_v(c)

            @block.scalar
            def _(act):
                def root(c):
                    act.wait_ge(var_done, c + 1)
                    nc.scalar.activation(sd, ve, ACT.Sqrt).then_inc(sqrt_done, 1)

                def turned_hi(c, k):
                    n = KT * c + k
                    if k == 0 and c >= 2:
                        act.wait_ge(v_sum, c - 1)
                    act.wait_ge(turned, n + 1)
                    nc.scalar.activation(xt[0][c % 2][:, k, :], turn[n % 2][:], ACT.Copy)
                    nc.scalar.activation(xh[:, k, c * CH:(c + 1) * CH], turn[n % 2][:], ACT.Copy, scale=XS
                                         ).then_inc(xh_done, 1)

                def values_hi(c):
                    act.wait_ge(v_turned, c + 1)
                    if c >= 1:
                        act.wait_ge(v_out, 16 * KVH * c)
                    nc.scalar.activation(vt[:, :, :, 0, :], vps[:].rearrange("p (j g d) -> p j g d", j=TPC, g=KVH),
                                         ACT.Copy).then_inc(v_hi, 1)

                root(0)
                act.wait_ge(w_in, 32)
                nc.scalar.activation(wkvs[0], wkv, ACT.Copy).then_inc(kv_hi, 1)
                for k in range(KT):
                    turned_hi(0, k)
                for k in range(KT):
                    nc.scalar.activation(by_heads(wq[0][:, k, :]), as_given(wqn[:, k, :]), ACT.Copy).then_inc(q_hi, 1)
                root(1)
                for c in range(NCH):
                    for j in range(NPROJ):
                        n = NPROJ * c + j
                        act.wait_ge(projected, n + 1)
                        if n >= 2:
                            wait_stored(act, n - 2)
                        nc.scalar.activation(ph[n % 2], proj[n % 2][:], ACT.Copy, scale=QSCALE if j else 1.0
                                             ).then_inc(part_hi, 1)
                        if c and j == 0:
                            values_hi(c - 1)
                        if c + 1 < NCH and j >= 1:
                            turned_hi(c + 1, j - 1)
                        if c + 2 < NCH and j == NORM_STEP + 1:
                            root(c + 2)
                        if (c, j) in TURN_FIRST_AT:
                            for a in range(2):
                                weights_hi(act, TURN_FIRST_AT[c, j], a, 0, 0)
                    act.wait_ge(v_sum, c + 1)
                    if c >= 1:
                        act.wait_ge(v_turned, c)
                    nc.scalar.activation(vsum, vps[:], ACT.Copy).then_inc(vsum_done, 1)
                for a in range(2):
                    weights_hi(act, 2, a, 0, 0)
                values_hi(NCH - 1)

            @block.vector
            def _(dve):
                steps = [0]

                def link(ins):
                    steps[0] += 1
                    ins.then_inc(dve_step, 1)
                    dve.wait_ge(dve_step, steps[0])

                def layer_norm(c):
                    statistics(c)
                    deviations(c)

                def statistics(c):
                    xc = xin[c % 2]
                    dve.wait_ge(x_in[c % 2], 16 * (c // 2 + 1))
                    for j in range(TPC):
                        last = nc.vector.bn_stats(stats[:, j, :], xc[:, j, :])
                    link(last)
                    if c:
                        dve.wait_ge(xn_done, c)
                    if c >= 3:
                        dve.wait_ge(xn_rest, c - 2)
                    for j in range(TPC):
                        last = nc.vector.bn_aggr(mv[:, j, :], stats[:, j, :])
                    last.then_inc(stats_done, 1)

                def deviations(c):
                    xc = xin[c % 2]
                    dve.wait_ge(stats_done, c + 1)
                    if c:
                        dve.wait_ge(sqrt_done, c)
                    link(nc.vector.tensor_scalar(ve, mv[:, :, 1], EPS, None, ALU.add))
                    nc.vector.tensor_copy(nt_, ve).then_inc(var_done, 1)
                    dve.wait_ge(sqrt_done, c + 1)
                    link(nc.vector.reciprocal(rs, sd))
                    link(nc.vector.tensor_tensor(nt_, rs, rs, ALU.mult))
                    link(nc.vector.tensor_tensor(nt_, nt_, ve, ALU.mult))
                    link(nc.vector.tensor_scalar(nt_, nt_, -0.5, 1.5, ALU.mult, ALU.add))
                    nc.vector.tensor_tensor(rs, rs, nt_, ALU.mult).then_inc(rs_done, 1)
                    dve.wait_ge(rs_done, c + 1)
                    for j in range(TPC if c < 2 else POOL_TILES):
                        last = nc.vector.tensor_scalar(xc[:, j, :], xc[:, j, :], mv[:, j, 0:1], rs[:, j:j + 1],
                                                       ALU.subtract, ALU.mult)
                    last.then_inc(xn_done, 1)

                def powers(src, dst, idst):
                    link(nc.vector.tensor_reduce(dst, src, AX.X, ALU.max))
                    link(nc.vector.tensor_reduce(idst, src, AX.X, ALU.min))
                    link(nc.vector.scalar_tensor_tensor(dst, idst, -1.0, dst, ALU.mult, ALU.max))
                    link(nc.vector.tensor_scalar(dst, dst, 1 / LIM, LIM, ALU.max, ALU.min))
                    link(nc.vector.tensor_scalar(dst.bitcast(I32), dst.bitcast(I32), 0x7F800000, None, ALU.bitwise_and))
                    link(nc.vector.tensor_scalar(idst.bitcast(I32), dst.bitcast(I32), -1.0, float(254 << 23),
                                                 ALU.mult, ALU.add))

                def row_scales(m):
                    dve.wait_ge(sc_in, 48)
                    if m < 2:
                        src = sraw[m].rearrange("p (t b) -> p t b", b=C // BLOCK)
                        powers(src, big[m], inv[m])
                        link(nc.vector.scalar_tensor_tensor(
                            sc[m][:].rearrange("p g (a b) -> p (g a) b", a=2), src, NIB * WS,
                            inv[m].unsqueeze(2).broadcast_to([P, 2 * NG, C // BLOCK]), ALU.mult, ALU.mult))
                        return
                    src = sraw[2].rearrange("p (k b) -> p k b", k=KT)
                    powers(src, big[2], inv[2])
                    for k in range(KT):
                        link(nc.vector.tensor_scalar(
                            sc[2][:].rearrange("p g (k b) -> p k g b", k=KT)[:, k],
                            src[:, k, :].rearrange("p (g b) -> p g b", g=NG), inv[2][:, k:k + 1], NIB * WS,
                            ALU.mult, ALU.mult))

                def scale_tables():
                    rows = big[0].rearrange("p (g a) -> p g a", a=2)
                    link(nc.vector.tensor_scalar(tab[:, :, 0:2], rows, float(np.sqrt(GELU_A)) / (XS * WS), None, ALU.mult))
                    link(nc.vector.tensor_scalar(tab[:, :, 2:4], rows, GELU_C / (XS * WS), None, ALU.mult))
                    link(nc.vector.tensor_tensor(rr, big[0], big[1], ALU.mult))
                    nc.vector.tensor_reduce(rmax, rr, AX.X, ALU.max).then_inc(rmax_done, 1)
                    dve.wait_ge(rall_done, 1)
                    link(nc.vector.tensor_scalar(rinv.bitcast(I32), rall.bitcast(I32), -1.0, float(254 << 23),
                                                 ALU.mult, ALU.add))
                    link(nc.vector.tensor_scalar(tab[:, :, 4:6], rr.rearrange("p (g a) -> p g a", a=2),
                                                 rinv[:, 0:1], None, ALU.mult))
                    link(nc.vector.tensor_scalar(oscale[:], big[2], rall[:, 0:1], 1 / (WS * IS), ALU.mult, ALU.mult))
                    nc.vector.tensor_copy(cur[0][:], tab[:, 0, :]).then_inc(cur_done, 1)

                def turned_lo(c, k):
                    n = KT * c + k
                    dve.wait_ge(xh_done, n + 1)
                    nc.vector.tensor_tensor(xt[1][c % 2][:, k, :], turn[n % 2][:], xt[0][c % 2][:, k, :].bitcast(F32),
                                            ALU.subtract).then_inc(xtlo_done, 1)
                    nc.vector.scalar_tensor_tensor(xl[:, k, c * CH:(c + 1) * CH], turn[n % 2][:], XS,
                                                   xh[:, k, c * CH:(c + 1) * CH], ALU.mult, ALU.subtract
                                                   ).then_inc(xl_done, 1)

                def values_lo(c):
                    dve.wait_ge(v_hi, c + 1)
                    nc.vector.tensor_tensor(vt[:, :, :, 1, :], vps[:].rearrange("p (j g d) -> p j g d", j=TPC, g=KVH),
                                            vt[:, :, :, 0, :].bitcast(F32), ALU.subtract).then_inc(v_lo, 1)

                layer_norm(0)
                for k in range(KT):
                    turned_lo(0, k)
                layer_norm(1)
                for c in range(NCH):
                    for j in range(NPROJ):
                        n = NPROJ * c + j
                        dve.wait_ge(part_hi, n + 1)
                        if n >= 2:
                            wait_stored(dve, n - 2)
                        nc.vector.scalar_tensor_tensor(pl[n % 2], proj[n % 2][:], QSCALE if j else 1.0,
                                                       ph[n % 2].bitcast(F32), ALU.mult, ALU.subtract
                                                       ).then_inc(part_lo, 1)
                        if c and j == 0:
                            values_lo(c - 1)
                        if c + 1 < NCH and j >= 1:
                            turned_lo(c + 1, j - 1)
                        if c + 2 < NCH and j == NORM_STEP:
                            statistics(c + 2)
                        if c + 2 < NCH and j == NORM_STEP + 1:
                            deviations(c + 2)
                        if (c, j) in TURN_FIRST_AT:
                            for a in range(2):
                                weights_lo(dve, TURN_FIRST_AT[c, j], a, 0, 0)
                        if (c, j) in SCALES_AT:
                            row_scales(SCALES_AT[c, j])
                        if (c, j) == TABLES_AT:
                            scale_tables()
                        if (c, j) in DECODE_FIRST_AT:
                            if DECODE_FIRST_AT[c, j] == 0:
                                dve.wait_ge(augk_done, 2 * NCH)
                            for step in range(5):
                                decode_step(dve, DECODE_FIRST_AT[c, j], step, 0, 0)
                for a in range(2):
                    weights_lo(dve, 2, a, 0, 0)
                values_lo(NCH - 1)


def main_loop(nc, e):
    q_s, k_s, v_s, aug_s, o_s = (e[n] for n in ("q_s", "k_s", "v_s", "aug_s", "o_s"))
    xh, xl, acc, ident, identb, mask_ts, mask_st, tab, on = (
        e[n] for n in ("xh", "xl", "acc", "ident", "identb", "mask_ts", "mask_st", "tab", "on"))
    wh, wl, cur, qst, kst, vst, o3 = (
        e[n] for n in ("wh", "wl", "cur", "qst", "kst", "vst", "o3"))
    Wo, wo, oc, wo_in, o_in, o_out, on_out, on_done = (
        e[n] for n in ("Wo", "wo", "oc", "wo_in", "o_in", "o_out", "on_out", "on_done"))
    raw_in, k_in, v_in, q_in, p_out, v_out, cur_done, wf_done, wl_done = (
        e[n] for n in ("raw_in", "k_in", "v_in", "q_in", "p_out", "v_out", "cur_done", "wf_done", "wl_done"))
    with ExitStack() as ctx:
        def sb(name, shape, dt):
            return ctx.enter_context(nc.sbuf_tensor(name, shape, dt))

        def bank(name):
            return ctx.enter_context(nc.psum_tensor(name, [P, CH], F32))

        def sem(name):
            return ctx.enter_context(nc.semaphore(name))

        gl = [sb(f"gl{a}", [P, CH], F32) for a in range(2)]
        prod = [sb(f"prod{a}", [P, CH], F32) for a in range(2)]
        ih = [sb(f"ih{b}", [P, 2, CH], F16) for b in range(2)]
        il = [sb(f"il{b}", [P, 2, CH], F16) for b in range(2)]
        identr = sb("identr", [P, P], F32R)
        PR, PP = 3, 4
        p32 = [sb(f"p32_{i}", [P, CH], F32) for i in range(PR)]
        phi = [sb(f"phi{i}", [P, CH], F32R) for i in range(PP)]
        plo = [sb(f"plo{i}", [P, CH], F32R) for i in range(PP)]
        mxp = [sb(f"mxp{i}", [P, TPC, NCH], F32) for i in range(2)]
        mxc = sb("mxc", [P, TPC], F32)
        nmx = sb("nmx", [P, TPC, NB], F32R)
        oraw = [sb(f"oraw{i}", [3 * HD, CH], F32) for i in range(2)]

        gate_ps, up_ps, turn_ps, max_ps, score_ps, o_ps = (
            bank(n) for n in ("gate_ps", "up_ps", "turn_ps", "max_ps", "score_ps", "o_ps"))
        down_ps = [bank(f"down_ps{i}") for i in range(2)]
        pair_ps = (max_ps, turn_ps)

        identr_done = sem("identr_done")
        o3_ones = sem("o3_ones")
        ones_done = sem("ones_done")
        gate_done = sem("gate_done")
        up_done = sem("up_done")
        down_done = sem("down_done")
        max_done = sem("max_done")
        maxt_done = sem("maxt_done")
        score_done = sem("score_done")
        pv_done = sem("pv_done")
        square_done = sem("square_done")
        inner_done = sem("inner_done")
        tanh_done = sem("tanh_done")
        gelu_done = sem("gelu_done")
        prod_done = sem("prod_done")
        ih_done = sem("ih_done")
        il_done = sem("il_done")
        exp_done = sem("exp_done")
        own_done = sem("own_done")
        masked_done = sem("masked_done")
        phi_done = sem("phi_done")
        plo_done = sem("plo_done")
        brow_done = sem("brow_done")
        oraw_done = sem("oraw_done")
        red_done = sem("red_done")
        mxc_done = sem("mxc_done")
        nhi_done = sem("nhi_done")
        nmx_done = sem("nmx_done")
        acc_done = sem("acc_done")

        load_raw, decode_step, turn_weights, weights_hi, weights_lo = weight_steps(nc, e, pair_ps)
        reciprocals, add_parts, normalise = output_steps(nc, e)

        def loop(eng, body):
            with eng.Fori(0, HEADS // 2) as pair:
                for par in range(2):
                    body(pair * 2 + par, par, pair)

        SEEDED = (gelu_done, prod_done, red_done, brow_done, exp_done, oraw_done, plo_done, il_done,
                  pv_done, down_done, mxc_done, maxt_done, square_done, on_done, on_out, *o_out)

        def since(base, k, ring):
            return base + max(k - ring + 1, 0)

        GU = 2 * NCH
        ND = NCH * TPC

        with nc.Block() as block:
            @block.sync
            def _(sp):
                def load_k(i, b):
                    for part, at in ((0, HD), (0, 2 * HD), (1, 3 * HD)):
                        sp.dma_start(kst[b][at:at + HD, :].bitcast(F32), k_s[part, bass.ds(i // REP * HD, HD), :]
                                     ).then_inc(k_in[b], 16)

                def load_v(i, b):
                    sp.dma_start(vst[b][:, :, 0:2 * HD].bitcast(F32),
                                 v_s[bass.ds(i // REP, 1)].rearrange("o p t d -> (o p) t d")).then_inc(v_in[b], 16)

                def load_q(i, c):
                    cols = slice(c * CH, (c + 1) * CH)
                    sp.dma_start(qst[0:AUG, c, :].bitcast(F32), aug_s[bass.ds(i * AUG, AUG), cols]).then_inc(q_in[c], 16)
                    for part, at in ((0, HD), (1, 2 * HD), (0, 3 * HD)):
                        sp.dma_start(qst[at:at + HD, c, :].bitcast(F32), q_s[part, bass.ds(i * HD, HD), cols]).then_inc(q_in[c], 16)

                for seeded in SEEDED:
                    sp.sem_inc(seeded, 1)
                sp.wait_ge(v_out, 16 * KVH * NCH)
                for stored in p_out:
                    sp.wait_ge(stored, 32 * NCH)
                load_v(0, 0)
                for m in range(3):
                    load_raw(sp, m, 1)

                def body(i, par, pair):
                    nxt = (i + 1) % HEADS
                    sp.wait_ge(pv_done, after(i * NBLK))
                    load_k(nxt, 1 - par)
                    load_v(nxt, 1 - par)
                    for c in range(NCH):
                        sp.wait_ge(score_done, i * NBLK + BLK_END[c])
                        load_q(nxt, c)
                        if c:
                            gather_o(i, c - 1, par)
                        if c == 2:
                            store_on(i)
                    for m in range(3):
                        sp.wait_ge(wf_done, (i + 1) * 6 + 2 * m + 2)
                        load_raw(sp, m, (i + 2) % HEADS)
                    gather_o(i, NCH - 1, par)

                def gather_o(i, c, par):
                    sp.wait_ge(oraw_done, after(i * NCH + c + 1))
                    if c == 0:
                        sp.wait_ge(on_done, after(i))
                    for part in range(3):
                        sp.dma_start(o3[par][c * HD:(c + 1) * HD, part, :],
                                     oraw[c % 2][part * HD:(part + 1) * HD, :]).then_inc(o_out[c % 2], 16)

                def store_on(i):
                    sp.wait_ge(on_done, after(i + 1))
                    sp.dma_start(o_s[bass.ds(i, 1)].rearrange("o d (c t) -> (o c) d t", c=NCH), on[:]
                                 ).then_inc(on_out, 16)

                loop(sp, body)
                sp.wait_ge(on_out, after(16 * HEADS))
                sp.wait_ge(up_done, HEADS * GU)
                for g in range(KVH):
                    sp.dma_start(wo[:, g, :], Wo.rearrange("(r g d) n -> g r d n", r=REP, g=KVH)[g]).then_inc(wo_in, 16)
                load_heads(sp, oc, o_s, o_in, 0)
                for m in range(3):
                    sp.wait_ge(raw_in[m], 16 * (HEADS + 2))
                sp.wait_ge(k_in[0], K_FIRST + 48 * (HEADS // 2))
                sp.wait_ge(v_in[0], 16 * (HEADS // 2 + 1))
                for c in range(NCH):
                    sp.wait_ge(q_in[c], 64 * (HEADS + 1))
                for b in range(2):
                    sp.wait_ge(o_out[b], after(48 * HEADS * NCH // 2))

            @block.tensor
            def _(pe):
                def body(i, par, pair):
                    def mlp(s, half):
                        kind, w, a, part = PIECES[s]
                        if kind == "down":
                            n = w * TPC + a
                            dst = down_ps[n % 2]
                            for q in range(3 * half, 3 * half + 3):
                                if q == 0:
                                    pe.wait_ge(ih_done, i * GU + 2 * w + 2)
                                    pe.wait_ge(acc_done, after(since(i * ND, n, 2)))
                                b, term = q // 3, q % 3
                                if term == 2:
                                    pe.wait_ge(il_done, after(i * GU + 2 * w + b + 1))
                                lhs = (ih, ih, il)[term][w % 2][:, b, a * P:(a + 1) * P]
                                rhs = (wh, wl, wh)[term][par][:, 2, b, :]
                                mm = nc.tensor.matmul(dst[:], lhs, rhs, start=(q == 0), stop=(q == 5))
                            if half:
                                mm.then_inc(down_done, 1)
                            return
                        m = 0 if kind == "gate" else 1
                        dst = gate_ps if m == 0 else up_ps
                        n = 2 * w + a
                        for q in range(6 * part + 3 * half, 6 * part + 3 * half + 3):
                            if q == 0:
                                pe.wait_ge(gelu_done if m == 0 else prod_done, after(i * GU + n))
                            k, term = q // 3, q % 3
                            lhs = (wh, wl, wh)[term][par][:, m, a, k * P:(k + 1) * P]
                            rhs = (xh, xh, xl)[term][:, k, w * CH:(w + 1) * CH]
                            mm = nc.tensor.matmul(dst[:], lhs, rhs, start=(q == 0), stop=(q == 11))
                        if part and half:
                            mm.then_inc(gate_done if m == 0 else up_done, 1)

                    def maximum(n):
                        c, t, m = MAXP[n]
                        if t == 0 and m == 0:
                            pe.wait_ge(q_in[c], (i + 1) * 64)
                        pe.wait_ge(red_done, after(since(i * NMAX, n, 2)))
                        dst = pair_ps[n % 2]
                        diag = m == c
                        cols = (t + 1) * P if diag else CH
                        mm = nc.tensor.matmul(dst[:, 0:cols], qst[:, c, t * P:(t + 1) * P],
                                                 kst[par][:, m * CH:m * CH + cols], start=True, stop=True)
                        if diag and c < DVE_MASKS_FROM:
                            mm = nc.tensor.matmul(dst[:, cols - P:cols], identb[:], mask_ts[:], start=False,
                                                     stop=True, skip_group_check=True)
                        mm.then_inc(max_done, 1)

                    def turn_max(c):
                        if c == 0:
                            pe.wait_ge(identr_done, 1)
                        pe.wait_ge(nmx_done, i * NCH + c + 1)
                        pe.wait_ge(exp_done, after(i * NBLK + BLOCKS_BY_TURN[c]))
                        for t in range(TPC):
                            mm = nc.tensor.matmul(score_ps[0:NB, t * P:(t + 1) * P], nmx[:, t, :], identr[:],
                                                  start=True, stop=True)
                        mm.then_inc(maxt_done, 1)

                    def score(n):
                        c, tiles, _ = BLOCKS[n]
                        if n in BLOCKS_BY_TURN:
                            pe.wait_ge(brow_done, after(i * NCH + BLOCKS_BY_TURN.index(n) + 1))
                        pe.wait_ge(exp_done, after(i * NBLK + n))
                        for j, col, tok in tiles:
                            width = CH - tok
                            mm = nc.tensor.matmul(score_ps[:, col:col + width], kst[par][:, j * P:(j + 1) * P],
                                                  qst[:, c, tok:CH], start=True, stop=True,
                                                  skip_group_check=True)
                        mm.then_inc(score_done, 1)

                    def values(n):
                        c, tiles, _ = BLOCKS[n]
                        if n == 0:
                            pe.wait_ge(ones_done, 2)
                            pe.wait_ge(v_in[par], (pair + 1) * 16)
                        if n == 0 or BLOCKS[n - 1][0] != c:
                            pe.wait_ge(oraw_done, after(i * NCH + c))
                        pe.wait_ge(phi_done, i * NBLK + n + 1)
                        pe.wait_ge(plo_done, after(i * NBLK + n + 1))
                        for src in (phi, plo):
                            for j, col, tok in tiles:
                                width = CH - tok
                                mm = nc.tensor.matmul(
                                    o_ps[0:3 * HD, tok:CH], vst[par][:, j, :], src[n % PP][:, col:col + width],
                                    start=(j == 0 and src is phi), stop=(n == BLK_END[c] - 1 and src is plo),
                                    skip_group_check=True)
                        mm.then_inc(pv_done, 1)

                    pe.wait_ge(k_in[par], pair * 48 + (K_FIRST if par == 0 else 48))
                    pe.wait_ge(wl_done, (i + 1) * 6)
                    for s in range(SLOTS):
                        if s in SCORE_AT:
                            score(SCORE_AT[s])
                        if MAX_AT[s]:
                            maximum(MAX_AT[s][0])
                        mlp(s, 0)
                        if s in VALUES_AT:
                            values(VALUES_AT[s])
                        if len(MAX_AT[s]) > 1:
                            maximum(MAX_AT[s][1])
                        mlp(s, 1)
                        if s in TURN_MAX_AT:
                            turn_max(TURN_MAX_AT[s])
                        if s in TURN_W_AT:
                            m, a = TURN_W_AT[s]
                            turn_weights(pe, m, a, i + 1, (red_done, after((i + 1) * NMAX)))

                loop(pe, body)

            @block.scalar
            def _(act):
                def body(i, par, pair):
                    def square(n):
                        a = n % 2
                        act.wait_ge(gate_done, i * GU + n + 1)
                        act.wait_ge(prod_done, after(since(i * GU, n, 2)))
                        nc.scalar.activation(gl[a][:], gate_ps[:], ACT.Square,
                                             scale=cur[par][:, a:a + 1]).then_inc(square_done, 1)

                    def tanh(n):
                        a = n % 2
                        act.wait_ge(inner_done, i * GU + n + 1)
                        nc.scalar.activation(gl[a][:], gl[a][:], ACT.Tanh,
                                             scale=cur[par][:, 2 + a:3 + a]).then_inc(tanh_done, 1)

                    def exp(n):
                        cols = BLOCKS[n][2]
                        if n in DIAG:
                            act.wait_ge(masked_done, i * len(DIAG) + DIAG.index(n) + 1)
                        else:
                            act.wait_ge(score_done, i * NBLK + n + 1)
                        act.wait_ge(plo_done, after(since(i * NBLK, n, PR)))
                        nc.scalar.activation(p32[n % PR][:, 0:cols], score_ps[:, 0:cols], ACT.Exp).then_inc(exp_done, 1)

                    def prob_hi(n):
                        cols = BLOCKS[n][2]
                        act.wait_ge(exp_done, after(i * NBLK + n + 1))
                        act.wait_ge(pv_done, after(since(i * NBLK, n, PP)))
                        nc.scalar.activation(phi[n % PP][:, 0:cols], p32[n % PR][:, 0:cols], ACT.Copy).then_inc(phi_done, 1)

                    def max_rows(c):
                        act.wait_ge(maxt_done, after(i * NCH + c + 1))
                        nc.scalar.activation(qst[0:NB, c, :], score_ps[0:NB, :], ACT.Copy).then_inc(brow_done, 1)

                    def o_copy(c):
                        act.wait_ge(pv_done, after(i * NBLK + BLK_END[c]))
                        act.wait_ge(o_out[c % 2], after((i * 2 + c // 2) * 48))
                        nc.scalar.activation(oraw[c % 2][:], o_ps[0:3 * HD, :], ACT.Copy).then_inc(oraw_done, 1)

                    act.wait_ge(cur_done, i + 1)
                    for s in range(SLOTS + 2):
                        if s - 1 in TURN_MAX_AT:
                            max_rows(TURN_MAX_AT[s - 1])
                        if 1 <= s <= SLOTS and PIECES[s - 1][0] == "gate" and PIECES[s - 1][3]:
                            square(2 * PIECES[s - 1][1] + PIECES[s - 1][2])
                        if 2 <= s and PIECES[s - 2][0] == "gate" and PIECES[s - 2][3]:
                            tanh(2 * PIECES[s - 2][1] + PIECES[s - 2][2])
                        if s in SCORE_AT:
                            exp(SCORE_AT[s])
                        if s - 1 in TURN_W_AT:
                            m, a = TURN_W_AT[s - 1]
                            if (m, a) == (0, 0):
                                act.wait_ge(down_done, after(i * ND))
                            weights_hi(act, m, a, i + 1, 1 - par)
                        if s in SCORE_AT:
                            prob_hi(SCORE_AT[s])
                        if VALUES_AT.get(s, -1) + 1 in BLK_END:
                            o_copy(BLOCKS[VALUES_AT[s]][0])

                loop(act, body)

            @block.vector
            def _(dve):
                def body(i, par, pair):
                    nxt = (i + 1) % HEADS

                    def inner(n):
                        a = n % 2
                        dve.wait_ge(square_done, after(i * GU + n + 1))
                        nc.vector.scalar_tensor_tensor(gl[a][:], gl[a][:], 1.0, gate_ps[:], ALU.add, ALU.mult
                                                       ).then_inc(inner_done, 1)

                    def gelu(n):
                        a = n % 2
                        dve.wait_ge(tanh_done, i * GU + n + 1)
                        nc.vector.scalar_tensor_tensor(gl[a][:], gl[a][:], 1.0, gate_ps[:], ALU.add, ALU.mult
                                                       ).then_inc(gelu_done, 1)

                    def product(n):
                        a = n % 2
                        dve.wait_ge(up_done, i * GU + n + 1)
                        dve.wait_ge(gelu_done, after(i * GU + n + 1))
                        dve.wait_ge(il_done, after(since(i * GU, n, 2)))
                        nc.vector.scalar_tensor_tensor(prod[a][:], gl[a][:], 0.5 * IS / (XS * WS) ** 2, up_ps[:],
                                                       ALU.mult, ALU.mult).then_inc(prod_done, 1)

                    def product_hi(n):
                        w, a = n // 2, n % 2
                        dve.wait_ge(prod_done, after(i * GU + n + 1))
                        if a == 0:
                            dve.wait_ge(down_done, after(i * ND + max(TPC * (w - 1), 0)))
                        nc.vector.tensor_copy(ih[w % 2][:, a, :], prod[a][:]).then_inc(ih_done, 1)

                    def accumulate(n):
                        dve.wait_ge(down_done, after(i * ND + n + 1))
                        if n == 0:
                            dve.wait_ge(acc_done, after(i * ND))
                        nc.vector.tensor_tensor(acc[:, n, :], down_ps[n % 2][:], acc[:, n, :], ALU.add
                                                ).then_inc(acc_done, 1)

                    def causal(n):
                        dve.wait_ge(score_done, i * NBLK + n + 1)
                        for _, col, _ in BLOCKS[n][1]:
                            last = nc.vector.tensor_tensor(score_ps[:, col:col + P], score_ps[:, col:col + P],
                                                           mask_st[:], ALU.add)
                        last.then_inc(masked_done, 1)

                    def reduce(n):
                        c, t, m = MAXP[n]
                        cols = (t + 1) * P if m == c else CH
                        dve.wait_ge(max_done, i * NMAX + n + 1)
                        if m == c >= DVE_MASKS_FROM:
                            own = pair_ps[n % 2][:, cols - P:cols]
                            nc.vector.tensor_tensor(own, own, mask_ts[:], ALU.add).then_inc(own_done, 1)
                            dve.wait_ge(own_done, (i * (NCH - DVE_MASKS_FROM) + c - DVE_MASKS_FROM) * TPC + t + 1)
                        if t == 0 and m == 0:
                            dve.wait_ge(mxc_done, after(since(i * NCH, c, 2)))
                        nc.vector.tensor_reduce(mxp[c % 2][:, t, m:m + 1], pair_ps[n % 2][:, 0:cols], AX.X, ALU.max
                                                ).then_inc(red_done, 1)

                    def negate_max(c):
                        dve.wait_ge(red_done, after(i * NMAX + MAX_END[c]))
                        nc.vector.tensor_reduce(mxc[:], mxp[c % 2][:, :, 0:c + 1], AX.X, ALU.max).then_inc(mxc_done, 1)
                        dve.wait_ge(mxc_done, after(i * NCH + c + 1))
                        dve.wait_ge(maxt_done, after(i * NCH + c))
                        nc.vector.tensor_scalar(nmx[:, :, 0], mxc[:], -1.0, None, ALU.mult).then_inc(nhi_done, 1)
                        dve.wait_ge(nhi_done, i * NCH + c + 1)
                        nc.vector.scalar_tensor_tensor(nmx[:, :, 1], mxc[:], -1.0, nmx[:, :, 0].bitcast(F32),
                                                       ALU.mult, ALU.subtract).then_inc(nmx_done, 1)

                    for s in range(SLOTS + 2):
                        if s in RECIP_AT:
                            reciprocals(dve, i, RECIP_AT[s], 1 - par)
                        last = PIECES[s - 1] if 1 <= s <= SLOTS else ("", 0, 0, 0)
                        n = 2 * last[1] + last[2]
                        if s in SCORE_AT and SCORE_AT[s] in DIAG:
                            causal(SCORE_AT[s])
                        if last[0] == "down":
                            accumulate(last[1] * TPC + last[2])
                        if s < SLOTS and MAX_AT[s]:
                            reduce(MAX_AT[s][0])
                        if last[0] == "up" and last[3]:
                            product(n)
                        if last[0] == "gate" and last[3]:
                            inner(n)
                        if s < SLOTS and MAX_AT[s] and MAX_AT[s][0] + 1 in MAX_END:
                            negate_max(MAXP[MAX_AT[s][0]][0])
                        if last[0] == "up" and last[3]:
                            product_hi(n)
                        gate = PIECES[s - 2] if 2 <= s else ("", 0, 0, 0)
                        if gate[0] == "gate" and gate[3]:
                            gelu(2 * gate[1] + gate[2])
                        if s < SLOTS and len(MAX_AT[s]) > 1:
                            reduce(MAX_AT[s][1])
                            if MAX_AT[s][1] + 1 in MAX_END:
                                negate_max(MAXP[MAX_AT[s][1]][0])
                        if s == DECODE_FIRST:
                            dve.wait_ge(gelu_done, after(i * GU))
                            dve.wait_ge(square_done, after(i * GU))
                            dve.wait_ge(wl_done, (i + 1) * 6)
                            nc.vector.tensor_copy(cur[1 - par][:], tab[:, bass.ds(nxt, 1), :].rearrange("p o c -> p (o c)")
                                                  ).then_inc(cur_done, 1)
                        if s in DECODE_AT:
                            decode_step(dve, *DECODE_AT[s], nxt, i + 1)
                        if s - 1 in TURN_W_AT:
                            weights_lo(dve, *TURN_W_AT[s - 1], i + 1, 1 - par)

                loop(dve, body)

            @block.gpsimd
            def _(pool):
                nc.gpsimd.tensor_scalar(identr[:], ident[:], 1.0, 1.0, ALU.mult, ALU.mult).then_inc(identr_done, 1)
                for b in range(2):
                    nc.gpsimd.memset(vst[b][:, :, 2 * HD:].bitcast(F32), 1.0).then_inc(ones_done, 1)
                nc.gpsimd.memset(o3[1][:], 1.0).then_inc(o3_ones, 1)
                pool.wait_ge(o3_ones, 1)
                nc.gpsimd.memset(acc[:], 0.0).then_inc(acc_done, 1)

                def body(i, par, pair):
                    def prob_lo(n):
                        cols = BLOCKS[n][2]
                        pool.wait_ge(phi_done, i * NBLK + n + 1)
                        pool.wait_ge(pv_done, after(since(i * NBLK, n, PP)))
                        nc.gpsimd.tensor_tensor(plo[n % PP][:, 0:cols], p32[n % PR][:, 0:cols],
                                                phi[n % PP][:, 0:cols].bitcast(F32), ALU.subtract).then_inc(plo_done, 1)

                    def product_lo(n):
                        w, a = n // 2, n % 2
                        pool.wait_ge(ih_done, i * GU + n + 1)
                        pool.wait_ge(down_done, after(i * ND + max(TPC * (w - 1), 0)))
                        nc.gpsimd.tensor_tensor(il[w % 2][:, a, :], prod[a][:], ih[w % 2][:, a, :], ALU.subtract
                                                ).then_inc(il_done, 1)

                    for s in range(SLOTS + 1):
                        if s == ADD_PARTS_AT:
                            add_parts(pool, i, 1 - par)
                        if s == NORMALISE_AT:
                            normalise(pool, i, 1 - par)
                        if 1 <= s and PIECES[s - 1][0] == "up" and PIECES[s - 1][3]:
                            product_lo(2 * PIECES[s - 1][1] + PIECES[s - 1][2])
                        if s in SCORE_AT:
                            prob_lo(SCORE_AT[s])

                loop(pool, body)

def epilogue(nc, e):
    x_d, out_d, bo, o_s = (e[n] for n in ("x_d", "out_d", "bo", "o_s"))
    acc, ident, oscale, on, wo, wo_in, o_in, on_done = (
        e[n] for n in ("acc", "ident", "oscale", "on", "wo", "wo_in", "o_in", "on_done"))
    with ExitStack() as ctx:
        def sb(name, shape, dt):
            return ctx.enter_context(nc.sbuf_tensor(name, shape, dt))

        def sem(name):
            return ctx.enter_context(nc.semaphore(name))

        oc = e["oc"] + [sb("oc_last", [P, KVH, CH], F32)]
        woh, wol = (sb(n, [P, KVH, C], F32R) for n in ("woh", "wol"))
        och, ocl = ([sb(f"{n}{i}", [P, KVH, CH], F32R) for i in range(2)] for n in ("och", "ocl"))
        bias = sb("bias", [P, C], F32)
        ones = sb("ones", [P, P], F32)
        diag = sb("diag", [P, KT, P], F32)
        orow = sb("orow", [P, C], F32)
        xr = [sb(f"xr{c}", [P, TPC, C], F32) for c in range(NCH)]
        row_ps = ctx.enter_context(nc.psum_tensor("row_ps", [P, C], F32))
        YB = 6
        y_ps = [ctx.enter_context(nc.psum_tensor(f"y_ps{i}", [P, C], F32)) for i in range(YB)]
        bias_in = sem("bias_in")
        last_in = [sem(f"last_in{c}") for c in range(NCH)]
        x_in2 = [sem(f"x_in2{c}") for c in range(NCH)]
        wo_hi = sem("wo_hi")
        wo_lo = sem("wo_lo")
        oc_hi = sem("oc_hi")
        oc_lo = [sem(f"oc_lo{c}") for c in range(NCH)]
        diag_done = sem("diag_done")
        row_done = sem("row_done")
        orow_done = sem("orow_done")
        xb_done = sem("xb_done")
        scaled = sem("scaled")
        base_done = sem("base_done")
        y_done = sem("y_done")
        y_read = sem("y_read")
        out_done = sem("out_done")
        PARTS = [(0, 0, KVH - 1), (0, KVH - 1, KVH)] + [(c, 0, KVH) for c in range(1, NCH)]

        reciprocals, add_parts, normalise = output_steps(nc, e)

        with nc.Block() as block:
            @block.sync
            def _(sp):
                load_heads(sp, oc, o_s, o_in, 1)
                sp.dma_start(bias[:], bo.rearrange("(o n) -> o n", o=1).broadcast_to([P, C])).then_inc(bias_in, 16)
                sp.wait_ge(on_done, after(HEADS + 1))
                for c in range(NCH):
                    sp.dma_start(oc[c][(REP - 1) * HD:, KVH - 1, :], on[c * HD:(c + 1) * HD, :]).then_inc(last_in[c], 16)
                for c in range(NCH):
                    if c + 2 < NCH:
                        load_heads(sp, oc, o_s, o_in, c + 2)
                    sp.dma_start(xr[c][:], x_d[c * CH:(c + 1) * CH, :].rearrange("(j p) h -> p j h", p=P)
                                 ).then_inc(x_in2[c], 16)
                for n in range(NT):
                    sp.wait_ge(y_read, n + 1)
                    sp.dma_start(out_d[n * P:(n + 1) * P, :], xr[n // TPC][:, n % TPC, :]).then_inc(out_done, 16)
                sp.wait_ge(out_done, 16 * NT)

            def rest(eng, ops, part):
                c, g0, g1 = PARTS[part]
                eng.wait_ge(oc_hi, part + 1)
                ops.tensor_tensor(ocl[c % 2][:, g0:g1], oc[c][:, g0:g1], och[c % 2][:, g0:g1].bitcast(F32), ALU.subtract
                                  ).then_inc(oc_lo[c], 1)

            @block.scalar
            def _(act):
                act.wait_ge(wo_in, 16 * KVH)
                nc.scalar.activation(woh[:], wo, ACT.Copy).then_inc(wo_hi, 1)
                for part, (c, g0, g1) in enumerate(PARTS):
                    if g0 == 0:
                        act.wait_ge(o_in[c], 32)
                    if g1 == KVH:
                        act.wait_ge(last_in[c], 16)
                    if c >= 2:
                        act.wait_ge(y_done, TPC * (c - 1))
                    nc.scalar.activation(och[c % 2][:, g0:g1], oc[c][:, g0:g1], ACT.Copy).then_inc(oc_hi, 1)

            @block.tensor
            def _(pe):
                def project(n, g):
                    c, t = n // TPC, n % TPC
                    cols = slice(t * P, (t + 1) * P)
                    terms = ((och, woh), (och, wol), (ocl, woh))
                    for q, (lhs, rhs) in enumerate(terms):
                        mm = nc.tensor.matmul(y_ps[n % YB][:], lhs[c % 2][:, g, cols], rhs[:, g, :],
                                              start=(g == 0 and q == 0), stop=(g == KVH - 1 and q == 2))
                    if g == KVH - 1:
                        mm.then_inc(y_done, 1)

                pe.wait_ge(diag_done, KT + 1)
                for k in range(KT):
                    mm = nc.tensor.matmul(row_ps[:, k * P:(k + 1) * P], ones[:], diag[:, k, :], start=True, stop=True)
                mm.then_inc(row_done, 1)
                pe.wait_ge(wo_lo, 1)
                pe.wait_ge(oc_lo[0], 1)
                for t in range(TPC):
                    for g in range(KVH - 1):
                        project(t, g)
                pe.wait_ge(oc_lo[0], 2)
                for t in range(TPC):
                    project(t, KVH - 1)
                for n in range(TPC, NT):
                    if n % TPC == 0:
                        pe.wait_ge(oc_lo[n // TPC], 1)
                    if n >= YB:
                        pe.wait_ge(y_read, n - YB + 1)
                    for g in range(KVH):
                        project(n, g)

            @block.gpsimd
            def _(pool):
                add_parts(pool, HEADS, 1)
                normalise(pool, HEADS, 1)
                pool.wait_ge(bias_in, 16)
                for c in range(NCH):
                    if c >= 2:
                        rest(pool, nc.gpsimd, c + 1)
                    pool.wait_ge(x_in2[c], 16)
                    nc.gpsimd.tensor_tensor(xr[c][:], xr[c][:], bias[:].unsqueeze(1).broadcast_to([P, TPC, C]), ALU.add
                                            ).then_inc(xb_done, 1)

            @block.vector
            def _(dve):
                nc.vector.memset(ones[:], 1.0).then_inc(diag_done, 1)
                for k in range(KT):
                    nc.vector.tensor_scalar(diag[:, k, :], ident[:], oscale[:, k:k + 1], None, ALU.mult
                                            ).then_inc(diag_done, 1)
                for q in range(4):
                    reciprocals(dve, HEADS, q, 1)
                dve.wait_ge(wo_hi, 1)
                nc.vector.tensor_tensor(wol[:], wo, woh[:].bitcast(F32), ALU.subtract).then_inc(wo_lo, 1)
                rest(dve, nc.vector, 0)
                rest(dve, nc.vector, 1)
                dve.wait_ge(row_done, 1)
                nc.vector.tensor_copy(orow[:], row_ps[:]).then_inc(orow_done, 1)
                rest(dve, nc.vector, 2)
                dve.wait_ge(orow_done, 1)
                for c in range(NCH):
                    part = acc[:, c * TPC:(c + 1) * TPC, :]
                    nc.vector.tensor_tensor(part, part, orow[:].unsqueeze(1).broadcast_to([P, TPC, C]), ALU.mult
                                            ).then_inc(scaled, 1)
                    dve.wait_ge(scaled, c + 1)
                    dve.wait_ge(xb_done, c + 1)
                    nc.vector.tensor_tensor(part, part, xr[c][:], ALU.add).then_inc(base_done, 1)
                    dve.wait_ge(base_done, c + 1)
                    for t in range(TPC):
                        n = TPC * c + t
                        dve.wait_ge(y_done, n + 1)
                        nc.vector.tensor_tensor(xr[c][:, t, :], y_ps[n % YB][:], acc[:, n, :], ALU.add
                                                ).then_inc(y_read, 1)


def _round12(v):
    m, ex = np.frexp(np.asarray(v, np.float64))
    return np.ldexp(np.rint(m * 4096) / 4096, ex)


def _alibi_rows():
    start = 2.0 ** (-2.0 ** (-(np.log2(HEADS) - 3.0)))
    pos = np.arange(T, dtype=np.float64)
    rows = np.zeros((HEADS, AUG, T))
    for i in range(HEADS):
        h = (i % REP) * KVH + i // REP
        slope = float(np.float32(start ** (h + 1)))
        hi = float(_round12(slope))
        lo = slope - hi
        a, c = -hi * pos, -lo * pos
        rows[i, 2], rows[i, 3] = hi, lo
        rows[i, 4] = _round12(a)
        rows[i, 5] = a - rows[i, 4]
        rows[i, 6] = _round12(c)
        rows[i, 7] = c - rows[i, 6]
    keys = np.ones((AUG, T))
    keys[2] = keys[3] = pos
    return rows.reshape(HEADS * AUG, T).astype(np.float32), keys.astype(np.float32)


_INS = ["L0_attn_x", "L0_attn_Wq", "L0_attn_Wkv", "L0_attn_Wo", "L0_attn_bo", "L0_ffn_gate_W_packed",
        "L0_ffn_gate_scales", "L0_ffn_up_W_packed", "L0_ffn_up_scales", "L0_ffn_down_W_packed", "L0_ffn_down_scales"]


def kernel(**inputs):
    import concourse.bacc as _bacc
    from concourse.bass_utils import run_bass_kernel_spmd as _run

    nc = _bacc.Bacc("TRN2", target_bir_lowering=False, num_devices=1)
    arrays, ap = {}, {}
    augq, augk = _alibi_rows()
    given = {name: np.ascontiguousarray(inputs[name]) for name in _INS}
    given["augq"], given["augk"] = augq, augk
    for name, a in given.items():
        arrays[f"in_{name}_dram"] = a
        ap[name] = nc.dram_tensor(f"in_{name}_dram", a.shape, mybir.dt.from_np(a.dtype), kind="ExternalInput").ap()
    out = nc.dram_tensor("out_0_dram", (1, T, C), F32, kind="ExternalOutput").ap()
    build(nc, ap["L0_attn_x"], ap["L0_attn_Wq"], ap["L0_attn_Wkv"], ap["L0_attn_Wo"], ap["L0_attn_bo"],
          [ap[f"L0_ffn_{m}_W_packed"] for m in ("gate", "up", "down")],
          [ap[f"L0_ffn_{m}_scales"] for m in ("gate", "up", "down")], ap["augq"], ap["augk"], out)
    r = _run(nc, [arrays], core_ids=[0])
    return r.results[0]["out_0_dram"]
```
